# Optimizing a Trainium2 kernel written in Bass

```python
import numpy as np
import jax
import jax.numpy as jnp

def _softmax(x, axis=-1):
    return jax.nn.softmax(x, axis=axis)

def _gelu(x):
    return jax.nn.gelu(x, approximate=True)

def _silu(x):
    return jax.nn.silu(x)

def _sigmoid(x):
    return jax.nn.sigmoid(x)

def _layernorm(x, axis=-1, eps=1e-05):
    m = jnp.mean(x, axis=axis, keepdims=True)
    v = jnp.var(x, axis=axis, keepdims=True)
    return (x - m) / jnp.sqrt(v + eps)

def _scatter_add(tgt, idx, src, axis=0):
    return tgt.at[idx].add(src)

def _segment_sum(src, seg, n):
    return jax.ops.segment_sum(src, seg, n)
kernel_name = 'mk_gps_d2_gnn_r8_716120'

def setup_inputs(seed: int=0):
    np.random.seed(seed)
    _w = jnp.asarray

    def _rec_inputs():
        import jax
        import jax.numpy as jnp
        _gk = jax.random.key(seed)
        x = -0.0002117 + 1 * jax.random.normal(jax.random.fold_in(_gk, 1), (6250, 256), jnp.float32)
        src = jax.random.randint(jax.random.fold_in(_gk, 2), (100000,), 0, 6250, jnp.int32)
        dst = jnp.minimum((6250 * jax.random.uniform(jax.random.fold_in(_gk, 3), (100000,)) ** 2.0).astype(jnp.int32), 49999)
        _o = jnp.argsort(dst, stable=True)
        src = src[_o]
        dst = dst[_o]
        return (x, src, dst)
    x, src, dst = _rec_inputs()

    def _L0_gnn_setup():
        import jax, jax.numpy as jnp
        import numpy as np
        key = jax.random.key(seed)
        k1, k2, k3 = jax.random.split(key, 3)
        N, E, D_IN, D_OUT = (12500, 400000, 256, 256)
        x = jax.random.normal(k1, (N, D_IN), dtype=jnp.float32)
        W = jax.random.normal(k2, (D_OUT, D_IN), dtype=jnp.float32) * (1.0 / np.sqrt(D_IN))
        edge_index = jax.random.randint(k3, (2, E), 0, N, dtype=jnp.int32)
        return {'x': x, 'W': W, 'edge_index': edge_index}
    _L0_gnn_all = _L0_gnn_setup()
    _L0_gnn_in = {k: v for k, v in _L0_gnn_all.items() if k in ('W',)}
    del _L0_gnn_all

    def _L0_mix_setup():
        import jax, jax.numpy as jnp
        import numpy as np
        C_CURV = 1.0
        MIN_NORM = 1e-15
        BALL_EPS = 1e-05
        ATT_EPS = 1e-15
        DIM = 32

        def _norm(x):
            return jnp.clip(jnp.linalg.norm(x, axis=-1, keepdims=True), MIN_NORM)

        def proj(x, c):
            maxnorm = (1.0 - BALL_EPS) / jnp.sqrt(c)
            n = _norm(x)
            return jnp.where(n > maxnorm, x / n * maxnorm, x)

        def expmap0(u, c):
            sc = jnp.sqrt(c)
            n = _norm(u)
            return jnp.tanh(sc * n) * u / (sc * n)

        def logmap0(p, c):
            sc = jnp.sqrt(c)
            n = _norm(p)
            return jnp.arctanh(jnp.clip(sc * n, -1.0 + 1e-07, 1.0 - 1e-07)) * p / (sc * n)

        def mobius_add(x, y, c):
            x2 = jnp.sum(x * x, -1, keepdims=True)
            y2 = jnp.sum(y * y, -1, keepdims=True)
            xy = jnp.sum(x * y, -1, keepdims=True)
            num = (1 + 2 * c * xy + c * y2) * x + (1 - c * x2) * y
            den = 1 + 2 * c * xy + c * c * x2 * y2
            return num / jnp.clip(den, MIN_NORM)

        def conv1d(x, w, pad, groups=1):
            return jax.lax.conv_general_dilated(x, w, (1,), [(pad, pad)], dimension_numbers=('NCH', 'OIH', 'NCH'), feature_group_count=groups)

        def batchnorm(x, gamma, beta):
            mean = jnp.mean(x, axis=(0, 2), keepdims=True)
            var = jnp.var(x, axis=(0, 2), keepdims=True)
            xn = (x - mean) * jax.lax.rsqrt(var + 1e-05)
            return gamma[None, :, None] * xn + beta[None, :, None]

        def _reference_tuple_inner(x, w_qkv, bn_gamma, bn_beta, w_dw, w_pw, w_res, b_res):
            c = C_CURV
            h = logmap0(proj(x, c), c)
            h = jnp.transpose(h, (1, 2, 0))
            h = conv1d(h, w_qkv, pad=2)
            h = batchnorm(h, bn_gamma, bn_beta)
            h = jax.nn.relu(jnp.transpose(h, (2, 0, 1)))
            qkv = proj(expmap0(h, c), c)
            t = jnp.transpose(logmap0(proj(qkv, c), c), (1, 2, 0))
            s = conv1d(t, w_dw, pad=2, groups=t.shape[1])
            s = conv1d(s, w_pw, pad=0, groups=t.shape[1] // DIM)
            cat = jnp.concatenate([t, s], axis=1)
            ai = proj(expmap0(jnp.transpose(cat, (2, 0, 1)), c), c)
            t2 = logmap0(proj(ai, c), c)
            L, N, C2 = t2.shape
            g = C2 // (3 * DIM)
            qkv3 = jnp.transpose(t2, (1, 2, 0)).reshape(N, g, 3 * DIM, L)
            q, k, v = jnp.split(qkv3, 3, axis=2)
            q = jax.nn.relu(q)
            k = jax.nn.relu(k)
            vk = jnp.einsum('ngdl,ngel->ngde', v, k)
            out = jnp.einsum('ngde,ngdl->ngdl', vk, q)
            out = out / (jnp.sum(v, -1, keepdims=True) + ATT_EPS)
            out = jnp.transpose(out.reshape(N, g * DIM, L), (2, 0, 1))
            fx_h = proj(expmap0(out, c), c)
            ft = jnp.transpose(logmap0(proj(fx_h, c), c), (1, 2, 0))
            ft = conv1d(ft, w_res, pad=0) + b_res[None, :, None]
            fx = proj(expmap0(jnp.transpose(ft, (2, 0, 1)), c), c)
            residual = mobius_add(fx, x, c)
            return (fx, residual)
        key = jax.random.key(seed)
        ks = jax.random.split(key, 6)
        L, N, C, TD = (256, 16, 256, 256)
        x = jax.random.normal(ks[0], (L, N, C), jnp.float32) * 0.05
        w_qkv = jax.random.normal(ks[1], (3 * TD, C, 5), jnp.float32) / np.sqrt(C * 5)
        bn_gamma = jnp.ones((3 * TD,), jnp.float32)
        bn_beta = jnp.zeros((3 * TD,), jnp.float32)
        w_dw = jax.random.normal(ks[2], (3 * TD, 1, 5), jnp.float32) / np.sqrt(5.0)
        w_pw = jax.random.normal(ks[3], (3 * TD, DIM, 1), jnp.float32) / np.sqrt(DIM)
        w_res = jax.random.normal(ks[4], (C, 2 * TD, 1), jnp.float32) / np.sqrt(2 * TD)
        b_res = jnp.zeros((C,), jnp.float32)
        return {'x': x, 'w_qkv': w_qkv, 'bn_gamma': bn_gamma, 'bn_beta': bn_beta, 'w_dw': w_dw, 'w_pw': w_pw, 'w_res': w_res, 'b_res': b_res}
    _L0_mix_all = _L0_mix_setup()
    _L0_mix_in = {k: v for k, v in _L0_mix_all.items() if k in ('w_qkv', 'bn_gamma', 'bn_beta', 'w_dw', 'w_pw', 'w_res', 'b_res')}
    del _L0_mix_all

    def _L0_ffn_setup():
        import jax, jax.numpy as jnp
        import numpy as np
        B, N, D = (16, 512, 256)
        NUM_EXPERTS, TOP_K, HEADS = (4, 2, 4)
        N_EDGES = 131072
        LN_EPS = 1e-05

        def _layernorm(x, g, b):
            mu = x.mean(-1, keepdims=True)
            var = ((x - mu) ** 2).mean(-1, keepdims=True)
            return (x - mu) * jax.lax.rsqrt(var + LN_EPS) * g + b

        def _forward(x, edge_index, W_gat, att_src, att_dst, b_gat, ln_gamma, ln_beta, W1, b1, W2, b2):
            Bc, Nc, Dc = x.shape
            M = Bc * Nc
            x_flat = x.reshape(M, Dc)
            h = (x_flat @ W_gat).reshape(M, HEADS, NUM_EXPERTS)
            loops = jnp.arange(M, dtype=edge_index.dtype)
            src = jnp.concatenate([edge_index[0], loops])
            dst = jnp.concatenate([edge_index[1], loops])
            a_src = (h * att_src).sum(-1)
            a_dst = (h * att_dst).sum(-1)
            e = jax.nn.leaky_relu(a_src[src] + a_dst[dst], negative_slope=0.2)
            e_max = jax.ops.segment_max(e, dst, num_segments=M)
            ee = jnp.exp(e - e_max[dst])
            denom = jax.ops.segment_sum(ee, dst, num_segments=M)
            alpha = ee / (denom[dst] + 1e-16)
            msg = h[src] * alpha[:, :, None]
            agg = jax.ops.segment_sum(msg, dst, num_segments=M).reshape(M, HEADS * NUM_EXPERTS) + b_gat
            scores = _layernorm(agg, ln_gamma, ln_beta).reshape(M, HEADS, NUM_EXPERTS).mean(1)
            scores = scores.reshape(Bc, Nc, NUM_EXPERTS)
            topk_s, topk_i = jax.lax.top_k(scores, TOP_K)
            w = jax.nn.softmax(topk_s, axis=-1)
            out = jnp.zeros_like(x)
            for ei in range(NUM_EXPERTS):
                g = jnp.where(topk_i == ei, w, 0.0).sum(-1)
                hh = jax.nn.gelu(x @ W1[ei] + b1[ei], approximate=False)
                out = out + g[..., None] * (hh @ W2[ei] + b2[ei])
            return out
        key = jax.random.key(seed)
        ks = jax.random.split(key, 8)
        s = 0.05
        return {'x': jax.random.normal(ks[0], (B, N, D), jnp.float32), 'W_gat': jax.random.normal(ks[1], (D, HEADS * NUM_EXPERTS), jnp.float32) * s, 'att_src': jax.random.normal(ks[2], (HEADS, NUM_EXPERTS), jnp.float32) * s, 'att_dst': jax.random.normal(ks[3], (HEADS, NUM_EXPERTS), jnp.float32) * s, 'b_gat': jnp.zeros((HEADS * NUM_EXPERTS,), jnp.float32), 'ln_gamma': jnp.ones((HEADS * NUM_EXPERTS,), jnp.float32), 'ln_beta': jnp.zeros((HEADS * NUM_EXPERTS,), jnp.float32), 'W1': jax.random.normal(ks[4], (NUM_EXPERTS, D, 2 * D), jnp.float32) * s, 'b1': jnp.zeros((NUM_EXPERTS, 2 * D), jnp.float32), 'W2': jax.random.normal(ks[5], (NUM_EXPERTS, 2 * D, D), jnp.float32) * s, 'b2': jnp.zeros((NUM_EXPERTS, D), jnp.float32), 'edge_index': jax.random.randint(ks[6], (2, N_EDGES), 0, B * N, jnp.int32)}
    _L0_ffn_all = _L0_ffn_setup()
    _L0_ffn_in = {k: v for k, v in _L0_ffn_all.items() if k in ('W_gat', 'att_src', 'att_dst', 'b_gat', 'ln_gamma', 'ln_beta', 'W1', 'b1', 'W2', 'b2', 'edge_index')}
    del _L0_ffn_all

    def _L1_gnn_setup():
        import jax, jax.numpy as jnp
        import numpy as np
        N_NODES = 12500
        N_EDGES = 200000
        HIDDEN = 256
        N_LAYERS = 2
        key = jax.random.key(seed)
        k = jax.random.split(key, 7)
        x = jax.random.normal(k[0], (N_NODES, HIDDEN), dtype=jnp.float32)
        edge_index = jax.random.randint(k[1], (2, N_EDGES), 0, N_NODES, dtype=jnp.int64)
        s = 1.0 / np.sqrt(HIDDEN)
        W = jax.random.uniform(k[2], (N_LAYERS, HIDDEN, HIDDEN), jnp.float32, -s, s)
        b = jax.random.uniform(k[3], (N_LAYERS, HIDDEN), jnp.float32, -s, s)
        resW = jax.random.uniform(k[4], (HIDDEN, HIDDEN), jnp.float32, -s, s)
        resb = jax.random.uniform(k[5], (HIDDEN,), jnp.float32, -s, s)
        return {'x': x, 'edge_index': edge_index, 'W': W, 'b': b, 'resW': resW, 'resb': resb}
    _L1_gnn_all = _L1_gnn_setup()
    _L1_gnn_in = {k: v for k, v in _L1_gnn_all.items() if k in ('W', 'b', 'resW', 'resb')}
    del _L1_gnn_all

    def _L1_mix_setup():
        import jax, jax.numpy as jnp
        import numpy as np
        HEADS, DIM_HEAD = (8, 64)
        EPS = 1e-05

        def instance_norm(t):
            mu = jnp.mean(t, axis=-1, keepdims=True)
            var = jnp.mean((t - mu) ** 2, axis=-1, keepdims=True)
            return (t - mu) * jax.lax.rsqrt(var + EPS)
        key = jax.random.key(seed)
        k1, k2, k3, k4 = jax.random.split(key, 4)
        B, N, D = (8, 1024, 256)
        inner = HEADS * DIM_HEAD
        x = jax.random.normal(k1, (B, N, D), jnp.float32)
        w_qkv = jax.random.normal(k2, (3 * inner, D), jnp.float32) / np.sqrt(D).astype(np.float32)
        w_out = jax.random.normal(k3, (D, inner), jnp.float32) / np.sqrt(inner).astype(np.float32)
        b_out = 0.01 * jax.random.normal(k4, (D,), jnp.float32)
        return {'x': x, 'w_qkv': w_qkv, 'w_out': w_out, 'b_out': b_out}
    _L1_mix_all = _L1_mix_setup()
    _L1_mix_in = {k: v for k, v in _L1_mix_all.items() if k in ('w_qkv', 'w_out', 'b_out')}
    del _L1_mix_all

    def _L1_ffn_setup():
        import jax, jax.numpy as jnp
        import numpy as np
        E = 8
        K = 2
        D = 256
        H = 512
        DOUT = 256
        EPS = 1e-05
        key = jax.random.key(seed)
        ks = jax.random.split(key, 9)
        s = 0.02
        return {'x': jax.random.normal(ks[0], (4, 1024, D), jnp.float32), 'gamma': 1.0 + 0.05 * jax.random.normal(ks[1], (D,), jnp.float32), 'beta': 0.05 * jax.random.normal(ks[2], (D,), jnp.float32), 'Wr': 0.01 * jax.random.normal(ks[3], (D, E), jnp.float32), 'br': jnp.zeros((E,), jnp.float32), 'W1': s * jax.random.normal(ks[4], (E, D, H), jnp.float32), 'b1': s * jax.random.normal(ks[5], (E, H), jnp.float32), 'W2': s * jax.random.normal(ks[6], (E, H, DOUT), jnp.float32), 'b2': s * jax.random.normal(ks[7], (E, DOUT), jnp.float32)}
    _L1_ffn_all = _L1_ffn_setup()
    _L1_ffn_in = {k: v for k, v in _L1_ffn_all.items() if k in ('gamma', 'beta', 'Wr', 'br', 'W1', 'b1', 'W2', 'b2')}
    del _L1_ffn_all
    return {'x': x, 'src': src, 'dst': dst, 'L0_gnn_W': _L0_gnn_in['W'], 'L0_mix_w_qkv': _L0_mix_in['w_qkv'], 'L0_mix_bn_gamma': _L0_mix_in['bn_gamma'], 'L0_mix_bn_beta': _L0_mix_in['bn_beta'], 'L0_mix_w_dw': _L0_mix_in['w_dw'], 'L0_mix_w_pw': _L0_mix_in['w_pw'], 'L0_mix_w_res': _L0_mix_in['w_res'], 'L0_mix_b_res': _L0_mix_in['b_res'], 'L0_ffn_W_gat': _L0_ffn_in['W_gat'], 'L0_ffn_att_src': _L0_ffn_in['att_src'], 'L0_ffn_att_dst': _L0_ffn_in['att_dst'], 'L0_ffn_b_gat': _L0_ffn_in['b_gat'], 'L0_ffn_ln_gamma': _L0_ffn_in['ln_gamma'], 'L0_ffn_ln_beta': _L0_ffn_in['ln_beta'], 'L0_ffn_W1': _L0_ffn_in['W1'], 'L0_ffn_b1': _L0_ffn_in['b1'], 'L0_ffn_W2': _L0_ffn_in['W2'], 'L0_ffn_b2': _L0_ffn_in['b2'], 'L0_ffn_edge_index': _L0_ffn_in['edge_index'], 'L1_gnn_W': _L1_gnn_in['W'], 'L1_gnn_b': _L1_gnn_in['b'], 'L1_gnn_resW': _L1_gnn_in['resW'], 'L1_gnn_resb': _L1_gnn_in['resb'], 'L1_mix_w_qkv': _L1_mix_in['w_qkv'], 'L1_mix_w_out': _L1_mix_in['w_out'], 'L1_mix_b_out': _L1_mix_in['b_out'], 'L1_ffn_gamma': _L1_ffn_in['gamma'], 'L1_ffn_beta': _L1_ffn_in['beta'], 'L1_ffn_Wr': _L1_ffn_in['Wr'], 'L1_ffn_br': _L1_ffn_in['br'], 'L1_ffn_W1': _L1_ffn_in['W1'], 'L1_ffn_b1': _L1_ffn_in['b1'], 'L1_ffn_W2': _L1_ffn_in['W2'], 'L1_ffn_b2': _L1_ffn_in['b2']}

def reference(x, src, dst, L0_gnn_W, L0_mix_w_qkv, L0_mix_bn_gamma, L0_mix_bn_beta, L0_mix_w_dw, L0_mix_w_pw, L0_mix_w_res, L0_mix_b_res, L0_ffn_W_gat, L0_ffn_att_src, L0_ffn_att_dst, L0_ffn_b_gat, L0_ffn_ln_gamma, L0_ffn_ln_beta, L0_ffn_W1, L0_ffn_b1, L0_ffn_W2, L0_ffn_b2, L0_ffn_edge_index, L1_gnn_W, L1_gnn_b, L1_gnn_resW, L1_gnn_resb, L1_mix_w_qkv, L1_mix_w_out, L1_mix_b_out, L1_ffn_gamma, L1_ffn_beta, L1_ffn_Wr, L1_ffn_br, L1_ffn_W1, L1_ffn_b1, L1_ffn_W2, L1_ffn_b2):
    import jax
    import jax.numpy as jnp

    def _L0_gnn_ref(x, W, edge_index):
        import jax, jax.numpy as jnp
        import numpy as np
        N = x.shape[0]
        loops = jnp.arange(N, dtype=edge_index.dtype)
        src = jnp.concatenate([edge_index[0], loops])
        dst = jnp.concatenate([edge_index[1], loops])
        deg = jax.ops.segment_sum(jnp.ones_like(src, dtype=x.dtype), src, num_segments=N)
        deg_rsqrt = jax.lax.rsqrt(deg)
        vals = deg_rsqrt[src] * deg_rsqrt[dst]
        h = x @ W.T
        msgs = vals[:, None] * h[dst]
        out = jax.ops.segment_sum(msgs, src, num_segments=N)
        return out

    def _L0_mix_ref(x, w_qkv, bn_gamma, bn_beta, w_dw, w_pw, w_res, b_res):
        import jax, jax.numpy as jnp
        import numpy as np
        C_CURV = 1.0
        MIN_NORM = 1e-15
        BALL_EPS = 1e-05
        ATT_EPS = 1e-15
        DIM = 32

        def _norm(x):
            return jnp.clip(jnp.linalg.norm(x, axis=-1, keepdims=True), MIN_NORM)

        def proj(x, c):
            maxnorm = (1.0 - BALL_EPS) / jnp.sqrt(c)
            n = _norm(x)
            return jnp.where(n > maxnorm, x / n * maxnorm, x)

        def expmap0(u, c):
            sc = jnp.sqrt(c)
            n = _norm(u)
            return jnp.tanh(sc * n) * u / (sc * n)

        def logmap0(p, c):
            sc = jnp.sqrt(c)
            n = _norm(p)
            return jnp.arctanh(jnp.clip(sc * n, -1.0 + 1e-07, 1.0 - 1e-07)) * p / (sc * n)

        def mobius_add(x, y, c):
            x2 = jnp.sum(x * x, -1, keepdims=True)
            y2 = jnp.sum(y * y, -1, keepdims=True)
            xy = jnp.sum(x * y, -1, keepdims=True)
            num = (1 + 2 * c * xy + c * y2) * x + (1 - c * x2) * y
            den = 1 + 2 * c * xy + c * c * x2 * y2
            return num / jnp.clip(den, MIN_NORM)

        def conv1d(x, w, pad, groups=1):
            return jax.lax.conv_general_dilated(x, w, (1,), [(pad, pad)], dimension_numbers=('NCH', 'OIH', 'NCH'), feature_group_count=groups)

        def batchnorm(x, gamma, beta):
            mean = jnp.mean(x, axis=(0, 2), keepdims=True)
            var = jnp.var(x, axis=(0, 2), keepdims=True)
            xn = (x - mean) * jax.lax.rsqrt(var + 1e-05)
            return gamma[None, :, None] * xn + beta[None, :, None]

        def _reference_tuple_inner(x, w_qkv, bn_gamma, bn_beta, w_dw, w_pw, w_res, b_res):
            c = C_CURV
            h = logmap0(proj(x, c), c)
            h = jnp.transpose(h, (1, 2, 0))
            h = conv1d(h, w_qkv, pad=2)
            h = batchnorm(h, bn_gamma, bn_beta)
            h = jax.nn.relu(jnp.transpose(h, (2, 0, 1)))
            qkv = proj(expmap0(h, c), c)
            t = jnp.transpose(logmap0(proj(qkv, c), c), (1, 2, 0))
            s = conv1d(t, w_dw, pad=2, groups=t.shape[1])
            s = conv1d(s, w_pw, pad=0, groups=t.shape[1] // DIM)
            cat = jnp.concatenate([t, s], axis=1)
            ai = proj(expmap0(jnp.transpose(cat, (2, 0, 1)), c), c)
            t2 = logmap0(proj(ai, c), c)
            L, N, C2 = t2.shape
            g = C2 // (3 * DIM)
            qkv3 = jnp.transpose(t2, (1, 2, 0)).reshape(N, g, 3 * DIM, L)
            q, k, v = jnp.split(qkv3, 3, axis=2)
            q = jax.nn.relu(q)
            k = jax.nn.relu(k)
            vk = jnp.einsum('ngdl,ngel->ngde', v, k)
            out = jnp.einsum('ngde,ngdl->ngdl', vk, q)
            out = out / (jnp.sum(v, -1, keepdims=True) + ATT_EPS)
            out = jnp.transpose(out.reshape(N, g * DIM, L), (2, 0, 1))
            fx_h = proj(expmap0(out, c), c)
            ft = jnp.transpose(logmap0(proj(fx_h, c), c), (1, 2, 0))
            ft = conv1d(ft, w_res, pad=0) + b_res[None, :, None]
            fx = proj(expmap0(jnp.transpose(ft, (2, 0, 1)), c), c)
            residual = mobius_add(fx, x, c)
            return (fx, residual)
        return _reference_tuple_inner(x, w_qkv, bn_gamma, bn_beta, w_dw, w_pw, w_res, b_res)[0]

    def _L0_ffn_ref(x, W_gat, att_src, att_dst, b_gat, ln_gamma, ln_beta, W1, b1, W2, b2, edge_index):
        import jax, jax.numpy as jnp
        import numpy as np
        B, N, D = (16, 512, 256)
        NUM_EXPERTS, TOP_K, HEADS = (4, 2, 4)
        N_EDGES = 131072
        LN_EPS = 1e-05

        def _layernorm(x, g, b):
            mu = x.mean(-1, keepdims=True)
            var = ((x - mu) ** 2).mean(-1, keepdims=True)
            return (x - mu) * jax.lax.rsqrt(var + LN_EPS) * g + b

        def _forward(x, edge_index, W_gat, att_src, att_dst, b_gat, ln_gamma, ln_beta, W1, b1, W2, b2):
            Bc, Nc, Dc = x.shape
            M = Bc * Nc
            x_flat = x.reshape(M, Dc)
            h = (x_flat @ W_gat).reshape(M, HEADS, NUM_EXPERTS)
            loops = jnp.arange(M, dtype=edge_index.dtype)
            src = jnp.concatenate([edge_index[0], loops])
            dst = jnp.concatenate([edge_index[1], loops])
            a_src = (h * att_src).sum(-1)
            a_dst = (h * att_dst).sum(-1)
            e = jax.nn.leaky_relu(a_src[src] + a_dst[dst], negative_slope=0.2)
            e_max = jax.ops.segment_max(e, dst, num_segments=M)
            ee = jnp.exp(e - e_max[dst])
            denom = jax.ops.segment_sum(ee, dst, num_segments=M)
            alpha = ee / (denom[dst] + 1e-16)
            msg = h[src] * alpha[:, :, None]
            agg = jax.ops.segment_sum(msg, dst, num_segments=M).reshape(M, HEADS * NUM_EXPERTS) + b_gat
            scores = _layernorm(agg, ln_gamma, ln_beta).reshape(M, HEADS, NUM_EXPERTS).mean(1)
            scores = scores.reshape(Bc, Nc, NUM_EXPERTS)
            topk_s, topk_i = jax.lax.top_k(scores, TOP_K)
            w = jax.nn.softmax(topk_s, axis=-1)
            out = jnp.zeros_like(x)
            for ei in range(NUM_EXPERTS):
                g = jnp.where(topk_i == ei, w, 0.0).sum(-1)
                hh = jax.nn.gelu(x @ W1[ei] + b1[ei], approximate=False)
                out = out + g[..., None] * (hh @ W2[ei] + b2[ei])
            return out
        return _forward(x, edge_index, W_gat, att_src, att_dst, b_gat, ln_gamma, ln_beta, W1, b1, W2, b2)

    def _L1_gnn_ref(x, edge_index, W, b, resW, resb):
        import jax, jax.numpy as jnp
        import numpy as np
        N_NODES = 12500
        N_EDGES = 200000
        HIDDEN = 256
        N_LAYERS = 2
        N = x.shape[0]
        loop = jnp.arange(N, dtype=edge_index.dtype)
        src = jnp.concatenate([edge_index[0], loop])
        dst = jnp.concatenate([edge_index[1], loop])
        ew = jnp.ones(src.shape[0], dtype=x.dtype)
        deg = jax.ops.segment_sum(ew, dst, num_segments=N)
        dis = jnp.where(deg > 0, jax.lax.rsqrt(jnp.where(deg > 0, deg, 1.0)), 0.0)
        norm = dis[src] * ew * dis[dst]
        for l in range(W.shape[0]):
            x_res = x
            h = x @ W[l]
            msg = norm[:, None] * h[src]
            agg = jax.ops.segment_sum(msg, dst, num_segments=N) + b[l]
            x = jax.nn.relu(agg + x_res @ resW + resb)
        return x

    def _L1_mix_ref(x, w_qkv, w_out, b_out):
        import jax, jax.numpy as jnp
        import numpy as np
        HEADS, DIM_HEAD = (8, 64)
        EPS = 1e-05

        def instance_norm(t):
            mu = jnp.mean(t, axis=-1, keepdims=True)
            var = jnp.mean((t - mu) ** 2, axis=-1, keepdims=True)
            return (t - mu) * jax.lax.rsqrt(var + EPS)
        B, N, _ = x.shape
        H, Dh = (HEADS, DIM_HEAD)
        qkv = jnp.einsum('bnd,ed->bne', x, w_qkv)
        q, k, v = jnp.split(qkv, 3, axis=-1)

        def to_heads(t):
            return t.reshape(B, N, H, Dh).transpose(0, 2, 1, 3)
        q, k, v = (to_heads(q), to_heads(k), to_heads(v))
        k = instance_norm(k)
        v = instance_norm(v)
        dots = jnp.einsum('bhnd,bhne->bhde', k, v)
        out = jnp.einsum('bhnd,bhde->bhne', q, dots) / N
        out = out.transpose(0, 2, 1, 3).reshape(B, N, H * Dh)
        return jnp.einsum('bne,de->bnd', out, w_out) + b_out

    def _L1_ffn_ref(x, gamma, beta, Wr, br, W1, b1, W2, b2):
        import jax, jax.numpy as jnp
        import numpy as np
        E = 8
        K = 2
        D = 256
        H = 512
        DOUT = 256
        EPS = 1e-05
        mu = jnp.mean(x, axis=-1, keepdims=True)
        var = jnp.mean(jnp.square(x - mu), axis=-1, keepdims=True)
        xn = (x - mu) * jax.lax.rsqrt(var + EPS) * gamma + beta
        logits = jnp.einsum('bsd,de->bse', xn, Wr) + br
        top_vals, top_idx = jax.lax.top_k(logits, K)
        w = jax.nn.softmax(top_vals, axis=-1)
        w_full = jnp.einsum('bsk,bske->bse', w, jax.nn.one_hot(top_idx, E, dtype=w.dtype))
        y = jnp.zeros(x.shape[:-1] + (DOUT,), x.dtype)
        for e in range(E):
            h = jax.nn.gelu(jnp.einsum('bsd,dh->bsh', xn, W1[e]) + b1[e], approximate=False)
            y_e = jnp.einsum('bsh,hd->bsd', h, W2[e]) + b2[e]
            y = y + y_e * w_full[..., e, None]
        return y
    edge_index = jnp.stack([src, dst])
    xn = _layernorm(x, axis=-1)
    x = x + _L0_gnn_ref(xn, L0_gnn_W, edge_index) + _L0_mix_ref(xn[None], L0_mix_w_qkv, L0_mix_bn_gamma, L0_mix_bn_beta, L0_mix_w_dw, L0_mix_w_pw, L0_mix_w_res, L0_mix_b_res)[0]
    x = x + _L0_ffn_ref(_layernorm(x, axis=-1)[None], L0_ffn_W_gat, L0_ffn_att_src, L0_ffn_att_dst, L0_ffn_b_gat, L0_ffn_ln_gamma, L0_ffn_ln_beta, L0_ffn_W1, L0_ffn_b1, L0_ffn_W2, L0_ffn_b2, L0_ffn_edge_index)[0]
    xn = _layernorm(x, axis=-1)
    x = x + _L1_gnn_ref(xn, edge_index, L1_gnn_W, L1_gnn_b, L1_gnn_resW, L1_gnn_resb) + _L1_mix_ref(xn[None], L1_mix_w_qkv, L1_mix_w_out, L1_mix_b_out)[0]
    x = x + _L1_ffn_ref(_layernorm(x, axis=-1)[None], L1_ffn_gamma, L1_ffn_beta, L1_ffn_Wr, L1_ffn_br, L1_ffn_W1, L1_ffn_b1, L1_ffn_W2, L1_ffn_b2)[0]
    return x

_drawn_inputs = setup_inputs


def setup_inputs(seed=0):
    import zlib

    import numpy as np

    out = dict(_drawn_inputs(seed))
    spreads = {'L0_mix_bn_gamma': (1.0, 0.595),
     'L0_mix_bn_beta': (0.0, 0.1),
     'L0_mix_b_res': (0.0, 0.1),
     'L0_ffn_b_gat': (0.0, 0.1),
     'L0_ffn_ln_gamma': (1.0, 0.2),
     'L0_ffn_ln_beta': (0.0, 0.1),
     'L0_ffn_b1': (0.0, 0.1),
     'L0_ffn_b2': (0.0, 0.1),
     'L1_ffn_br': (0.0, 0.1)}
    factors = {'L1_mix_b_out': 7.649,
     'L1_ffn_gamma': 6.011,
     'L1_ffn_beta': 5.836,
     'L1_ffn_b1': 8.0,
     'L1_ffn_b2': 5.23}
    for name, (base, spread) in spreads.items():
        noise = np.random.default_rng([zlib.crc32(name.encode()), seed]).standard_normal(out[name].shape)
        drawn = base * np.exp(spread * noise) if base else spread * noise
        out[name] = jnp.asarray(drawn.astype(out[name].dtype))
    for name, factor in factors.items():
        out[name] = (out[name] * factor).astype(out[name].dtype)
    return out
```

```python
from contextlib import ExitStack

import numpy as np

import concourse.bass as bass
from concourse import mybir

F32 = mybir.dt.float32
BF16 = mybir.dt.bfloat16
I32 = mybir.dt.int32
U8 = mybir.dt.uint8
ALU = mybir.AluOpType
ACT = mybir.ActivationFunctionType
AX = mybir.AxisListType

P = 128
N = 6250
D = 256
NT = (N + P - 1) // P
NP = NT * P
LAST = N - (NT - 1) * P
LN_EPS = 1e-5
MAXNORM = float(np.float32(1.0 - 1e-5))
ATANH_MAX = float(np.arctanh(np.float64(MAXNORM)))
MIN_NORM = 1e-15
U = 4


def rounded_chunks(n_edges):
    most = (n_edges + NT * (P - 1)) // P
    return -(-most // (4 * U)) * 4 * U


E_GNN = 100000
GNN_ROWS, GNN_COLS = 125, 800
E_GAT = 131072
GAT_ROWS, GAT_COLS = 128, 1024
NCH_GNN = rounded_chunks(E_GNN)
NCH_GAT = rounded_chunks(E_GAT)


class Chain:

    def __init__(self, engine, sem):
        self.engine, self.sem, self.count = engine, sem, 0

    def go(self, instruction):
        instruction.then_inc(self.sem, 1)
        self.count += 1

    def sync(self):
        if self.count:
            self.engine.wait_ge(self.sem, self.count)

    def run(self, instruction):
        self.go(instruction)
        self.sync()

    def reset(self):
        if self.count:
            self.sync()
            self.engine.sem_inc(self.sem, -self.count)
            self.count = 0


def take(engine, sem, n=1):
    engine.wait_ge(sem, n)
    engine.sem_inc(sem, -n)


def program(nc, a, out, dbg=None):
    top = ExitStack()
    with top:
        _program(nc, a, out, top, dbg or {})


def _program(nc, a, out, top, dbg):
    PE, DVE, ACTE, POOL, SP = nc.tensor, nc.vector, nc.scalar, nc.gpsimd, nc.sync

    names = {}

    def fresh(name):
        names[name] = names.get(name, 0) + 1
        return name if names[name] == 1 else f"{name}_{names[name]}"

    def sem(name):
        return top.enter_context(nc.semaphore(fresh(name)))

    links = {(p, q): sem(f"{p}_to_{q}") for p, q in ("vp", "pv", "vs", "va", "av", "gv", "vg", "ap", "pa")}
    engines = {"v": DVE, "p": PE, "a": ACTE, "g": POOL, "s": SP}

    def tell(p, q):
        engines[p].sem_inc(links[p, q], 1)

    def hear(p, q):
        take(engines[q], links[p, q])

    V = Chain(DVE, sem("dve_own"))
    S = Chain(ACTE, sem("act_own"))
    G = Chain(POOL, sem("pool_own"))

    def sb(ctx, name, shape, dt=F32):
        return ctx.enter_context(nc.sbuf_tensor(fresh(name), shape, dt))

    def ps(ctx, name, shape, dt=F32):
        return ctx.enter_context(nc.psum_tensor(fresh(name), shape, dt))

    def dram(name, shape, dt=F32):
        return nc.dram_tensor(fresh(name), shape, dt).ap()

    def barrier():
        V.reset(); S.reset(); G.reset()
        nc.all_engine_barrier()

    load_sem = sem("loads")
    loads = [0]

    def load(dst, src):
        SP.dma_start(dst, src).then_inc(load_sem, 16)
        loads[0] += 16

    def loads_done(*engines):
        for e in engines:
            e.wait_ge(load_sem, loads[0])

    def tiles(body):
        V.reset(); S.reset(); G.reset()
        with nc.Fori(0, NT // 2) as i:
            for slot in range(2):
                body(i * 2 + slot, slot, False)
                V.reset(); S.reset(); G.reset()
        body(NT - 1, 0, True)
        V.reset(); S.reset(); G.reset()

    ident = sb(top, "ident", [P, P])
    ones = sb(top, "ones", [P, P])
    before = sb(top, "before", [P, P])
    iota_row = sb(top, "iota_row", [P, P])
    zeros = sb(top, "zeros", [P, P])
    zwide = sb(top, "zwide", [P, D + 1])
    row_no = sb(top, "row_no", [P, 1])
    window = sb(top, "window", [P, 2 * NT])
    x_all = sb(top, "x_all", [P, NT, D])
    deg_src = sb(top, "deg_src", [P, NT])
    deg_dst = sb(top, "deg_dst", [P, NT])
    mean = sb(top, "mean", [P, NT])
    var = sb(top, "var", [P, NT])
    rstd = sb(top, "rstd", [P, NT])

    with ExitStack() as c:
        it = sb(c, "it", [P, P], I32)
        ir = sb(c, "ir", [P, 1], I32)
        s_iota = sem("iota_made")
        POOL.iota(it[:], [[1, P]], 0, 0).then_inc(s_iota, 1)
        POOL.iota(ir[:], [[0, 1]], 0, 1).then_inc(s_iota, 1)
        DVE.wait_ge(s_iota, 2)
        V.go(DVE.memset(ones[:], 1.0))
        V.go(DVE.memset(zeros[:], 0.0))
        V.go(DVE.memset(zwide[:], 0.0))
        V.go(DVE.memset(window[:], 0.0))
        V.go(DVE.memset(x_all[:, NT - 1, :], 0.0))
        V.go(DVE.tensor_copy(iota_row[:], it[:]))
        V.run(DVE.tensor_copy(row_no[:], ir[:]))
        V.go(DVE.memset(zeros[:], 0.0))
        V.go(DVE.memset(zwide[:], 0.0))
        V.go(DVE.memset(window[:, NT - 1:NT], 1.0))
        V.go(DVE.tensor_scalar(ident[:], iota_row[:], row_no[:, 0:1], None, ALU.is_equal))
        V.run(DVE.tensor_scalar(before[:], iota_row[:], row_no[:, 0:1], None, ALU.is_gt))
        barrier()
    load(x_all[:, 0:NT - 1, :], a["x"][0:(NT - 1) * P, :].rearrange("(t p) d -> p t d", p=P))
    load(x_all[0:LAST, NT - 1, :], a["x"][(NT - 1) * P:N, :])
    loads_done(DVE)

    def bucket(tag, key, other, rows, cols, nch, clamp):
        lst = dram(f"list_{tag}", [P * nch, 2], I32)
        tile_of = dram(f"tile_of_{tag}", [1, nch], I32)
        tile_f = sb(top, "tile_f", [P, nch])
        with ExitStack() as c:
            k_i = sb(c, "k_i", [rows, cols], I32)
            t_i = sb(c, "t_i", [rows, cols], I32)
            t_f = sb(c, "t_f", [rows, cols])
            payload = sb(c, "payload", [rows, cols, 2], I32)
            o_i = sb(c, "o_i", [rows, cols], I32)
            same = sb(c, "same", [rows, cols])
            mask = sb(c, "mask", [rows, cols], U8)
            run_ = sb(c, "run", [rows, cols])
            pos = sb(c, "pos", [rows, cols])
            zero = sb(c, "zero", [rows, cols])
            total = sb(c, "total", [rows, NT])
            start = sb(c, "start", [rows, NT])
            cap_f = sb(c, "cap_f", [NT, 1])
            cap_i = sb(c, "cap_i", [NT, 1], I32)
            base = sb(c, "base", [NT, 1])
            end = sb(c, "end", [NT, 1])
            dbase = sb(c, "dbase", [NT, NT])
            chunk_i = sb(c, "chunk_i", [NT, nch], I32)
            ge = sb(c, "ge", [NT, nch])
            tl = sb(c, "tl", [1, nch], I32)
            empty = sb(c, "empty", [P, nch, 2], I32)
            stage_i = sb(c, "stage_i", [rows, 2, 8], I32)
            stage_p = sb(c, "stage_p", [rows, 2, 8, 2], I32)
            ps_a = ps(c, "ps_a", [P, 512])
            ps_b = ps(c, "ps_b", [P, 512])
            ps_t = ps(c, "ps_t", [P, 3, 512])
            cleared = sem("cleared")
            staged = [sem(f"staged{i}") for i in range(2)]
            written = [sem(f"written{i}") for i in range(2)]

            load(k_i[:], key)
            load(o_i[:], other)
            loads_done(DVE)
            V.go(DVE.memset(empty[:, :, 0], NP - 1))
            V.run(DVE.memset(empty[:, :, 1].bitcast(F32), -1.0))
            tell("v", "s")
            hear("v", "s")
            SP.dma_start(lst.rearrange("(p c) w -> p c w", p=P), empty[:]).then_inc(cleared, 16)
            if clamp:
                V.go(DVE.tensor_scalar(k_i[:], k_i[:], NP - 1, None, ALU.min))
                V.run(DVE.tensor_scalar(o_i[:], o_i[:], N - 1, None, ALU.min))
            V.go(DVE.tensor_scalar(t_i[:], k_i[:], 7, None, ALU.arith_shift_right))
            V.go(DVE.tensor_copy(payload[:, :, 0], o_i[:]))
            V.go(DVE.memset(zero[:], 0.0))
            V.run(DVE.tensor_scalar(k_i[:], k_i[:], 127, None, ALU.bitwise_and))
            V.go(DVE.tensor_copy(payload[:, :, 1].bitcast(F32), k_i[:]))
            V.run(DVE.tensor_copy(t_f[:], t_i[:]))
            for b in range(NT):
                V.run(DVE.tensor_scalar(same[:], t_f[:], float(b), 0.0, ALU.is_equal, ALU.add,
                                        accum_out=total[:, b:b + 1]))
            tell("v", "p")
            hear("v", "p")
            PE.matmul(ps_b[0:NT, 0:1], total[:], ones[0:rows, 0:1], start=True, stop=True).then_inc(links["p", "v"], 1)
            hear("p", "v")
            V.run(DVE.tensor_scalar(cap_i[:], ps_b[0:NT, 0:1], 127.0, None, ALU.add))
            V.run(DVE.tensor_scalar(cap_i[:], cap_i[:], 7, 7, ALU.arith_shift_right, ALU.arith_shift_left))
            V.run(DVE.tensor_copy(cap_f[:], cap_i[:]))
            tell("v", "p")
            hear("v", "p")
            PE.matmul(ps_b[0:NT, 1:2], before[0:NT, 0:NT], cap_f[:], start=True, stop=True).then_inc(links["p", "v"], 1)
            hear("p", "v")
            V.run(DVE.tensor_copy(base[:], ps_b[0:NT, 1:2]))
            V.go(DVE.tensor_tensor(end[:], base[:], cap_f[:], ALU.add))
            V.run(DVE.tensor_scalar(dbase[:], ident[0:NT, 0:NT], base[:, 0:1], None, ALU.mult))
            tell("v", "p")
            hear("v", "p")
            PE.matmul(ps_a[0:rows, 0:NT], before[0:rows, 0:rows], total[:], start=True, stop=False)
            PE.matmul(ps_a[0:rows, 0:NT], ones[0:NT, 0:rows], dbase[:], start=False, stop=True).then_inc(links["p", "v"], 1)
            hear("p", "v")
            V.run(DVE.tensor_scalar(start[:], ps_a[0:rows, 0:NT], -1.0, None, ALU.add))
            G.run(POOL.iota(chunk_i[:], [[P, nch]], 0, 0))
            tell("g", "v")
            hear("g", "v")
            V.run(DVE.tensor_scalar(ge[:], chunk_i[:], end[:, 0:1], None, ALU.is_ge))
            tell("v", "p")
            hear("v", "p")
            for q in range(0, nch, 512):
                w = min(512, nch - q)
                mm = PE.matmul(ps_t[:, q // 512, 0:w], ones[0:NT, :], ge[:, q:q + w], start=True, stop=True)
            mm.then_inc(links["p", "v"], 1)
            hear("p", "v")
            for q in range(0, nch, 512):
                w = min(512, nch - q)
                V.go(DVE.tensor_scalar(tile_f[:, q:q + w], ps_t[:, q // 512, 0:w], float(NT - 1), None, ALU.min))
            V.sync()
            V.run(DVE.tensor_copy(tl[:], tile_f[0:1, :]))
            tell("v", "s")
            hear("v", "s")
            SP.dma_start(tile_of, tl[:]).then_inc(load_sem, 16)
            loads[0] += 16
            for b in range(NT):
                V.go(DVE.tensor_scalar(mask[:], t_f[:], float(b), None, ALU.is_equal))
                V.run(DVE.tensor_scalar(same[:], t_f[:], float(b), None, ALU.is_equal))
                V.run(DVE.tensor_tensor_scan(run_[:], same[:], zero[:], start[:, b:b + 1], ALU.add, ALU.add))
                V.run(DVE.copy_predicated(pos[:], mask[:], run_[:]) if b else DVE.tensor_copy(pos[:], run_[:]))
            V.run(DVE.tensor_copy(k_i[:], pos[:]))
            V.go(DVE.tensor_scalar(t_i[:], k_i[:], 7, None, ALU.arith_shift_right))
            V.run(DVE.tensor_scalar(k_i[:], k_i[:], 127, None, ALU.bitwise_and))
            V.run(DVE.scalar_tensor_tensor(k_i[:], k_i[:], float(nch), t_i[:], ALU.mult, ALU.add))

            def stage(first, slot):
                V.go(DVE.tensor_copy(stage_i[:, slot, :], k_i[:, bass.ds(first, 8)]))
                V.run(DVE.tensor_copy(stage_p[:, slot], payload[:, bass.ds(first, 8), :]))
                DVE.sem_inc(staged[slot], 1)
                take(POOL, staged[slot])
                for j in range(8):
                    POOL.indirect_dma_start(
                        lst, bass.IndirectOffsetOnAxis(ap=stage_i[:, slot, j:j + 1], axis=0),
                        stage_p[:, slot, j, :], None).then_inc(written[slot], 16)

            POOL.wait_ge(cleared, 16)
            V.reset()
            for slot in range(2):
                stage(8 * slot, slot)
            V.reset()
            with nc.Fori(1, cols // 16) as i:
                for slot in range(2):
                    DVE.wait_ge(written[slot], i * 128)
                    stage(i * 16 + 8 * slot, slot)
                    V.reset()
            for slot in range(2):
                SP.wait_ge(written[slot], cols // 16 * 128)
            loads_done(SP)
            barrier()
        return lst, tile_of, tile_f

    def onehot(dst, low):
        return DVE.tensor_scalar(dst, iota_row[:], low, None, ALU.is_equal)

    def degrees(lst, tile_f, nch, deg):
        with ExitStack() as c:
            l_sb = sb(c, "l_sb", [P, nch, 2], I32)
            oh = sb(c, "oh_deg", [P, 2, U, P], BF16)
            at = sb(c, "at_deg", [P, 2, U, NT], BF16)
            cnt = ps(c, "cnt", [P, 512])
            made = sem("oh_made")
            free = sem("oh_free")
            load(l_sb[:], lst.rearrange("(p c) w -> p c w", p=P))
            loads_done(DVE)
            PE.matmul(cnt[:, 0:NT], zeros[:], zeros[:, 0:NT], start=True, stop=False)
            V.reset()
            DVE.sem_inc(free, 2)
            with nc.Fori(0, nch // (2 * U)) as i:
                for slot in range(2):
                    take(DVE, free)
                    for u in range(U):
                        j = (i * 2 + slot) * U + u
                        V.go(DVE.tensor_scalar(oh[:, slot, u, :], iota_row[:],
                                               l_sb[:, bass.ds(j, 1), 1].bitcast(F32), None, ALU.is_equal))
                        V.go(DVE.tensor_scalar(at[:, slot, u, :], iota_row[:, 0:NT],
                                               tile_f[:, bass.ds(j, 1)], None, ALU.is_equal))
                    V.sync()
                    DVE.sem_inc(made, 1)
                    V.reset()
                    take(PE, made)
                    for u in range(U):
                        mm = PE.matmul(cnt[:, 0:NT], oh[:, slot, u, :], at[:, slot, u, :], start=False, stop=False)
                    mm.then_inc(free, 1)
            PE.matmul(cnt[:, 0:NT], zeros[:], zeros[:, 0:NT], start=False, stop=True).then_inc(links["p", "v"], 1)
            hear("p", "v")
            take(DVE, free, 2)
            V.run(DVE.tensor_scalar(deg[:], cnt[:, 0:NT], 1.0, None, ALU.add))
            V.run(DVE.reciprocal(deg[:], deg[:]))
            tell("v", "a")
            hear("v", "a")
            S.run(ACTE.activation(deg[:], deg[:], ACT.Sqrt))
            barrier()

    def gather_sum(acc, table, lst, tile_of, nch):
        with ExitStack() as c:
            l_sb = sb(c, "l_sb", [P, nch, 2], I32)
            tl = sb(c, "tl", [1, nch], I32)
            idx = sb(c, "idx", [P, 2, U], I32)
            rows = sb(c, "rows", [P, 2, U, D])
            oh = sb(c, "oh", [P, 2, U, P])
            pp = ps(c, "pp", [P, 2, U, D])
            idx_made = [sem(f"idx_made{s}") for s in range(2)]
            got = [[sem(f"got{s}{u}") for u in range(U)] for s in range(2)]
            oh_made = sem("oh_made")
            summed = sem("summed")
            slot_free = sem("slot_free")
            rows_free = [sem(f"rows_free{s}") for s in range(2)]
            load(l_sb[:], lst.rearrange("(p c) w -> p c w", p=P))
            load(tl[:], tile_of)
            loads_done(DVE, ACTE)
            S.reset(); V.reset()
            for s in range(2):
                ACTE.sem_inc(rows_free[s], 1)
            DVE.sem_inc(slot_free, 2)
            with nc.Fori(0, nch // (2 * U)) as i:
                for s in range(2):
                    first = (i * 2 + s) * U
                    take(ACTE, rows_free[s])
                    S.run(ACTE.activation(idx[:, s, :], l_sb[:, bass.ds(first, U), 0], ACT.Copy))
                    ACTE.sem_inc(idx_made[s], 1)
                    S.reset()
                    take(POOL, idx_made[s])
                    for u in range(U):
                        POOL.indirect_dma_start(rows[:, s, u, :], None, table,
                                                bass.IndirectOffsetOnAxis(ap=idx[:, s, u:u + 1], axis=0)
                                                ).then_inc(got[s][u], 16)
                for s in range(2):
                    first = (i * 2 + s) * U
                    take(DVE, slot_free)
                    for u in range(U):
                        V.go(onehot(oh[:, s, u, :], l_sb[:, bass.ds(first + u, 1), 1].bitcast(F32)))
                    V.sync()
                    DVE.sem_inc(oh_made, 1)
                    V.reset()
                    take(PE, oh_made)
                    for u in range(U):
                        PE.wait_ge(got[s][u], i * 16 + 16)
                        mm = PE.matmul(pp[:, s, u, :], oh[:, s, u, :], rows[:, s, u, :], start=True, stop=True)
                    mm.then_inc(summed, 1)
                for s in range(2):
                    first = (i * 2 + s) * U
                    take(DVE, summed)
                    for u in range(U):
                        t = DVE.value_load(tl[0:1, bass.ds(first + u, 1)], min_val=0, max_val=NT - 1)
                        at = acc[:, bass.ds(t, 1), :]
                        V.run(DVE.tensor_tensor(at, at, pp[:, s, u, :], ALU.add))
                    DVE.sem_inc(slot_free, 1)
                    DVE.sem_inc(rows_free[s], 1)
                    V.reset()
            take(DVE, slot_free, 2)
            for s in range(2):
                take(ACTE, rows_free[s])
            barrier()


    def norm_stats():
        with ExitStack() as c:
            st = sb(c, "st", [P, NT, 6])
            tmp = sb(c, "tmp", [P, NT])
            V.reset()
            with DVE.Fori(0, NT) as t:
                V.run(DVE.bn_stats(st[:, bass.ds(t, 1), :], x_all[:, bass.ds(t, 1), :]))
                V.reset()
            V.go(DVE.tensor_tensor(mean[:], st[:, :, 1], st[:, :, 4], ALU.add))
            V.go(DVE.tensor_tensor(tmp[:], st[:, :, 1], st[:, :, 4], ALU.subtract))
            V.go(DVE.tensor_tensor(var[:], st[:, :, 2], st[:, :, 5], ALU.add))
            V.sync()
            V.go(DVE.tensor_scalar(mean[:], mean[:], 0.5, None, ALU.mult))
            V.run(DVE.tensor_tensor(tmp[:], tmp[:], tmp[:], ALU.mult))
            V.go(DVE.tensor_scalar(tmp[:], tmp[:], 0.25, None, ALU.mult))
            V.run(DVE.tensor_scalar(var[:], var[:], 1.0 / D, None, ALU.mult))
            V.run(DVE.tensor_tensor(var[:], var[:], tmp[:], ALU.add))
            V.run(DVE.tensor_scalar(rstd[:], var[:], LN_EPS, None, ALU.add))
            tell("v", "a")
            hear("v", "a")
            S.run(ACTE.activation(rstd[:], rstd[:], ACT.Sqrt))
            tell("a", "v")
            hear("a", "v")
            V.run(DVE.reciprocal(rstd[:], rstd[:]))
            barrier()

    def one(x, t):
        return x[:, t:t + 1] if isinstance(t, int) else x[:, bass.ds(t, 1)]

    def row(x, t):
        return x[:, t, :] if isinstance(t, int) else x[:, bass.ds(t, 1), :]

    def normalize(dst, t, scale=None):
        return DVE.tensor_scalar(dst, row(x_all, t), one(mean, t), one(rstd, t), ALU.subtract, ALU.mult)

    def transpose(dst_ps, src, blocks):
        for k in range(blocks):
            last = PE.transpose(dst_ps[:, k * P:(k + 1) * P], src[:, k * P:(k + 1) * P], ident[:])
        return last

    def broadcast_row(dst, src, width):
        load(dst, src.broadcast_to([P, width]))

    def tile_rows(x):
        return x.rearrange("(t p) d -> p t d", p=P)

    P2V, P2A = ("p", "v"), ("p", "a")

    def gcn0_table(acc, table, z_scale, cov, zmean):
        with ExitStack() as c:
            w0t = sb(c, "w0t", [P, 2, D])
            xn = sb(c, "xn", [P, D])
            z = sb(c, "z", [P, D + 1])
            xnt = sb(c, "xnt", [P, D])
            ps_x = ps(c, "ps_x", [P, 512])
            ps_h = ps(c, "ps_h", [P, 512])
            gram = ps(c, "gram", [P, 2, 512])
            tmp = sb(c, "tmp", [P, NT])
            tm2 = sb(c, "tm2", [P, NT])
            nrm = sb(c, "nrm", [P, NT])
            msk = sb(c, "msk", [P, NT])
            load(w0t[:], a["w0t"].rearrange("(k p) d -> p k d", p=P))
            loads_done(PE)
            tell("v", "a"); hear("v", "a")
            S.run(ACTE.activation(nrm[:], var[:], ACT.Sqrt, scale=float(D)))
            tell("a", "v"); hear("a", "v")
            V.run(DVE.tensor_tensor(nrm[:], nrm[:], rstd[:], ALU.mult))
            V.go(DVE.tensor_scalar(msk[:], nrm[:], MAXNORM, None, ALU.is_gt))
            V.go(DVE.tensor_scalar(tmp[:], nrm[:], MAXNORM, None, ALU.min))
            V.run(DVE.tensor_scalar(nrm[:], nrm[:], MIN_NORM, None, ALU.max))
            V.go(DVE.tensor_scalar(tm2[:], tmp[:], -1.0, 1.0, ALU.mult, ALU.add))
            V.run(DVE.tensor_scalar(tmp[:], tmp[:], 1.0, None, ALU.add))
            V.run(DVE.reciprocal(tm2[:], tm2[:]))
            V.run(DVE.tensor_tensor(tmp[:], tmp[:], tm2[:], ALU.mult))
            tell("v", "a"); hear("v", "a")
            S.run(ACTE.activation(tmp[:], tmp[:], ACT.Ln))
            tell("a", "v"); hear("a", "v")
            V.run(DVE.tensor_scalar(tmp[:], tmp[:], 0.5, None, ALU.mult))
            V.go(DVE.tensor_scalar(tm2[:], msk[:], ATANH_MAX, None, ALU.mult))
            V.run(DVE.tensor_scalar(msk[:], msk[:], -1.0, 1.0, ALU.mult, ALU.add))
            V.run(DVE.tensor_tensor(tmp[:], tmp[:], msk[:], ALU.mult))
            V.run(DVE.tensor_tensor(tmp[:], tmp[:], tm2[:], ALU.add))
            V.run(DVE.reciprocal(nrm[:], nrm[:]))
            V.run(DVE.tensor_tensor(z_scale[:], tmp[:], nrm[:], ALU.mult))
            V.run(DVE.memset(z[:, D:D + 1], 1.0))
            for k in range(2):
                PE.matmul(gram[:, k, 0:D + 1], zeros[:], zwide[:, 0:D + 1], start=True, stop=False)

            def body(t, slot, last):
                V.run(normalize(xn[:], t))
                V.run(DVE.tensor_scalar(z[:, 0:D], xn[:], one(z_scale, t), None, ALU.mult))
                tell("v", "p"); hear("v", "p")
                transpose(ps_x, xn, 2).then_inc(links["p", "a"], 1)
                for k in range(2):
                    mm = PE.matmul(gram[:, k, 0:D + 1], z[:, k * P:(k + 1) * P], z[:], start=False, stop=False)
                hear("p", "a")
                S.run(ACTE.activation(xnt[:], ps_x[:, 0:D], ACT.Copy))
                tell("a", "p"); hear("a", "p")
                for k in range(2):
                    mm = PE.matmul(ps_h[:, 0:D], xnt[:, k * P:(k + 1) * P], w0t[:, k, :], start=(k == 0), stop=(k == 1))
                mm.then_inc(links["p", "v"], 1)
                hear("p", "v")
                V.run(DVE.tensor_scalar(row(acc, t), ps_h[:, 0:D], one(deg_src, t), None, ALU.mult))
            tiles(body)
            for k in range(2):
                mm = PE.matmul(gram[:, k, 0:D + 1], zeros[:], z[:], start=False, stop=True)
            mm.then_inc(links["p", "v"], 1)
            hear("p", "v")
            mr = sb(c, "mr", [P, 2, D])
            dm = sb(c, "dm", [P, 2, P])
            for k in range(2):
                V.run(DVE.tensor_scalar(zmean[:, k, :], gram[:, k, D:D + 1], 1.0 / N, None, ALU.mult))
                V.run(DVE.tensor_scalar(dm[:, k, :], ident[:], zmean[:, k, 0:1], None, ALU.mult))
                V.run(DVE.tensor_scalar(cov[:, k, :], gram[:, k, 0:D], 1.0 / N, None, ALU.mult))
            tell("v", "p"); hear("v", "p")
            for k in range(2):
                mm = PE.matmul(ps_h[:, k * P:(k + 1) * P], ones[:], dm[:, k, :], start=True, stop=True)
            mm.then_inc(links["p", "v"], 1)
            hear("p", "v")
            for k in range(2):
                V.run(DVE.tensor_scalar(mr[:, k, :], ps_h[:, 0:D], zmean[:, k, 0:1], None, ALU.mult))
                V.run(DVE.tensor_tensor(cov[:, k, :], cov[:, k, :], mr[:, k, :], ALU.subtract))
            tell("v", "s"); hear("v", "s")
            load(tile_rows(table), acc[:])
            loads_done(SP)
            barrier()

    C3 = 768

    def mix0(z_scale, cov, zmean):
        with ExitStack() as c:
            wq = sb(c, "wq", [P, 2, C3])
            vec = sb(c, "vec", [P, C3])
            bias = sb(c, "bias", [P, C3])
            prod = sb(c, "prod", [P, 2, C3])
            mb = sb(c, "mb", [P, 2, P])
            pw = sb(c, "pw", [P, 6, P])
            dw = sb(c, "dw", [P, 6])
            rest = sb(c, "rest", [P, 4, D])
            bres = sb(c, "bres", [P, D])
            xn = sb(c, "xn", [P, D])
            zt = sb(c, "zt", [P, D])
            y = sb(c, "y", [P, 2 * C3])
            rt = sb(c, "rt", [P, C3])
            sq = sb(c, "sq", [P, C3])
            kk = sb(c, "kk", [P, 16, 32])
            dots = sb(c, "dots", [P, 16])
            den = sb(c, "den", [P, 16, 32])
            vv = sb(c, "vv", [P, 16, 32])
            o = sb(c, "o", [P, 512])
            ot = sb(c, "ot", [P, 512])
            ft = sb(c, "ft", [P, D])
            nn = sb(c, "nn", [P, 12])
            ps_a = ps(c, "ps_a", [P, 2, 512])
            ps_b = ps(c, "ps_b", [P, 2, 512])
            ps_c = ps(c, "ps_c", [P, 2, 512])
            ps_d = ps(c, "ps_d", [P, 512])
            V.run(DVE.memset(pw[:], 0.0))
            tell("v", "s"); hear("v", "s")
            load(wq[:], a["qkvt"].rearrange("(k p) d -> p k d", p=P))
            load(dw[:], a["dw"])
            for g in range(4):
                load(pw[32 * g:32 * g + 32, :, 32 * g:32 * g + 32],
                     a["pwt"].rearrange("(b g) i o -> g i b o", g=4)[g])
            load(rest[:], a["rest"].rearrange("(k p) d -> p k d", p=P))
            broadcast_row(bres[:], a["bres"], D)
            broadcast_row(vec[:], a["gamma"], C3)
            broadcast_row(bias[:], a["beta"], C3)
            loads_done(DVE, PE)
            for b in range(6):
                V.go(DVE.tensor_scalar(pw[:, b, :], pw[:, b, :], dw[:, b:b + 1], None, ALU.mult))
            for k in range(2):
                V.go(DVE.tensor_scalar(mb[:, k, :], ones[:], zmean[:, k, 0:1], None, ALU.mult))
            V.sync()
            tell("v", "p"); hear("v", "p")
            H = C3 // 2
            for m in range(2):
                for h in range(2):
                    for k in range(2):
                        mm = PE.matmul((ps_a if m == 0 else ps_b)[:, h, 0:H], cov[:, k, m * P:(m + 1) * P],
                                       wq[:, k, h * H:(h + 1) * H], start=(k == 0), stop=(k == 1))
            for h in range(2):
                for k in range(2):
                    mm = PE.matmul(ps_c[:, h, 0:H], mb[:, k, :], wq[:, k, h * H:(h + 1) * H],
                                   start=(k == 0), stop=(k == 1))
            mm.then_inc(links["p", "v"], 1)
            hear("p", "v")
            for m in range(2):
                V.go(DVE.tensor_tensor(prod[:, m, :].rearrange("p (h w) -> p h w", h=2), (ps_a if m == 0 else ps_b)[:, :, 0:H],
                                       wq[:, m, :].rearrange("p (h w) -> p h w", h=2), ALU.mult))
            V.sync()
            tell("v", "p"); hear("v", "p")
            for h in range(2):
                for m in range(2):
                    mm = PE.matmul(ps_a[:, h, 0:H], ones[:], prod[:, m, h * H:(h + 1) * H], start=(m == 0), stop=(m == 1))
            mm.then_inc(links["p", "v"], 1)
            hear("p", "v")
            var_row = prod[:, 0, :].rearrange("p (h w) -> p h w", h=2)
            V.run(DVE.tensor_scalar(var_row, ps_a[:, :, 0:H], 0.0, LN_EPS, ALU.max, ALU.add))
            tell("v", "a"); hear("v", "a")
            S.run(ACTE.activation(prod[:, 0, :], prod[:, 0, :], ACT.Sqrt))
            tell("a", "v"); hear("a", "v")
            V.run(DVE.reciprocal(prod[:, 0, :], prod[:, 0, :]))
            V.run(DVE.tensor_tensor(vec[:], vec[:], prod[:, 0, :], ALU.mult))
            V.run(DVE.tensor_tensor(prod[:, 1, :].rearrange("p (h w) -> p h w", h=2), ps_c[:, :, 0:H],
                                    vec[:].rearrange("p (h w) -> p h w", h=2), ALU.mult))
            V.go(DVE.tensor_tensor(bias[:], bias[:], prod[:, 1, :], ALU.subtract))
            for k in range(2):
                V.go(DVE.tensor_tensor(wq[:, k, :], wq[:, k, :], vec[:], ALU.mult))
            V.sync()
            qkv = y[:].rearrange("p (g s j) -> p g s j", g=16, s=3)

            def body(t, slot, last):
                V.run(normalize(xn[:], t))
                V.run(DVE.tensor_scalar(xn[:], xn[:], one(z_scale, t), None, ALU.mult))
                tell("v", "p"); hear("v", "p")
                transpose(ps_d, xn, 2).then_inc(links["p", "a"], 1)
                hear("p", "a")
                S.run(ACTE.activation(zt[:], ps_d[:, 0:D], ACT.Copy))
                tell("a", "p"); hear("a", "p")
                for h in range(2):
                    for k in range(2):
                        mm = PE.matmul(ps_a[:, h, 0:H], zt[:, k * P:(k + 1) * P], wq[:, k, h * H:(h + 1) * H],
                                       start=(k == 0), stop=(k == 1))
                mm.then_inc(links["p", "v"], 1)
                hear("p", "v")
                r = y[:, 0:C3]
                V.run(DVE.tensor_tensor(r.rearrange("p (h w) -> p h w", h=2), ps_a[:, :, 0:H],
                                        bias[:].rearrange("p (h w) -> p h w", h=2), ALU.add))
                V.run(DVE.tensor_scalar(r, r, 0.0, None, ALU.max))
                tell("v", "p"); hear("v", "p")
                tell("v", "a")
                for b in range(6):
                    tr = PE.transpose(ps_b[:, b // 4, (b % 4) * P:(b % 4 + 1) * P], y[:, b * P:(b + 1) * P], ident[:])
                tr.then_inc(links["p", "a"], 1)
                hear("v", "a")
                S.run(ACTE.activation(sq[:], r, ACT.Square, accum_out=nn[:, 0:1]))
                hear("p", "a")
                S.go(ACTE.activation(rt[:, 0:512], ps_b[:, 0, :], ACT.Copy))
                S.run(ACTE.activation(rt[:, 512:C3], ps_b[:, 1, 0:256], ACT.Copy))
                tell("a", "p"); hear("a", "p")
                for b in range(6):
                    mm = PE.matmul(ps_c[:, b // 4, (b % 4) * P:(b % 4 + 1) * P], rt[:, b * P:(b + 1) * P], pw[:, b, :],
                                   start=True, stop=True)
                mm.then_inc(links["p", "a"], 1)
                hear("p", "a")
                S.go(ACTE.activation(y[:, C3:C3 + 512], ps_c[:, 0, :], ACT.Copy))
                S.run(ACTE.activation(y[:, C3 + 512:2 * C3], ps_c[:, 1, 0:256], ACT.Copy))
                S.run(ACTE.activation(sq[:], y[:, C3:2 * C3], ACT.Square, accum_out=nn[:, 1:2]))
                tell("a", "v"); hear("a", "v")
                V.run(DVE.tensor_tensor(nn[:, 2:3], nn[:, 0:1], nn[:, 1:2], ALU.add))
                tell("v", "a"); hear("v", "a")
                S.run(ACTE.activation(nn[:, 3:4], nn[:, 2:3], ACT.Sqrt))
                tell("a", "v")
                V.go(DVE.tensor_scalar(kk[:], qkv[:, :, 1, :], 0.0, None, ALU.max))
                V.sync()
                V.run(DVE.tensor_reduce(dots[:], kk[:], AX.X, ALU.add))
                hear("a", "v")
                V.run(DVE.tensor_scalar(nn[:, 3:4], nn[:, 3:4], MIN_NORM, None, ALU.max))
                V.run(DVE.reciprocal(nn[:, 3:4], nn[:, 3:4]))
                V.run(DVE.tensor_scalar(nn[:, 3:4], nn[:, 3:4], ATANH_MAX, 1.0, ALU.mult, ALU.min))
                V.go(DVE.tensor_scalar(dots[:], dots[:], nn[:, 3:4], nn[:, 3:4], ALU.mult, ALU.mult))
                V.go(DVE.tensor_scalar(vv[:], qkv[:, :, 2, :], nn[:, 3:4], None, ALU.mult))
                V.run(DVE.tensor_scalar(den[:], qkv[:, :, 2, :], nn[:, 3:4], 1e-15, ALU.mult, ALU.add))
                V.go(DVE.reciprocal(den[:], den[:]))
                V.run(DVE.scalar_tensor_tensor(vv[:], qkv[:, :, 0, :], 0.0, vv[:], ALU.max, ALU.mult))
                V.run(DVE.tensor_tensor(vv[:], vv[:], dots[:].unsqueeze(2).broadcast_to([P, 16, 32]), ALU.mult))
                V.run(DVE.tensor_tensor(o[:].rearrange("p (g j) -> p g j", g=16), vv[:], den[:], ALU.mult))
                tell("v", "p"); hear("v", "p")
                transpose(ps_d, o, 4).then_inc(links["p", "a"], 1)
                tell("v", "a"); hear("v", "a")
                S.run(ACTE.activation(sq[:, 0:512], o[:], ACT.Square, accum_out=nn[:, 4:5]))
                S.run(ACTE.activation(nn[:, 5:6], nn[:, 4:5], ACT.Sqrt))
                hear("p", "a")
                S.run(ACTE.activation(ot[:], ps_d[:], ACT.Copy))
                tell("a", "p"); hear("a", "p")
                tell("a", "v"); hear("a", "v")
                for k in range(4):
                    mm = PE.matmul(ps_a[:, 0, 0:D], ot[:, k * P:(k + 1) * P], rest[:, k, :], start=(k == 0), stop=(k == 3))
                mm.then_inc(links["p", "v"], 1)
                V.run(DVE.tensor_scalar(nn[:, 5:6], nn[:, 5:6], MIN_NORM, None, ALU.max))
                V.run(DVE.reciprocal(nn[:, 5:6], nn[:, 5:6]))
                V.run(DVE.tensor_scalar(nn[:, 5:6], nn[:, 5:6], ATANH_MAX, 1.0, ALU.mult, ALU.min))
                hear("p", "v")
                V.run(DVE.scalar_tensor_tensor(ft[:], ps_a[:, 0, 0:D], nn[:, 5:6], bres[:], ALU.mult, ALU.add))
                tell("v", "a"); hear("v", "a")
                S.run(ACTE.activation(sq[:, 0:D], ft[:], ACT.Square, accum_out=nn[:, 6:7]))
                S.run(ACTE.activation(nn[:, 7:8], nn[:, 6:7], ACT.Sqrt))
                S.run(ACTE.activation(nn[:, 8:9], nn[:, 7:8], ACT.Tanh))
                tell("a", "v"); hear("a", "v")
                V.go(DVE.tensor_scalar(nn[:, 8:9], nn[:, 8:9], MAXNORM, None, ALU.min))
                V.run(DVE.tensor_scalar(nn[:, 7:8], nn[:, 7:8], MIN_NORM, None, ALU.max))
                V.run(DVE.reciprocal(nn[:, 7:8], nn[:, 7:8]))
                V.run(DVE.tensor_tensor(nn[:, 9:10], nn[:, 7:8], nn[:, 8:9], ALU.mult))
                V.run(DVE.scalar_tensor_tensor(row(x_all, t), ft[:], nn[:, 9:10], row(x_all, t), ALU.mult, ALU.add))
            tiles(body)
            barrier()

    def add_scaled(acc, deg):
        with DVE.Fori(0, NT) as t:
            V.run(DVE.scalar_tensor_tensor(row(x_all, t), row(acc, t), one(deg, t), row(x_all, t), ALU.mult, ALU.add))
            V.reset()

    GH = 4
    TW = 20

    def leaky(dst, src):
        return DVE.scalar_tensor_tensor(dst, src, 0.2, src, ALU.mult, ALU.max)

    def gat_scores(lst, tile_of, nch, gate):
        with ExitStack() as c:
            wg = sb(c, "wg", [P, 2, 16])
            att = sb(c, "att", [P, 2, 16])
            bg = sb(c, "bg", [P, 3, 16])
            node = sb(c, "node", [P, NT, TW])
            pr = sb(c, "pr", [P, NT, 16])
            dm = sb(c, "dm", [P, NT, 8])
            top = sb(c, "topv", [P, NT, GH])
            least = sb(c, "least", [P, 1])
            shift = sb(c, "shift", [P, 1])
            sums = sb(c, "sums", [P, NT, TW])
            rows_all = sb(c, "rows_all", [P, nch, TW])
            l_sb = sb(c, "l_sb", [P, nch, 2], I32)
            tl = sb(c, "tl", [1, nch], I32)
            load(wg[:], a["wgat"].rearrange("(k p) d -> p k d", p=P))
            broadcast_row(att[:, 0, :], a["att_src"], 16)
            broadcast_row(att[:, 1, :], a["att_dst"], 16)
            for q, n in enumerate(("bgat", "lng", "lnb")):
                broadcast_row(bg[:, q, :], a[n], 16)
            load(l_sb[:], lst.rearrange("(p c) w -> p c w", p=P))
            load(tl[:], tile_of)
            loads_done(DVE, PE, ACTE)
            table = dram("gat_table", [NP, TW])
            with ExitStack() as d:
                xn = sb(d, "xn", [P, D])
                xnt = sb(d, "xnt", [P, D])
                ps_x = ps(d, "ps_x", [P, 512])
                ps_h = ps(d, "ps_h", [P, 512])

                def body(t, slot, last):
                    V.run(normalize(xn[:], t))
                    tell("v", "p"); hear("v", "p")
                    transpose(ps_x, xn, 2).then_inc(links["p", "a"], 1)
                    hear("p", "a")
                    S.run(ACTE.activation(xnt[:], ps_x[:, 0:D], ACT.Copy))
                    tell("a", "p"); hear("a", "p")
                    for k in range(2):
                        mm = PE.matmul(ps_h[:, 0:16], xnt[:, k * P:(k + 1) * P], wg[:, k, :], start=(k == 0), stop=(k == 1))
                    mm.then_inc(links["p", "v"], 1)
                    hear("p", "v")
                    at = node[:, t, 0:16] if isinstance(t, int) else node[:, bass.ds(t, 1), 0:16]
                    V.run(DVE.tensor_copy(at, ps_h[:, 0:16]))
                tiles(body)
                for q, dst in enumerate((node[:, :, 16:20], dm[:, :, 0:4])):
                    V.run(DVE.tensor_tensor(pr[:], node[:, :, 0:16], att[:, q, :].unsqueeze(1).broadcast_to([P, NT, 16]), ALU.mult))
                    V.run(DVE.tensor_reduce(dst, pr[:].rearrange("p t (h j) -> p t h j", h=GH), AX.X, ALU.add))
                V.run(DVE.tensor_reduce(least[:], node[:, :, 16:20], AX.XY, ALU.min))
                tell("v", "p"); hear("v", "p")
                PE.transpose(ps_x[0:1, 0:P], least[:], ident[:]).then_inc(links["p", "v"], 1)
                hear("p", "v")
                V.run(DVE.tensor_reduce(least[0:1, :], ps_x[0:1, 0:P], AX.X, ALU.min))
                tell("v", "p"); hear("v", "p")
                PE.matmul(ps_h[:, 0:1], ones[0:1, :], least[0:1, :], start=True, stop=True).then_inc(links["p", "v"], 1)
                hear("p", "v")
                V.run(DVE.tensor_scalar(shift[:], ps_h[:, 0:1], -1.0, 1.0, ALU.mult, ALU.add))
                V.run(DVE.tensor_scalar(top[:], node[:, :, 16:20], shift[:, 0:1], None, ALU.add))
                tell("v", "s"); hear("v", "s")
                load(tile_rows(table), node[:])
                loads_done(SP)
                barrier()
            with ExitStack() as d:
                idx = sb(d, "idx", [P, 2, U], I32)
                rows = sb(d, "rows", [P, 2, U, TW])
                oh = sb(d, "oh", [P, 2, U, P])
                sv = sb(d, "sv", [P, 2, U, GH])
                diag = sb(d, "diag", [P, U, GH, P])
                mx = sb(d, "mx", [P, U, GH])
                pp = ps(d, "pp", [P, 2, U, 512])
                idx_made = [sem(f"gat_idx_made{s}") for s in range(2)]
                got = [sem(f"gat_got{s}") for s in range(2)]
                rows_free = [sem(f"gat_rows_free{s}") for s in range(2)]
                slot_free = sem("gat_slot_free")
                sv_made = sem("gat_sv_made")
                diag_made = sem("gat_diag_made")
                diag_free = sem("gat_diag_free")
                summed = sem("gat_summed")
                for s in range(2):
                    ACTE.sem_inc(rows_free[s], 1)
                DVE.sem_inc(slot_free, 2)
                ACTE.sem_inc(diag_free, 1)
                S.reset(); V.reset()
                with nc.Fori(0, nch // (2 * U)) as i:
                    for s in range(2):
                        first = (i * 2 + s) * U
                        take(ACTE, rows_free[s])
                        S.run(ACTE.activation(idx[:, s, :], l_sb[:, bass.ds(first, U), 0], ACT.Copy))
                        ACTE.sem_inc(idx_made[s], 1)
                        S.reset()
                        take(POOL, idx_made[s])
                        for u in range(U):
                            POOL.indirect_dma_start(rows[:, s, u, :], None, table,
                                                    bass.IndirectOffsetOnAxis(ap=idx[:, s, u:u + 1], axis=0)
                                                    ).then_inc(got[s], 16)
                    for s in range(2):
                        first = (i * 2 + s) * U
                        take(DVE, slot_free)
                        for u in range(U):
                            V.go(DVE.tensor_scalar(oh[:, s, u, :], iota_row[:], l_sb[:, bass.ds(first + u, 1), 1].bitcast(F32),
                                                   None, ALU.is_equal))
                        V.sync()
                        DVE.wait_ge(got[s], i * (16 * U) + 16 * U)
                        V.go(DVE.tensor_scalar(sv[:, s], rows[:, s, :, 16:20], shift[:, 0:1], None, ALU.add))
                        V.run(DVE.tensor_copy(rows_all[:, bass.ds(first, U), :], rows[:, s]))
                        DVE.sem_inc(sv_made, 1)
                        DVE.sem_inc(rows_free[s], 1)
                        V.reset()
                        take(ACTE, sv_made)
                        take(ACTE, diag_free)
                        for u in range(U):
                            for h in range(GH):
                                S.go(ACTE.activation(diag[:, u, h, :], ident[:], ACT.Copy, scale=sv[:, s, u, h:h + 1]))
                        S.sync()
                        ACTE.sem_inc(diag_made, 1)
                        S.reset()
                        take(PE, diag_made)
                        for u in range(U):
                            mm = PE.matmul(pp[:, s, u, :], oh[:, s, u, :], diag[:, u].rearrange("p h j -> p (h j)"),
                                           start=True, stop=True)
                        mm.then_inc(summed, 1)
                    for s in range(2):
                        first = (i * 2 + s) * U
                        take(DVE, summed)
                        DVE.sem_inc(diag_free, 1)
                        V.run(DVE.tensor_reduce(mx[:], pp[:, s].rearrange("p u (h j) -> p u h j", h=GH), AX.X, ALU.max))
                        for u in range(U):
                            t = DVE.value_load(tl[0:1, bass.ds(first + u, 1)], min_val=0, max_val=NT - 1)
                            at = top[:, bass.ds(t, 1), :]
                            V.run(DVE.tensor_tensor(at, at, mx[:, u, :], ALU.max))
                        DVE.sem_inc(slot_free, 1)
                        V.reset()
                take(DVE, slot_free, 2)
                for s in range(2):
                    take(ACTE, rows_free[s])
                take(ACTE, diag_free)
                barrier()
            sl = sb(c, "sl", [P, NT, GH])
            V.run(DVE.tensor_scalar(top[:], top[:], shift[:, 0:1], None, ALU.subtract))
            V.run(DVE.tensor_tensor(top[:], top[:], dm[:, :, 0:4], ALU.add))
            V.run(leaky(dm[:, :, 4:8], top[:]))
            V.run(DVE.tensor_tensor(sl[:], node[:, :, 16:20], dm[:, :, 0:4], ALU.add))
            V.run(leaky(top[:], sl[:]))
            V.run(DVE.tensor_tensor(top[:], top[:], dm[:, :, 4:8], ALU.subtract))
            V.run(DVE.tensor_scalar(top[:], top[:], 0.0, None, ALU.min))
            tell("v", "a"); hear("v", "a")
            S.run(ACTE.activation(sums[:, :, 16:20], top[:], ACT.Exp))
            tell("a", "v"); hear("a", "v")
            V.run(DVE.tensor_tensor(sums[:, :, 0:16].rearrange("p t (h j) -> p t h j", h=GH),
                                    node[:, :, 0:16].rearrange("p t (h j) -> p t h j", h=GH),
                                    sums[:, :, 16:20].unsqueeze(3).broadcast_to([P, NT, GH, GH]), ALU.mult))
            W = 2 * U
            with ExitStack() as d:
                oh = sb(d, "oh", [P, 2, W, P])
                oht = sb(d, "oht", [P, 2, W, P])
                tgt = sb(d, "tgt", [P, 2, W, 8])
                lg = sb(d, "lg", [P, 2, W, GH])
                ex = sb(d, "ex", [P, 2, W, GH])
                msg = sb(d, "msg", [P, 2, W, TW])
                ps_t = ps(d, "ps_t", [P, 2, 2, 512])
                ps_m = ps(d, "ps_m", [P, 2, 512])
                ps_s = ps(d, "ps_s", [P, 2, 512])
                v2p = sem("gat2_onehots")
                p2a = sem("gat2_turned")
                a2p = sem("gat2_turned_copied")
                p2v = sem("gat2_targets")
                v2a = sem("gat2_logits")
                a2v = sem("gat2_weights")
                v2p2 = sem("gat2_messages")
                p2v2 = sem("gat2_sums")
                S.reset(); V.reset()
                with nc.Fori(0, nch // (2 * W)) as i:
                    for s in range(2):
                        first = (i * 2 + s) * W
                        for w in range(W):
                            V.go(DVE.tensor_scalar(oh[:, s, w, :], iota_row[:], l_sb[:, bass.ds(first + w, 1), 1].bitcast(F32),
                                                   None, ALU.is_equal))
                            t = DVE.value_load(tl[0:1, bass.ds(first + w, 1)], min_val=0, max_val=NT - 1)
                            V.go(DVE.tensor_copy(tgt[:, s, w, :], dm[:, bass.ds(t, 1), :]))
                        V.sync()
                        DVE.sem_inc(v2p, 1)
                        V.reset()
                        take(PE, v2p)
                        for w in range(W):
                            tr = PE.transpose(ps_t[:, s, w // 4, (w % 4) * P:(w % 4 + 1) * P], oh[:, s, w, :], ident[:])
                        tr.then_inc(p2a, 1)
                        take(ACTE, p2a)
                        S.run(ACTE.activation(oht[:, s].rearrange("p (b w) j -> p b (w j)", b=2), ps_t[:, s], ACT.Copy))
                        ACTE.sem_inc(a2p, 1)
                        S.reset()
                    for s in range(2):
                        take(PE, a2p)
                        for w in range(W):
                            mm = PE.matmul(ps_m[:, s, 8 * w:8 * w + 8], oht[:, s, w, :], tgt[:, s, w, :], start=True, stop=True)
                        mm.then_inc(p2v, 1)
                    for s in range(2):
                        first = (i * 2 + s) * W
                        pm = ps_m[:, s, 0:8 * W].rearrange("p (w j) -> p w j", j=8)
                        take(DVE, p2v)
                        V.run(DVE.tensor_tensor(lg[:, s], rows_all[:, bass.ds(first, W), 16:20], pm[:, :, 0:4], ALU.add))
                        V.run(leaky(ex[:, s], lg[:, s]))
                        V.run(DVE.tensor_tensor(lg[:, s], ex[:, s], pm[:, :, 4:8], ALU.subtract))
                        V.run(DVE.tensor_scalar(lg[:, s], lg[:, s], 0.0, None, ALU.min))
                        DVE.sem_inc(v2a, 1)
                        V.reset()
                        take(ACTE, v2a)
                        S.run(ACTE.activation(msg[:, s, :, 16:20], lg[:, s], ACT.Exp))
                        ACTE.sem_inc(a2v, 1)
                        S.reset()
                    for s in range(2):
                        first = (i * 2 + s) * W
                        take(DVE, a2v)
                        for h in range(GH):
                            V.go(DVE.tensor_tensor(msg[:, s, :, 4 * h:4 * h + 4], rows_all[:, bass.ds(first, W), 4 * h:4 * h + 4],
                                                   msg[:, s, :, 16 + h:17 + h].broadcast_to([P, W, GH]), ALU.mult))
                        V.sync()
                        DVE.sem_inc(v2p2, 1)
                        V.reset()
                        take(PE, v2p2)
                        for w in range(W):
                            mm = PE.matmul(ps_s[:, s, 32 * w:32 * w + TW], oh[:, s, w, :], msg[:, s, w, :], start=True, stop=True)
                        mm.then_inc(p2v2, 1)
                    for s in range(2):
                        first = (i * 2 + s) * W
                        take(DVE, p2v2)
                        for w in range(W):
                            t = DVE.value_load(tl[0:1, bass.ds(first + w, 1)], min_val=0, max_val=NT - 1)
                            at = sums[:, bass.ds(t, 1), :]
                            V.run(DVE.tensor_tensor(at, at, ps_s[:, s, 32 * w:32 * w + TW], ALU.add))
                        V.reset()
                barrier()
            den = sb(c, "den", [P, NT, GH])
            sc = sb(c, "sc", [P, NT, GH])
            m1 = sb(c, "m1", [P, NT])
            v1 = sb(c, "v1", [P, NT])

            def over_nodes(q):
                return bg[:, q, :].unsqueeze(1).broadcast_to([P, NT, 16])

            def per_node(x):
                return x[:].unsqueeze(2).broadcast_to([P, NT, 16])
            V.run(DVE.tensor_scalar(den[:], sums[:, :, 16:20], 1e-16, None, ALU.add))
            V.run(DVE.reciprocal(den[:], den[:]))
            V.run(DVE.tensor_tensor(pr[:].rearrange("p t (h j) -> p t h j", h=GH),
                                    sums[:, :, 0:16].rearrange("p t (h j) -> p t h j", h=GH),
                                    den[:].unsqueeze(3).broadcast_to([P, NT, GH, GH]), ALU.mult))
            V.run(DVE.tensor_tensor(pr[:], pr[:], over_nodes(0), ALU.add))
            V.run(DVE.tensor_reduce(m1[:], pr[:], AX.X, ALU.add))
            V.run(DVE.tensor_scalar(m1[:], m1[:], 1.0 / 16, None, ALU.mult))
            V.run(DVE.tensor_tensor(pr[:], pr[:], per_node(m1), ALU.subtract))
            V.run(DVE.tensor_tensor(sums[:, :, 0:16], pr[:], pr[:], ALU.mult))
            V.run(DVE.tensor_reduce(v1[:], sums[:, :, 0:16], AX.X, ALU.add))
            V.run(DVE.tensor_scalar(v1[:], v1[:], 1.0 / 16, LN_EPS, ALU.mult, ALU.add))
            tell("v", "a"); hear("v", "a")
            S.run(ACTE.activation(v1[:], v1[:], ACT.Sqrt))
            tell("a", "v"); hear("a", "v")
            V.run(DVE.reciprocal(v1[:], v1[:]))
            V.run(DVE.tensor_tensor(pr[:], pr[:], per_node(v1), ALU.mult))
            V.run(DVE.tensor_tensor(pr[:], pr[:], over_nodes(1), ALU.mult))
            V.run(DVE.tensor_tensor(pr[:], pr[:], over_nodes(2), ALU.add))
            V.run(DVE.tensor_reduce(sc[:], pr[:].rearrange("p t (h j) -> p t j h", h=GH), AX.X, ALU.add))
            V.run(DVE.tensor_scalar(sc[:], sc[:], 1.0 / GH, None, ALU.mult))
            top2(sc, gate, GH)
            barrier()

    def top2(sc, gate, n):
        with ExitStack() as c:
            earlier = sb(c, "earlier", [P, n, n])
            gt = sb(c, "gt", [P, NT, n, n])
            eq = sb(c, "eq", [P, NT, n, n])
            rank = sb(c, "rank", [P, NT, n])
            m = sb(c, "m", [P, NT])
            full = [P, NT, n, n]
            mine, other = sc[:].unsqueeze(3).broadcast_to(full), sc[:].unsqueeze(2).broadcast_to(full)
            V.run(DVE.memset(earlier[:], 0.0))
            for e in range(1, n):
                V.go(DVE.memset(earlier[:, e, 0:e], 1.0))
            V.go(DVE.tensor_tensor(gt[:], other, mine, ALU.is_gt))
            V.run(DVE.tensor_tensor(eq[:], other, mine, ALU.is_equal))
            V.run(DVE.tensor_tensor(eq[:].rearrange("p t a b -> p t (a b)"), eq[:].rearrange("p t a b -> p t (a b)"),
                                    earlier[:].rearrange("p a b -> p (a b)").unsqueeze(1).broadcast_to([P, NT, n * n]), ALU.mult))
            V.run(DVE.tensor_tensor(gt[:], gt[:], eq[:], ALU.add))
            V.go(DVE.tensor_reduce(rank[:], gt[:], AX.X, ALU.add))
            V.run(DVE.tensor_reduce(m[:], sc[:], AX.X, ALU.max))
            V.go(DVE.tensor_scalar(rank[:], rank[:], 1.5, None, ALU.is_lt))
            V.run(DVE.tensor_tensor(gate[:], sc[:], m[:].unsqueeze(2).broadcast_to([P, NT, n]), ALU.subtract))
            tell("v", "a"); hear("v", "a")
            S.run(ACTE.activation(gate[:], gate[:], ACT.Exp))
            tell("a", "v"); hear("a", "v")
            V.run(DVE.tensor_tensor(gate[:], gate[:], rank[:], ALU.mult))
            V.run(DVE.tensor_reduce(m[:], gate[:], AX.X, ALU.add))
            V.run(DVE.reciprocal(m[:], m[:]))
            V.run(DVE.tensor_tensor(gate[:], gate[:], m[:].unsqueeze(2).broadcast_to([P, NT, n]), ALU.mult))

    def experts(tag, n, gate, rs, affine):
        BT = 7
        HALF = BT * P // 2
        with ExitStack() as c:
            w1 = sb(c, "w1", [P, n, 2, 512])
            w2 = sb(c, "w2", [P, n, 4, D])
            b1 = sb(c, "b1", [P, n, 4])
            b2 = sb(c, "b2", [P, n, D])
            xs = sb(c, "xs", [P, 2, D])
            xnt = sb(c, "xnt", [P, 2, BT * P])
            ht = sb(c, "ht", [P, 2, 4, BT * P])
            ps_x = ps(c, "ps_x", [P, 2, 512])
            ps_h = ps(c, "ps_h", [P, 2, 2, 512])
            ps_y = ps(c, "ps_y", [P, 2, 512])
            x_made, x_turned, xs_free, px_free, xnt_full = (sem(f"{q}_{tag}") for q in
                                                           ("x_made", "x_turned", "xs_free", "px_free", "xnt_full"))
            h_full, h_free, ht_full, ht_free, y_full, y_free = (
                sem(f"{q}_{tag}") for q in ("h_full", "h_free", "ht_full", "ht_free", "y_full", "y_free"))
            for e in range(n):
                load(w1[:, e], a["w1_" + tag][e].rearrange("(k p) d -> p k d", p=P))
                load(w2[:, e], a["w2_" + tag][e].rearrange("(k p) d -> p k d", p=P))
                broadcast_row(b2[:, e], a["b2_" + tag][e:e + 1, :], D)
            load(b1[:], a["b1_" + tag])
            loads_done(PE, ACTE, DVE)
            PE.sem_inc(h_free, 2)
            PE.sem_inc(y_free, 2)
            PE.sem_inc(px_free, 2)
            ACTE.sem_inc(ht_free, 2)
            DVE.sem_inc(xs_free, 2)
            V.reset(); S.reset()
            with nc.Fori(0, NT // BT) as blk:
                for j in range(BT):
                    t = blk * BT + j
                    take(DVE, xs_free)
                    V.run(DVE.tensor_scalar(xs[:, j % 2, :], row(x_all, t), one(mean, t), one(rs, t), ALU.subtract, ALU.mult))
                    DVE.sem_inc(x_made, 1)
                    take(PE, x_made)
                    take(PE, px_free)
                    transpose(ps_x[:, j % 2], xs[:, j % 2], 2).then_inc(x_turned, 1)
                    take(ACTE, x_turned)
                    for k in range(2):
                        src = ps_x[:, j % 2, k * P:(k + 1) * P]
                        if affine is None:
                            S.go(ACTE.activation(xnt[:, k, j * P:(j + 1) * P], src, ACT.Copy))
                        else:
                            S.go(ACTE.activation(xnt[:, k, j * P:(j + 1) * P], src, ACT.Identity,
                                                 scale=affine[:, 0, k:k + 1], bias=affine[:, 1, k:k + 1]))
                    S.sync()
                    ACTE.sem_inc(px_free, 1)
                    ACTE.sem_inc(xs_free, 1)
                ACTE.sem_inc(xnt_full, 1)
                S.reset()
                V.reset()

                def hidden(e):
                    for hb in range(4):
                        take(PE, h_free)
                        for half in range(2):
                            for k in range(2):
                                mm = PE.matmul(ps_h[:, hb % 2, half, 0:HALF], w1[:, e, k, hb * P:(hb + 1) * P],
                                               xnt[:, k, half * HALF:(half + 1) * HALF], start=(k == 0), stop=(k == 1))
                        mm.then_inc(h_full, 1)
                        if hb == 0:
                            take(ACTE, ht_free)
                        take(ACTE, h_full)
                        S.run(ACTE.activation(ht[:, e % 2, hb, :].rearrange("p (h w) -> p h w", h=2), ps_h[:, hb % 2, :, 0:HALF],
                                              ACT.Gelu, bias=b1[:, e, hb:hb + 1]))
                        ACTE.sem_inc(h_free, 1)
                    ACTE.sem_inc(ht_full, 1)
                    S.reset()

                def output(e):
                    take(PE, ht_full)
                    for j in range(BT):
                        if j % 2 == 0:
                            take(PE, y_free)
                        for hb in range(4):
                            mm = PE.matmul(ps_y[:, j // 2 % 2, (j % 2) * D:(j % 2 + 1) * D], ht[:, e % 2, hb, j * P:(j + 1) * P],
                                           w2[:, e, hb, :], start=(hb == 0), stop=(hb == 3))
                        if j % 2 == 1 or j == BT - 1:
                            mm.then_inc(y_full, 1)
                    for j in range(BT):
                        t = blk * BT + j
                        g = gate[:, bass.ds(t, 1), e:e + 1]
                        if j % 2 == 0:
                            take(DVE, y_full)
                        V.run(DVE.scalar_tensor_tensor(row(x_all, t), ps_y[:, j // 2 % 2, (j % 2) * D:(j % 2 + 1) * D], g,
                                                       row(x_all, t), ALU.mult, ALU.add))
                        if j % 2 == 1 or j == BT - 1:
                            DVE.sem_inc(y_free, 1)
                    DVE.sem_inc(ht_free, 1)
                    for j in range(BT):
                        t = blk * BT + j
                        V.run(DVE.scalar_tensor_tensor(row(x_all, t), b2[:, e, :], gate[:, bass.ds(t, 1), e:e + 1],
                                                       row(x_all, t), ALU.mult, ALU.add))
                    V.reset()

                take(PE, xnt_full)
                hidden(0)
                for e in range(n):
                    if e + 1 < n:
                        hidden(e + 1)
                    output(e)
            take(PE, h_free, 2)
            take(PE, y_free, 2)
            take(PE, px_free, 2)
            take(ACTE, ht_free, 2)
            take(DVE, xs_free, 2)
            barrier()

    HD = 64
    NH = 8

    def attention_matrix(mat):
        with ExitStack() as c:
            wkv = sb(c, "wkv", [P, 2, 2 * NH, HD])
            mu = sb(c, "mu", [P, 2, 2 * NH])
            wqn = sb(c, "wqn", [HD, NH, D])
            wo = sb(c, "wo", [HD, NH, D])
            xn = sb(c, "xn", [P, 2, D])
            xnt = sb(c, "xnt", [P, 2, D])
            kv = sb(c, "kv", [P, 2, 2 * NH, HD])
            sq = sb(c, "sq", [P, 2 * NH, HD])
            vr = sb(c, "vr", [P, 2 * NH])
            dots = sb(c, "dots", [HD, NH * HD])
            bh = sb(c, "bh", [HD, NH, D])
            ps_x = ps(c, "ps_x", [P, 2, 512])
            ps_kv = ps(c, "ps_kv", [P, 2, 2, 512])
            ps_d = ps(c, "ps_d", [P, 512])
            x_made, x_free, x_turned, px_free, xt_full, xt_free, kv_full, kv_free, sq_made, sd_asked, sd_made, out_made, out_free = (
                sem("mix1_" + q) for q in ("x_made", "x_free", "x_turned", "px_free", "xt_full", "xt_free", "kv_full", "kv_free",
                                           "sq_made", "sd_asked", "sd_made", "out_made", "out_free"))
            load(wkv[:].rearrange("p k h e -> p k (h e)"), a["mqkvt"][:, NH * HD:3 * NH * HD].rearrange("(k p) d -> p k d", p=P))
            load(wqn[:], a["mqkv"][0:NH * HD, :].rearrange("(h e) d -> e h d", e=HD))
            load(wo[:], a["woutt"].rearrange("(h e) d -> e h d", e=HD))
            loads_done(DVE, PE)
            for k in range(2):
                V.run(DVE.tensor_reduce(mu[:, k, :], wkv[:, k], AX.X, ALU.add))
                V.run(DVE.tensor_scalar(mu[:, k, :], mu[:, k, :], 1.0 / HD, None, ALU.mult))
                V.run(DVE.tensor_tensor(wkv[:, k], wkv[:, k], mu[:, k, :].unsqueeze(2).broadcast_to([P, 2 * NH, HD]), ALU.subtract))
            tell("v", "p"); hear("v", "p")
            PE.matmul(ps_d[0:HD, :], zeros[:, 0:HD], wkv[:, 0, 0:NH, :].rearrange("p h e -> p (h e)"), start=True, stop=False)
            PE.sem_inc(px_free, 2)
            PE.sem_inc(xt_free, 2)
            PE.sem_inc(kv_free, 2)
            DVE.sem_inc(x_free, 2)
            DVE.sem_inc(out_free, 2)

            def prepare(t, s):
                take(DVE, x_free)
                V.run(normalize(xn[:, s, :], t))
                DVE.sem_inc(x_made, 1)
                take(PE, x_made)
                take(PE, px_free)
                transpose(ps_x[:, s], xn[:, s], 2).then_inc(x_turned, 1)
                take(ACTE, x_turned)
                S.run(ACTE.activation(xnt[:, s, :], ps_x[:, s, 0:D], ACT.Copy))
                ACTE.sem_inc(px_free, 1)
                ACTE.sem_inc(x_free, 1)
                ACTE.sem_inc(xt_full, 1)
                take(PE, xt_full)
                take(PE, kv_free)
                for h in range(2):
                    for k in range(2):
                        mm = PE.matmul(ps_kv[:, s, h, :], xnt[:, s, k * P:(k + 1) * P],
                                       wkv[:, k, NH * h:NH * h + NH, :].rearrange("p h e -> p (h e)"), start=(k == 0), stop=(k == 1))
                mm.then_inc(kv_full, 1)

            def finish(t, s, rows):
                take(DVE, kv_full)
                take(DVE, out_free)
                V.run(DVE.tensor_copy(kv[:, s].rearrange("p (b h) e -> p b (h e)", b=2), ps_kv[:, s]))
                DVE.sem_inc(kv_free, 1)
                V.run(DVE.tensor_tensor(sq[:], kv[:, s], kv[:, s], ALU.mult))
                V.run(DVE.tensor_reduce(vr[:], sq[:], AX.X, ALU.add))
                V.run(DVE.tensor_scalar(vr[:], vr[:], 1.0 / HD, LN_EPS, ALU.mult, ALU.add))
                DVE.sem_inc(sd_asked, 1)
                take(ACTE, sd_asked)
                S.run(ACTE.activation(vr[:], vr[:], ACT.Sqrt))
                ACTE.sem_inc(sd_made, 1)
                take(DVE, sd_made)
                V.run(DVE.tensor_tensor(vr[:, 0:NH], vr[:, 0:NH], vr[:, NH:2 * NH], ALU.mult))
                V.run(DVE.reciprocal(vr[:, 0:NH], vr[:, 0:NH]))
                V.run(DVE.tensor_tensor(kv[:, s, 0:NH, :], kv[:, s, 0:NH, :], vr[:, 0:NH].unsqueeze(2).broadcast_to([P, NH, HD]), ALU.mult))
                DVE.sem_inc(out_made, 1)
                take(PE, out_made)
                for h in range(NH):
                    mm = PE.matmul(ps_d[0:HD, h * HD:(h + 1) * HD], kv[0:rows, s, NH + h, :], kv[0:rows, s, h, :],
                                   start=False, stop=False)
                mm.then_inc(out_free, 1)

            V.reset(); S.reset()
            with nc.Fori(0, NT // 2) as i:
                for s in range(2):
                    prepare(i * 2 + s, s)
                for s in range(2):
                    finish(i * 2 + s, s, P)
                V.reset(); S.reset()
            prepare(NT - 1, 0)
            finish(NT - 1, 0, LAST)
            PE.matmul(ps_d[0:HD, :], zeros[:, 0:HD], wkv[:, 0, 0:NH, :].rearrange("p h e -> p (h e)"),
                      start=False, stop=True).then_inc(links["p", "v"], 1)
            hear("p", "v")
            take(DVE, out_free, 2)
            take(DVE, x_free, 2)
            take(PE, kv_free, 2)
            take(PE, px_free, 2)
            take(PE, xt_free, 2)
            V.run(DVE.tensor_scalar(dots[:], ps_d[0:HD, :], 1.0 / N, None, ALU.mult))
            tell("v", "p"); hear("v", "p")
            for h in range(NH):
                mm = PE.matmul(ps_kv[0:HD, h // 4, h // 2 % 2, (h % 2) * D:(h % 2 + 1) * D], dots[:, h * HD:(h + 1) * HD], wo[:, h, :],
                               start=True, stop=True)
            mm.then_inc(links["p", "v"], 1)
            hear("p", "v")
            V.run(DVE.tensor_copy(bh[:].rearrange("p (b h) d -> p b (h d)", b=4), ps_kv[0:HD].rearrange("p a b w -> p (a b) w")))
            tell("v", "p"); hear("v", "p")
            for k in range(2):
                for h in range(NH):
                    mm = PE.matmul(ps_x[:, k, 0:D], wqn[:, h, k * P:(k + 1) * P], bh[:, h, :], start=(h == 0), stop=(h == NH - 1))
            mm.then_inc(links["p", "v"], 1)
            hear("p", "v")
            V.run(DVE.tensor_copy(mat[:], ps_x[:, :, 0:D]))
            barrier()

    def gcn1_project(layer, acc, res, table, mat):
        with ExitStack() as c:
            w = sb(c, "w", [P, 2, D])
            rw = sb(c, "rw", [P, 2, D])
            b = sb(c, "b", [P, 3, D])
            x = sb(c, "x", [P, D])
            xt = sb(c, "xt", [P, D])
            ps_x = ps(c, "ps_x", [P, 512])
            ps_h = ps(c, "ps_h", [P, 3, 512])
            load(w[:], a["gw"][layer].rearrange("(k p) d -> p k d", p=P))
            load(rw[:], a["resw"].rearrange("(k p) d -> p k d", p=P))
            broadcast_row(b[:, 0, :], a["gb"][layer:layer + 1, :], D)
            broadcast_row(b[:, 1, :], a["resb"], D)
            broadcast_row(b[:, 2, :], a["bout"], D)
            loads_done(PE, DVE)
            V.run(DVE.tensor_tensor(b[:, 0, :], b[:, 0, :], b[:, 1, :], ALU.add))

            def body(t, slot, last):
                if layer == 0:
                    V.run(normalize(x[:], t))
                else:
                    V.run(DVE.scalar_tensor_tensor(x[:], row(acc, t), one(deg_dst, t), row(res, t), ALU.mult, ALU.add))
                    V.run(DVE.tensor_scalar(x[:], x[:], 0.0, None, ALU.max))
                tell("v", "p"); hear("v", "p")
                transpose(ps_x, x, 2).then_inc(links["p", "a"], 1)
                hear("p", "a")
                S.run(ACTE.activation(xt[:], ps_x[:, 0:D], ACT.Copy))
                tell("a", "p"); hear("a", "p")
                for q, m in enumerate((w, rw) if layer else (w, rw, mat)):
                    for k in range(2):
                        mm = PE.matmul(ps_h[:, q, 0:D], xt[:, k * P:(k + 1) * P], m[:, k, :], start=(k == 0), stop=(k == 1))
                mm.then_inc(links["p", "v"], 1)
                hear("p", "v")
                V.go(DVE.tensor_scalar(row(acc, t), ps_h[:, 0, 0:D], one(deg_dst, t), None, ALU.mult))
                V.go(DVE.tensor_tensor(row(res, t), ps_h[:, 1, 0:D], b[:, 0, :], ALU.add))
                if layer == 0:
                    V.run(DVE.tensor_tensor(row(x_all, t), row(x_all, t), ps_h[:, 2, 0:D], ALU.add))
                    V.run(DVE.tensor_tensor(row(x_all, t), row(x_all, t), b[:, 2, :], ALU.add))
                V.sync()
            tiles(body)
            tell("v", "s"); hear("v", "s")
            load(tile_rows(table), acc[:])
            loads_done(SP)
            barrier()

    def gcn1_finish(acc, res):
        V.reset()
        with DVE.Fori(0, NT) as t:
            V.run(DVE.scalar_tensor_tensor(row(acc, t), row(acc, t), one(deg_dst, t), row(res, t), ALU.mult, ALU.add))
            V.run(DVE.scalar_tensor_tensor(row(x_all, t), row(acc, t), 0.0, row(x_all, t), ALU.max, ALU.add))
            V.reset()
        barrier()

    def route1(gate, rs, affine):
        with ExitStack() as c:
            wr = sb(c, "wr", [P, 2, 8])
            br = sb(c, "br", [P, 8])
            sc = sb(c, "sc", [P, NT, 8])
            x = sb(c, "x", [P, D])
            xt = sb(c, "xt", [P, D])
            ps_x = ps(c, "ps_x", [P, 512])
            ps_h = ps(c, "ps_h", [P, 512])
            load(wr[:], a["wr"].rearrange("(k p) d -> p k d", p=P))
            load(affine[:, 0, :], a["fg"])
            load(affine[:, 1, :], a["fb"])
            broadcast_row(br[:], a["br"], 8)
            loads_done(PE, DVE, ACTE)
            V.run(DVE.tensor_tensor(rs[:], rstd[:], rstd[:], ALU.mult))
            V.run(DVE.tensor_tensor(rs[:], rs[:], var[:], ALU.mult))
            V.run(DVE.tensor_scalar(rs[:], rs[:], LN_EPS, None, ALU.add))
            tell("v", "a"); hear("v", "a")
            S.run(ACTE.activation(rs[:], rs[:], ACT.Sqrt))
            tell("a", "v"); hear("a", "v")
            V.run(DVE.reciprocal(rs[:], rs[:]))
            V.run(DVE.tensor_tensor(rs[:], rs[:], rstd[:], ALU.mult))

            def body(t, slot, last):
                V.run(DVE.tensor_scalar(x[:], row(x_all, t), one(mean, t), one(rs, t), ALU.subtract, ALU.mult))
                tell("v", "p"); hear("v", "p")
                transpose(ps_x, x, 2).then_inc(links["p", "a"], 1)
                hear("p", "a")
                for k in range(2):
                    S.run(ACTE.activation(xt[:, k * P:(k + 1) * P], ps_x[:, k * P:(k + 1) * P], ACT.Identity,
                                          scale=affine[:, 0, k:k + 1], bias=affine[:, 1, k:k + 1]))
                tell("a", "p"); hear("a", "p")
                for k in range(2):
                    mm = PE.matmul(ps_h[:, 0:8], xt[:, k * P:(k + 1) * P], wr[:, k, :], start=(k == 0), stop=(k == 1))
                mm.then_inc(links["p", "v"], 1)
                hear("p", "v")
                V.run(DVE.tensor_tensor(row(sc, t), ps_h[:, 0:8], br[:], ALU.add))
            tiles(body)
            top2(sc, gate, 8)
            barrier()

    def edges(name, rows):
        return a[name].rearrange("(r c) -> r c", r=rows)

    def show(stage):
        if dbg.get("stage") == stage:
            load(out[0:(NT - 1) * P, :].rearrange("(t p) d -> p t d", p=P), x_all[:, 0:NT - 1, :])
            load(out[(NT - 1) * P:N, :], x_all[0:LAST, NT - 1, :])
            loads_done(SP)
            return True

    list0, _t, tile0 = bucket("l0", edges("src", GNN_ROWS), edges("dst", GNN_ROWS), GNN_ROWS, GNN_COLS, NCH_GNN, False)
    degrees(list0, tile0, NCH_GNN, deg_src)
    norm_stats()
    table0 = dram("table0", [NP, D])
    with ExitStack() as c:
        acc = sb(c, "acc", [P, NT, D])
        z_scale = sb(c, "z_scale", [P, NT])
        cov = sb(c, "cov", [P, 2, D])
        zmean = sb(c, "zmean", [P, 2, 1])
        gcn0_table(acc, table0, z_scale, cov, zmean)
        mix0(z_scale, cov, zmean)
        if show(2):
            return
        gather_sum(acc, table0, list0, _t, NCH_GNN)
        add_scaled(acc, deg_src)
        barrier()
    if show(3):
        return

    listg, _tg, tileg = bucket("gat", edges("gat_dst", GAT_ROWS), edges("gat_src", GAT_ROWS), GAT_ROWS, GAT_COLS, NCH_GAT, True)
    norm_stats()
    gate0 = sb(top, "gate0", [P, NT, GH])
    gat_scores(listg, _tg, NCH_GAT, gate0)
    if dbg.get("stage") == 4:
        load(dbg["gate"], gate0[:].rearrange("p t e -> p (t e)"))
        loads_done(SP)
        show(4)
        return
    experts("0", GH, gate0, rstd, None)
    if show(5):
        return

    list1, _t1, tile1 = bucket("l1", edges("dst", GNN_ROWS), edges("src", GNN_ROWS), GNN_ROWS, GNN_COLS, NCH_GNN, False)
    degrees(list1, tile1, NCH_GNN, deg_dst)
    norm_stats()
    with ExitStack() as c:
        mat = sb(c, "mat", [P, 2, D])
        attention_matrix(mat)
        acc = sb(c, "acc", [P, NT, D])
        res = sb(c, "res", [P, NT, D])
        for layer in range(2):
            table = dram(f"table1{layer}", [NP, D])
            gcn1_project(layer, acc, res, table, mat)
            gather_sum(acc, table, list1, _t1, NCH_GNN)
        gcn1_finish(acc, res)
    if show(6):
        return
    norm_stats()
    gate1 = sb(top, "gate1", [P, NT, 8])
    rs = sb(top, "rs", [P, NT])
    affine = sb(top, "affine", [P, 2, 2])
    route1(gate1, rs, affine)
    experts("1", 8, gate1, rs, affine)
    store_sem = sem("stores")
    SP.dma_start(out[0:(NT - 1) * P, :].rearrange("(t p) d -> p t d", p=P), x_all[:, 0:NT - 1, :]).then_inc(store_sem, 16)
    SP.dma_start(out[(NT - 1) * P:N, :], x_all[0:LAST, NT - 1, :]).then_inc(store_sem, 16)
    SP.wait_ge(store_sem, 32)


def lay_out(inputs):
    c = np.ascontiguousarray
    i = {k: np.asarray(v) for k, v in inputs.items()}
    return {
        "x": c(i["x"]), "src": c(i["src"]), "dst": c(i["dst"]),
        "gat_src": c(i["L0_ffn_edge_index"][0]), "gat_dst": c(i["L0_ffn_edge_index"][1]),
        "w0t": c(i["L0_gnn_W"].T),
        "qkvt": c(i["L0_mix_w_qkv"][:, :, 2].T),
        "gamma": c(i["L0_mix_bn_gamma"].reshape(1, -1)), "beta": c(i["L0_mix_bn_beta"].reshape(1, -1)),
        "dw": c(i["L0_mix_w_dw"][:, 0, 2].reshape(6, P).T),
        "pwt": c(i["L0_mix_w_pw"][:, :, 0].reshape(24, 32, 32).transpose(0, 2, 1)),
        "rest": c(i["L0_mix_w_res"][:, :, 0].T), "bres": c(i["L0_mix_b_res"].reshape(1, -1)),
        "wgat": c(i["L0_ffn_W_gat"]),
        "att_src": c(i["L0_ffn_att_src"].reshape(1, -1)), "att_dst": c(i["L0_ffn_att_dst"].reshape(1, -1)),
        "bgat": c(i["L0_ffn_b_gat"].reshape(1, -1)),
        "lng": c(i["L0_ffn_ln_gamma"].reshape(1, -1)), "lnb": c(i["L0_ffn_ln_beta"].reshape(1, -1)),
        "w1_0": c(i["L0_ffn_W1"]), "b1_0": c(i["L0_ffn_b1"].reshape(4, 4, P).transpose(2, 0, 1)), "w2_0": c(i["L0_ffn_W2"]), "b2_0": c(i["L0_ffn_b2"]),
        "gw": c(i["L1_gnn_W"]), "gb": c(i["L1_gnn_b"]), "resw": c(i["L1_gnn_resW"]),
        "resb": c(i["L1_gnn_resb"].reshape(1, -1)),
        "mqkv": c(i["L1_mix_w_qkv"]), "mqkvt": c(i["L1_mix_w_qkv"].T), "woutt": c(i["L1_mix_w_out"].T),
        "bout": c(i["L1_mix_b_out"].reshape(1, -1)),
        "fg": c(i["L1_ffn_gamma"].reshape(2, P).T), "fb": c(i["L1_ffn_beta"].reshape(2, P).T),
        "wr": c(i["L1_ffn_Wr"]), "br": c(i["L1_ffn_br"].reshape(1, -1)),
        "w1_1": c(i["L1_ffn_W1"]), "b1_1": c(i["L1_ffn_b1"].reshape(8, 4, P).transpose(2, 0, 1)), "w2_1": c(i["L1_ffn_W2"]), "b2_1": c(i["L1_ffn_b2"]),
    }


def kernel(**inputs):
    import concourse.bacc as _bacc
    from concourse import mybir as _mybir
    from concourse.bass_utils import run_bass_kernel_spmd as _run

    laid = lay_out(inputs)
    nc = _bacc.Bacc("TRN2", target_bir_lowering=False, num_devices=1)
    arrays, aps = {}, {}
    for name, v in laid.items():
        arrays[f"in_{name}"] = v
        aps[name] = nc.dram_tensor(f"in_{name}", v.shape, _mybir.dt.from_np(v.dtype), kind="ExternalInput").ap()
    out = nc.dram_tensor("out_x", (N, D), F32, kind="ExternalOutput").ap()
    program(nc, aps, out)
    r = _run(nc, [arrays], core_ids=[0])
    return r.results[0]["out_x"]
```

```python
from contextlib import ExitStack

import numpy as np

import concourse.bass as bass
from concourse import mybir

F32 = mybir.dt.float32
BF16 = mybir.dt.bfloat16
I32 = mybir.dt.int32
U8 = mybir.dt.uint8
ALU = mybir.AluOpType
ACT = mybir.ActivationFunctionType
AX = mybir.AxisListType

P = 128
N = 6250
D = 256
NT = (N + P - 1) // P
NP = NT * P
LAST = N - (NT - 1) * P
LN_EPS = 1e-5
MAXNORM = float(np.float32(1.0 - 1e-5))
ATANH_MAX = float(np.arctanh(np.float64(MAXNORM)))
MIN_NORM = 1e-15
U = 4


def rounded_chunks(n_edges):
    most = (n_edges + NT * (P - 1)) // P
    return -(-most // (4 * U)) * 4 * U


E_GNN = 100000
GNN_ROWS, GNN_COLS = 125, 800
E_GAT = 131072
GAT_ROWS, GAT_COLS = 128, 1024
NCH_GNN = rounded_chunks(E_GNN)
NCH_GAT = rounded_chunks(E_GAT)


class Chain:

    def __init__(self, engine, sem):
        self.engine, self.sem, self.count = engine, sem, 0

    def go(self, instruction):
        instruction.then_inc(self.sem, 1)
        self.count += 1

    def sync(self):
        if self.count:
            self.engine.wait_ge(self.sem, self.count)

    def run(self, instruction):
        self.go(instruction)
        self.sync()

    def reset(self):
        if self.count:
            self.sync()
            self.engine.sem_inc(self.sem, -self.count)
            self.count = 0


def take(engine, sem, n=1):
    engine.wait_ge(sem, n)
    engine.sem_inc(sem, -n)


def program(nc, a, out, dbg=None):
    top = ExitStack()
    with top:
        _program(nc, a, out, top, dbg or {})


def _program(nc, a, out, top, dbg):
    PE, DVE, ACTE, POOL, SP = nc.tensor, nc.vector, nc.scalar, nc.gpsimd, nc.sync

    names = {}

    def fresh(name):
        names[name] = names.get(name, 0) + 1
        return name if names[name] == 1 else f"{name}_{names[name]}"

    def sem(name):
        return top.enter_context(nc.semaphore(fresh(name)))

    links = {(p, q): sem(f"{p}_to_{q}") for p, q in ("vp", "pv", "va", "av", "gv", "ap", "pa", "as", "ag", "vg")}
    engines = {"v": DVE, "p": PE, "a": ACTE, "g": POOL, "s": SP}

    def tell(p, q):
        engines[p].sem_inc(links[p, q], 1)

    def hear(p, q):
        take(engines[q], links[p, q])

    V = Chain(DVE, sem("dve_own"))
    S = Chain(ACTE, sem("act_own"))
    G = Chain(POOL, sem("pool_own"))

    def sb(ctx, name, shape, dt=F32):
        return ctx.enter_context(nc.sbuf_tensor(fresh(name), shape, dt))

    def ps(ctx, name, shape, dt=F32):
        return ctx.enter_context(nc.psum_tensor(fresh(name), shape, dt))

    def dram(name, shape, dt=F32):
        return nc.dram_tensor(fresh(name), shape, dt).ap()

    met = {q: sem(f"met_{q}") for q in ("pe_to_dve", "act_to_dve", "dve_to_pe", "dve_to_act")}

    def barrier():
        V.reset(); S.reset()
        PE.drain().then_inc(met["pe_to_dve"], 1)
        ACTE.sem_inc(met["act_to_dve"], 1)
        take(DVE, met["pe_to_dve"]); take(DVE, met["act_to_dve"])
        DVE.sem_inc(met["dve_to_pe"], 1); DVE.sem_inc(met["dve_to_act"], 1)
        take(PE, met["dve_to_pe"]); take(ACTE, met["dve_to_act"])

    load_sem = sem("loads")
    loads = [0]

    def load(dst, src):
        ACTE.dma_start(dst, src).then_inc(load_sem, 16)
        loads[0] += 16

    def loads_done(*engines):
        for e in engines:
            e.wait_ge(load_sem, loads[0])

    def tiles(body):
        V.reset(); S.reset();
        with nc.Fori(0, NT // 2) as i:
            for slot in range(2):
                body(i * 2 + slot, slot, False)
                V.reset(); S.reset();
        body(NT - 1, 0, True)
        V.reset(); S.reset();

    ident = sb(top, "ident", [P, P])
    ones = sb(top, "ones", [P, P])
    before = sb(top, "before", [P, P])
    iota_row = sb(top, "iota_row", [P, P])
    zeros = sb(top, "zeros", [P, P])
    zwide = sb(top, "zwide", [P, D + 1])
    row_no = sb(top, "row_no", [P, 1])
    window = sb(top, "window", [P, 2 * NT])
    x_all = sb(top, "x_all", [P, NT, D])
    RING = 4
    COLS = 8
    place_slot = sb(top, "place_slot", [P, RING, COLS, 3], I32)
    index_slot = sb(top, "index_slot", [P, RING, U, 2], I32)
    row_slot = sb(top, "row_slot", [P, RING, U, D])
    deg_src = sb(top, "deg_src", [P, NT])
    deg_dst = sb(top, "deg_dst", [P, NT])
    mean = sb(top, "mean", [P, NT])
    var = sb(top, "var", [P, NT])
    rstd = sb(top, "rstd", [P, NT])

    with ExitStack() as c:
        it = sb(c, "it", [P, P], I32)
        ir = sb(c, "ir", [P, 1], I32)
        s_iota = sem("iota_made")
        POOL.iota(it[:], [[1, P]], 0, 0).then_inc(s_iota, 1)
        POOL.iota(ir[:], [[0, 1]], 0, 1).then_inc(s_iota, 1)
        DVE.wait_ge(s_iota, 2)
        V.go(DVE.memset(ones[:], 1.0))
        V.go(DVE.memset(zeros[:], 0.0))
        V.go(DVE.memset(zwide[:], 0.0))
        V.go(DVE.memset(window[:], 0.0))
        V.go(DVE.memset(x_all[:, NT - 1, :], 0.0))
        V.go(DVE.tensor_copy(iota_row[:], it[:]))
        V.run(DVE.tensor_copy(row_no[:], ir[:]))
        V.go(DVE.memset(zeros[:], 0.0))
        V.go(DVE.memset(zwide[:], 0.0))
        V.go(DVE.memset(window[:, NT - 1:NT], 1.0))
        V.go(DVE.tensor_scalar(ident[:], iota_row[:], row_no[:, 0:1], None, ALU.is_equal))
        V.run(DVE.tensor_scalar(before[:], iota_row[:], row_no[:, 0:1], None, ALU.is_gt))
        barrier()
    load(x_all[:, 0:NT - 1, :], a["x"][0:(NT - 1) * P, :].rearrange("(t p) d -> p t d", p=P))
    load(x_all[0:LAST, NT - 1, :], a["x"][(NT - 1) * P:N, :])
    loads_done(DVE)

    def bucket(tag, key, other, rows, cols, nch, clamp, stride, tile_f=None):
        places = dram(f"places_{tag}", [rows, cols, 3], I32)
        written = [sem(f"written_{tag}{s}") for s in range(RING)]
        lst = dram(f"list_{tag}", [P * nch, 2], I32)
        tile_of = dram(f"tile_of_{tag}", [1, nch], I32)
        with ExitStack() as c:
            if tile_f is None:
                tile_f = sb(c, "tile_f", [P, nch])
            k_i = sb(c, "k_i", [rows, cols], I32)
            t_i = sb(c, "t_i", [rows, cols], I32)
            t_f = sb(c, "t_f", [rows, cols])
            place = sb(c, "place", [rows, cols, 3], I32)
            o_i = sb(c, "o_i", [rows, cols], I32)
            same = sb(c, "same", [rows, cols])
            mask = sb(c, "mask", [rows, cols], U8)
            run_ = sb(c, "run", [rows, cols])
            pos = sb(c, "pos", [rows, cols])
            zero = sb(c, "zero", [rows, cols])
            total = sb(c, "total", [rows, NT])
            start = sb(c, "start", [rows, NT])
            cap_f = sb(c, "cap_f", [NT, 1])
            cap_i = sb(c, "cap_i", [NT, 1], I32)
            base = sb(c, "base", [NT, 1])
            end = sb(c, "end", [NT, 1])
            dbase = sb(c, "dbase", [NT, NT])
            chunk_i = sb(c, "chunk_i", [NT, nch], I32)
            ge = sb(c, "ge", [NT, nch])
            tl = sb(c, "tl", [1, nch], I32)
            empty = sb(c, "empty", [P, nch, 2], I32)
            ps_a = ps(c, "ps_a", [P, 512])
            ps_b = ps(c, "ps_b", [P, 512])
            ps_t = ps(c, "ps_t", [P, 3, 512])
            cleared = sem("cleared")
            staged = [sem(f"staged{s}") for s in range(RING)]
            placed = sem("placed")

            load(k_i[:], key)
            load(o_i[:], other)
            loads_done(DVE)
            V.go(DVE.memset(empty[:, :, 0], NP - 1))
            V.run(DVE.memset(empty[:, :, 1].bitcast(F32), -1.0))
            tell("v", "a")
            hear("v", "a")
            ACTE.dma_start(lst.rearrange("(p c) w -> p c w", p=P), empty[:]).then_inc(cleared, 16)
            if clamp:
                V.go(DVE.tensor_scalar(k_i[:], k_i[:], NP - 1, None, ALU.min))
                V.run(DVE.tensor_scalar(o_i[:], o_i[:], N - 1, None, ALU.min))
            V.go(DVE.tensor_scalar(t_i[:], k_i[:], 7, None, ALU.arith_shift_right))
            V.go(DVE.tensor_copy(place[:, :, 1], o_i[:]))
            V.go(DVE.memset(zero[:], 0.0))
            V.run(DVE.tensor_scalar(k_i[:], k_i[:], 127, None, ALU.bitwise_and))
            V.go(DVE.tensor_copy(place[:, :, 2].bitcast(F32), k_i[:]))
            V.run(DVE.tensor_copy(t_f[:], t_i[:]))
            for b in range(NT):
                V.run(DVE.tensor_scalar(same[:], t_f[:], float(b), 0.0, ALU.is_equal, ALU.add,
                                        accum_out=total[:, b:b + 1]))
            tell("v", "p")
            hear("v", "p")
            PE.matmul(ps_b[0:NT, 0:1], total[:], ones[0:rows, 0:1], start=True, stop=True).then_inc(links["p", "v"], 1)
            hear("p", "v")
            V.run(DVE.tensor_scalar(cap_i[:], ps_b[0:NT, 0:1], 127.0, None, ALU.add))
            V.run(DVE.tensor_scalar(cap_i[:], cap_i[:], 7, 7, ALU.arith_shift_right, ALU.arith_shift_left))
            V.run(DVE.tensor_copy(cap_f[:], cap_i[:]))
            tell("v", "p")
            hear("v", "p")
            PE.matmul(ps_b[0:NT, 1:2], before[0:NT, 0:NT], cap_f[:], start=True, stop=True).then_inc(links["p", "v"], 1)
            hear("p", "v")
            V.run(DVE.tensor_copy(base[:], ps_b[0:NT, 1:2]))
            V.go(DVE.tensor_tensor(end[:], base[:], cap_f[:], ALU.add))
            V.run(DVE.tensor_scalar(dbase[:], ident[0:NT, 0:NT], base[:, 0:1], None, ALU.mult))
            tell("v", "p")
            hear("v", "p")
            PE.matmul(ps_a[0:rows, 0:NT], before[0:rows, 0:rows], total[:], start=True, stop=False)
            PE.matmul(ps_a[0:rows, 0:NT], ones[0:NT, 0:rows], dbase[:], start=False, stop=True).then_inc(links["p", "v"], 1)
            hear("p", "v")
            V.run(DVE.tensor_scalar(start[:], ps_a[0:rows, 0:NT], -1.0, None, ALU.add))
            tell("v", "g"); hear("v", "g")
            G.run(POOL.iota(chunk_i[:], [[P, nch]], 0, 0))
            tell("g", "v")
            hear("g", "v")
            V.run(DVE.tensor_scalar(ge[:], chunk_i[:], end[:, 0:1], None, ALU.is_ge))
            tell("v", "p")
            hear("v", "p")
            for q in range(0, nch, 512):
                w = min(512, nch - q)
                mm = PE.matmul(ps_t[:, q // 512, 0:w], ones[0:NT, :], ge[:, q:q + w], start=True, stop=True)
            mm.then_inc(links["p", "v"], 1)
            hear("p", "v")
            for q in range(0, nch, 512):
                w = min(512, nch - q)
                V.go(DVE.tensor_scalar(tile_f[:, q:q + w], ps_t[:, q // 512, 0:w], float(NT - 1), None, ALU.min))
            V.sync()
            V.run(DVE.tensor_scalar(tl[:], tile_f[0:1, :], float(stride), None, ALU.mult))
            tell("v", "a")
            hear("v", "a")
            ACTE.dma_start(tile_of, tl[:]).then_inc(load_sem, 16)
            loads[0] += 16
            for b in range(NT):
                V.go(DVE.tensor_scalar(mask[:], t_f[:], float(b), None, ALU.is_equal))
                V.run(DVE.tensor_scalar(same[:], t_f[:], float(b), None, ALU.is_equal))
                V.run(DVE.tensor_tensor_scan(run_[:], same[:], zero[:], start[:, b:b + 1], ALU.add, ALU.add))
                V.run(DVE.copy_predicated(pos[:], mask[:], run_[:]) if b else DVE.tensor_copy(pos[:], run_[:]))
            V.run(DVE.tensor_copy(k_i[:], pos[:]))
            V.go(DVE.tensor_scalar(t_i[:], k_i[:], 7, None, ALU.arith_shift_right))
            V.run(DVE.tensor_scalar(k_i[:], k_i[:], 127, None, ALU.bitwise_and))
            V.run(DVE.scalar_tensor_tensor(place[:, :, 0], k_i[:], float(nch), t_i[:], ALU.mult, ALU.add))
            tell("v", "a")
            hear("v", "a")
            ACTE.dma_start(places, place[:]).then_inc(placed, 16)
            SP.wait_ge(placed, 16)
            ACTE.wait_ge(placed, 16)
            POOL.wait_ge(cleared, 16)
            loads_done(ACTE)
            barrier()

        def bring(first, s):
            SP.dma_start(place_slot[0:rows, s], places[:, bass.ds(first, COLS), :]).then_inc(staged[s], 16)

        def put(s):
            take(POOL, staged[s], 16)
            for j in range(COLS):
                POOL.indirect_dma_start(lst, bass.IndirectOffsetOnAxis(ap=place_slot[0:rows, s, j, 0:1], axis=0),
                                        place_slot[0:rows, s, j, 1:3], None).then_inc(written[s], 16)

        turns = cols // (COLS * RING)
        for s in range(RING):
            bring(COLS * s, s)
        with SP.Fori(1, turns) as i:
            for s in range(RING):
                SP.wait_ge(written[s], i * (16 * COLS))
                bring(i * (COLS * RING) + COLS * s, s)
        with POOL.Fori(0, turns) as i:
            for s in range(RING):
                put(s)

        def list_done(engine):
            for s in range(RING):
                engine.wait_ge(written[s], turns * 16 * COLS)
        list_done(SP)
        return lst, tile_of, list_done

    def onehots(dst, low):
        n = dst.shape[1]
        return DVE.tensor_tensor(dst, iota_row[:].unsqueeze(1).broadcast_to([P, n, P]),
                                 low.broadcast_to([P, n, P]), ALU.is_equal)

    def tile_offsets(tl, first, n, most):
        _, values = nc.values_load_multi_w_load_instructions(
            tl[0:1, bass.ds(first, n)], engines=[mybir.EngineType.DVE], min_val=0, max_val=most,
            skip_runtime_bounds_check_because="bucket() takes the minimum with the last tile")
        return values

    def degrees(lst, list_done, tile_f, nch, deg):
        W = 2 * U
        with ExitStack() as c:
            l_sb = sb(c, "l_sb", [P, nch, 2], I32)
            oh = sb(c, "oh_deg", [P, 2, W, P], BF16)
            at = sb(c, "at_deg", [P, 2, W, NT], BF16)
            cnt = ps(c, "cnt", [P, 512])
            made = sem("oh_made")
            free = sem("oh_free")
            list_done(ACTE)
            load(l_sb[:], lst.rearrange("(p c) w -> p c w", p=P))
            loads_done(DVE)
            PE.matmul(cnt[:, 0:NT], zeros[:], zeros[:, 0:NT], start=True, stop=False)
            V.reset()
            DVE.sem_inc(free, 2)
            with nc.Fori(0, nch // (2 * W)) as i:
                for slot in range(2):
                    first = (i * 2 + slot) * W
                    take(DVE, free)
                    V.go(onehots(oh[:, slot], l_sb[:, bass.ds(first, W), 1:2].bitcast(F32)))
                    V.go(DVE.tensor_tensor(at[:, slot], iota_row[:, 0:NT].unsqueeze(1).broadcast_to([P, W, NT]),
                                           tile_f[:, bass.ds(first, W)].unsqueeze(2).broadcast_to([P, W, NT]), ALU.is_equal))
                    V.sync()
                    DVE.sem_inc(made, 1)
                    V.reset()
                    take(PE, made)
                    for w in range(W):
                        mm = PE.matmul(cnt[:, 0:NT], oh[:, slot, w, :], at[:, slot, w, :], start=False, stop=False)
                    mm.then_inc(free, 1)
            PE.matmul(cnt[:, 0:NT], zeros[:], zeros[:, 0:NT], start=False, stop=True).then_inc(links["p", "v"], 1)
            hear("p", "v")
            take(DVE, free, 2)
            V.run(DVE.tensor_scalar(deg[:], cnt[:, 0:NT], 1.0, None, ALU.add))
            V.run(DVE.reciprocal(deg[:], deg[:]))
            tell("v", "a")
            hear("v", "a")
            S.run(ACTE.activation(deg[:], deg[:], ACT.Sqrt))
            barrier()

    def gathers(tag, table, lst, nch, width):
        staged = [sem(f"index_staged_{tag}{s}") for s in range(RING)]
        got = [sem(f"got_{tag}{s}") for s in range(RING)]
        slot_free = [sem(f"slot_free_{tag}{s}") for s in range(RING)]
        tell("a", "s"); hear("a", "s")
        tell("a", "g"); hear("a", "g")
        indices = lst.rearrange("(p c) w -> p c w", p=P)
        for s in range(RING):
            SP.sem_inc(slot_free[s], 1)
        with SP.Fori(0, nch // (RING * U)) as i:
            for s in range(RING):
                take(SP, slot_free[s])
                SP.dma_start(index_slot[:, s], indices[:, bass.ds((i * RING + s) * U, U), :]).then_inc(staged[s], 16)
        for s in range(RING):
            take(SP, slot_free[s])
        with POOL.Fori(0, nch // (RING * U)) as i:
            for s in range(RING):
                take(POOL, staged[s], 16)
                for u in range(U):
                    POOL.indirect_dma_start(row_slot[:, s, u, 0:width], None, table,
                                            bass.IndirectOffsetOnAxis(ap=index_slot[:, s, u, 0:1], axis=0)
                                            ).then_inc(got[s], 16)
        return got, slot_free

    def ring_loop(nch, begin, end):
        turns = nch // (RING * U)

        def turn(i, first):
            for s in range(RING):
                begin(i, s)
                if s:
                    end(i, s - 1)
                elif not first:
                    end(i - 1, RING - 1)
        V.reset(); S.reset()
        turn(0, True)
        V.reset(); S.reset()
        with nc.Fori(1, turns) as i:
            turn(i, False)
            V.reset(); S.reset()
        end(turns - 1, RING - 1)
        V.reset(); S.reset()

    def gather_sum(tag, acc, table, lst, tile_of, nch):
        with ExitStack() as c:
            l_sb = sb(c, "l_sb", [P, nch, 2], I32)
            tl = sb(c, "tl", [1, nch], I32)
            oh = sb(c, "oh", [P, 2, U, P])
            pp = ps(c, "pp", [P, 2, U, D])
            oh_made = sem("oh_made")
            summed = sem("summed")
            load(l_sb[:], lst.rearrange("(p c) w -> p c w", p=P))
            load(tl[:], tile_of)
            loads_done(DVE)
            got, slot_free = gathers(tag, table, lst, nch, D)
            flat = acc[:].rearrange("p t d -> p (t d)")

            def begin(i, s):
                V.run(onehots(oh[:, s % 2], l_sb[:, bass.ds((i * RING + s) * U, U), 1:2].bitcast(F32)))
                DVE.sem_inc(oh_made, 1)
                take(PE, oh_made)
                PE.wait_ge(got[s], i * (16 * U) + 16 * U)
                for u in range(U):
                    mm = PE.matmul(pp[:, s % 2, u, :], oh[:, s % 2, u, :], row_slot[:, s, u, :], start=True, stop=True)
                mm.then_inc(summed, 1)

            def end(i, s):
                offsets = tile_offsets(tl, (i * RING + s) * U, U, (NT - 1) * D)
                take(DVE, summed)
                DVE.sem_inc(slot_free[s], 1)
                for u in range(U):
                    at = flat[:, bass.ds(offsets[u], D)]
                    V.run(DVE.tensor_tensor(at, at, pp[:, s % 2, u, :], ALU.add))
            ring_loop(nch, begin, end)
            barrier()

    def norm_stats():
        with ExitStack() as c:
            st = sb(c, "st", [P, NT, 6])
            tmp = sb(c, "tmp", [P, NT])
            V.reset()
            with DVE.Fori(0, NT) as t:
                V.run(DVE.bn_stats(st[:, bass.ds(t, 1), :], x_all[:, bass.ds(t, 1), :]))
                V.reset()
            V.go(DVE.tensor_tensor(mean[:], st[:, :, 1], st[:, :, 4], ALU.add))
            V.go(DVE.tensor_tensor(tmp[:], st[:, :, 1], st[:, :, 4], ALU.subtract))
            V.go(DVE.tensor_tensor(var[:], st[:, :, 2], st[:, :, 5], ALU.add))
            V.sync()
            V.go(DVE.tensor_scalar(mean[:], mean[:], 0.5, None, ALU.mult))
            V.run(DVE.tensor_tensor(tmp[:], tmp[:], tmp[:], ALU.mult))
            V.go(DVE.tensor_scalar(tmp[:], tmp[:], 0.25, None, ALU.mult))
            V.run(DVE.tensor_scalar(var[:], var[:], 1.0 / D, None, ALU.mult))
            V.run(DVE.tensor_tensor(var[:], var[:], tmp[:], ALU.add))
            V.run(DVE.tensor_scalar(rstd[:], var[:], LN_EPS, None, ALU.add))
            tell("v", "a")
            hear("v", "a")
            S.run(ACTE.activation(rstd[:], rstd[:], ACT.Sqrt))
            tell("a", "v")
            hear("a", "v")
            V.run(DVE.reciprocal(rstd[:], rstd[:]))
            barrier()

    def one(x, t):
        return x[:, t:t + 1] if isinstance(t, int) else x[:, bass.ds(t, 1)]

    def row(x, t):
        return x[:, t, :] if isinstance(t, int) else x[:, bass.ds(t, 1), :]

    def normalize(dst, t, scale=None):
        return DVE.tensor_scalar(dst, row(x_all, t), one(mean, t), one(rstd, t), ALU.subtract, ALU.mult)

    def transpose(dst_ps, src, blocks):
        for k in range(blocks):
            last = PE.transpose(dst_ps[:, k * P:(k + 1) * P], src[:, k * P:(k + 1) * P], ident[:])
        return last

    def broadcast_row(dst, src, width):
        load(dst, src.broadcast_to([P, width]))

    def tile_rows(x):
        return x.rearrange("(t p) d -> p t d", p=P)

    P2V, P2A = ("p", "v"), ("p", "a")

    def gcn0_table(acc, table, z_scale, cov, zmean):
        with ExitStack() as c:
            w0t = sb(c, "w0t", [P, 2, D])
            xn = sb(c, "xn", [P, D])
            z = sb(c, "z", [P, D + 1])
            xnt = sb(c, "xnt", [P, D])
            ps_x = ps(c, "ps_x", [P, 512])
            ps_h = ps(c, "ps_h", [P, 512])
            gram = ps(c, "gram", [P, 2, 512])
            tmp = sb(c, "tmp", [P, NT])
            tm2 = sb(c, "tm2", [P, NT])
            nrm = sb(c, "nrm", [P, NT])
            msk = sb(c, "msk", [P, NT])
            load(w0t[:], a["w0t"].rearrange("(k p) d -> p k d", p=P))
            loads_done(PE)
            tell("v", "a"); hear("v", "a")
            S.run(ACTE.activation(nrm[:], var[:], ACT.Sqrt, scale=float(D)))
            tell("a", "v"); hear("a", "v")
            V.run(DVE.tensor_tensor(nrm[:], nrm[:], rstd[:], ALU.mult))
            V.go(DVE.tensor_scalar(msk[:], nrm[:], MAXNORM, None, ALU.is_gt))
            V.go(DVE.tensor_scalar(tmp[:], nrm[:], MAXNORM, None, ALU.min))
            V.run(DVE.tensor_scalar(nrm[:], nrm[:], MIN_NORM, None, ALU.max))
            V.go(DVE.tensor_scalar(tm2[:], tmp[:], -1.0, 1.0, ALU.mult, ALU.add))
            V.run(DVE.tensor_scalar(tmp[:], tmp[:], 1.0, None, ALU.add))
            V.run(DVE.reciprocal(tm2[:], tm2[:]))
            V.run(DVE.tensor_tensor(tmp[:], tmp[:], tm2[:], ALU.mult))
            tell("v", "a"); hear("v", "a")
            S.run(ACTE.activation(tmp[:], tmp[:], ACT.Ln))
            tell("a", "v"); hear("a", "v")
            V.run(DVE.tensor_scalar(tmp[:], tmp[:], 0.5, None, ALU.mult))
            V.go(DVE.tensor_scalar(tm2[:], msk[:], ATANH_MAX, None, ALU.mult))
            V.run(DVE.tensor_scalar(msk[:], msk[:], -1.0, 1.0, ALU.mult, ALU.add))
            V.run(DVE.tensor_tensor(tmp[:], tmp[:], msk[:], ALU.mult))
            V.run(DVE.tensor_tensor(tmp[:], tmp[:], tm2[:], ALU.add))
            V.run(DVE.reciprocal(nrm[:], nrm[:]))
            V.run(DVE.tensor_tensor(z_scale[:], tmp[:], nrm[:], ALU.mult))
            V.run(DVE.memset(z[:, D:D + 1], 1.0))
            for k in range(2):
                PE.matmul(gram[:, k, 0:D + 1], zeros[:], zwide[:, 0:D + 1], start=True, stop=False)

            def body(t, slot, last):
                V.run(normalize(xn[:], t))
                V.run(DVE.tensor_scalar(z[:, 0:D], xn[:], one(z_scale, t), None, ALU.mult))
                tell("v", "p"); hear("v", "p")
                transpose(ps_x, xn, 2).then_inc(links["p", "a"], 1)
                for k in range(2):
                    mm = PE.matmul(gram[:, k, 0:D + 1], z[:, k * P:(k + 1) * P], z[:], start=False, stop=False)
                hear("p", "a")
                S.run(ACTE.activation(xnt[:], ps_x[:, 0:D], ACT.Copy))
                tell("a", "p"); hear("a", "p")
                for k in range(2):
                    mm = PE.matmul(ps_h[:, 0:D], xnt[:, k * P:(k + 1) * P], w0t[:, k, :], start=(k == 0), stop=(k == 1))
                mm.then_inc(links["p", "v"], 1)
                hear("p", "v")
                V.run(DVE.tensor_scalar(row(acc, t), ps_h[:, 0:D], one(deg_src, t), None, ALU.mult))
            tiles(body)
            for k in range(2):
                mm = PE.matmul(gram[:, k, 0:D + 1], zeros[:], z[:], start=False, stop=True)
            mm.then_inc(links["p", "v"], 1)
            hear("p", "v")
            mr = sb(c, "mr", [P, 2, D])
            dm = sb(c, "dm", [P, 2, P])
            for k in range(2):
                V.run(DVE.tensor_scalar(zmean[:, k, :], gram[:, k, D:D + 1], 1.0 / N, None, ALU.mult))
                V.run(DVE.tensor_scalar(dm[:, k, :], ident[:], zmean[:, k, 0:1], None, ALU.mult))
                V.run(DVE.tensor_scalar(cov[:, k, :], gram[:, k, 0:D], 1.0 / N, None, ALU.mult))
            tell("v", "p"); hear("v", "p")
            for k in range(2):
                mm = PE.matmul(ps_h[:, k * P:(k + 1) * P], ones[:], dm[:, k, :], start=True, stop=True)
            mm.then_inc(links["p", "v"], 1)
            hear("p", "v")
            for k in range(2):
                V.run(DVE.tensor_scalar(mr[:, k, :], ps_h[:, 0:D], zmean[:, k, 0:1], None, ALU.mult))
                V.run(DVE.tensor_tensor(cov[:, k, :], cov[:, k, :], mr[:, k, :], ALU.subtract))
            tell("v", "a"); hear("v", "a")
            load(tile_rows(table), acc[:])
            loads_done(ACTE)
            barrier()

    C3 = 768

    def mix0(z_scale, cov, zmean):
        with ExitStack() as c:
            wq = sb(c, "wq", [P, 2, C3])
            vec = sb(c, "vec", [P, C3])
            bias = sb(c, "bias", [P, C3])
            prod = sb(c, "prod", [P, 2, C3])
            mb = sb(c, "mb", [P, 2, P])
            pw = sb(c, "pw", [P, 6, P])
            dw = sb(c, "dw", [P, 6])
            rest = sb(c, "rest", [P, 4, D])
            bres = sb(c, "bres", [P, D])
            xn = sb(c, "xn", [P, D])
            zt = sb(c, "zt", [P, D])
            y = sb(c, "y", [P, 2 * C3])
            rt = sb(c, "rt", [P, C3])
            sq = sb(c, "sq", [P, C3])
            kk = sb(c, "kk", [P, 16, 32])
            dots = sb(c, "dots", [P, 16])
            den = sb(c, "den", [P, 16, 32])
            vv = sb(c, "vv", [P, 16, 32])
            o = sb(c, "o", [P, 512])
            ot = sb(c, "ot", [P, 512])
            ft = sb(c, "ft", [P, D])
            nn = sb(c, "nn", [P, 12])
            ps_a = ps(c, "ps_a", [P, 2, 512])
            ps_b = ps(c, "ps_b", [P, 2, 512])
            ps_c = ps(c, "ps_c", [P, 2, 512])
            ps_d = ps(c, "ps_d", [P, 512])
            V.run(DVE.memset(pw[:], 0.0))
            tell("v", "a"); hear("v", "a")
            load(wq[:], a["qkvt"].rearrange("(k p) d -> p k d", p=P))
            load(dw[:], a["dw"])
            for g in range(4):
                load(pw[32 * g:32 * g + 32, :, 32 * g:32 * g + 32],
                     a["pwt"].rearrange("(b g) i o -> g i b o", g=4)[g])
            load(rest[:], a["rest"].rearrange("(k p) d -> p k d", p=P))
            broadcast_row(bres[:], a["bres"], D)
            broadcast_row(vec[:], a["gamma"], C3)
            broadcast_row(bias[:], a["beta"], C3)
            loads_done(DVE, PE)
            for b in range(6):
                V.go(DVE.tensor_scalar(pw[:, b, :], pw[:, b, :], dw[:, b:b + 1], None, ALU.mult))
            for k in range(2):
                V.go(DVE.tensor_scalar(mb[:, k, :], ones[:], zmean[:, k, 0:1], None, ALU.mult))
            V.sync()
            tell("v", "p"); hear("v", "p")
            H = C3 // 2
            for m in range(2):
                for h in range(2):
                    for k in range(2):
                        mm = PE.matmul((ps_a if m == 0 else ps_b)[:, h, 0:H], cov[:, k, m * P:(m + 1) * P],
                                       wq[:, k, h * H:(h + 1) * H], start=(k == 0), stop=(k == 1))
            for h in range(2):
                for k in range(2):
                    mm = PE.matmul(ps_c[:, h, 0:H], mb[:, k, :], wq[:, k, h * H:(h + 1) * H],
                                   start=(k == 0), stop=(k == 1))
            mm.then_inc(links["p", "v"], 1)
            hear("p", "v")
            for m in range(2):
                V.go(DVE.tensor_tensor(prod[:, m, :].rearrange("p (h w) -> p h w", h=2), (ps_a if m == 0 else ps_b)[:, :, 0:H],
                                       wq[:, m, :].rearrange("p (h w) -> p h w", h=2), ALU.mult))
            V.sync()
            tell("v", "p"); hear("v", "p")
            for h in range(2):
                for m in range(2):
                    mm = PE.matmul(ps_a[:, h, 0:H], ones[:], prod[:, m, h * H:(h + 1) * H], start=(m == 0), stop=(m == 1))
            mm.then_inc(links["p", "v"], 1)
            hear("p", "v")
            var_row = prod[:, 0, :].rearrange("p (h w) -> p h w", h=2)
            V.run(DVE.tensor_scalar(var_row, ps_a[:, :, 0:H], 0.0, LN_EPS, ALU.max, ALU.add))
            tell("v", "a"); hear("v", "a")
            S.run(ACTE.activation(prod[:, 0, :], prod[:, 0, :], ACT.Sqrt))
            tell("a", "v"); hear("a", "v")
            V.run(DVE.reciprocal(prod[:, 0, :], prod[:, 0, :]))
            V.run(DVE.tensor_tensor(vec[:], vec[:], prod[:, 0, :], ALU.mult))
            V.run(DVE.tensor_tensor(prod[:, 1, :].rearrange("p (h w) -> p h w", h=2), ps_c[:, :, 0:H],
                                    vec[:].rearrange("p (h w) -> p h w", h=2), ALU.mult))
            V.go(DVE.tensor_tensor(bias[:], bias[:], prod[:, 1, :], ALU.subtract))
            for k in range(2):
                V.go(DVE.tensor_tensor(wq[:, k, :], wq[:, k, :], vec[:], ALU.mult))
            V.sync()
            qkv = y[:].rearrange("p (g s j) -> p g s j", g=16, s=3)

            def body(t, slot, last):
                V.run(normalize(xn[:], t))
                V.run(DVE.tensor_scalar(xn[:], xn[:], one(z_scale, t), None, ALU.mult))
                tell("v", "p"); hear("v", "p")
                transpose(ps_d, xn, 2).then_inc(links["p", "a"], 1)
                hear("p", "a")
                S.run(ACTE.activation(zt[:], ps_d[:, 0:D], ACT.Copy))
                tell("a", "p"); hear("a", "p")
                for h in range(2):
                    for k in range(2):
                        mm = PE.matmul(ps_a[:, h, 0:H], zt[:, k * P:(k + 1) * P], wq[:, k, h * H:(h + 1) * H],
                                       start=(k == 0), stop=(k == 1))
                mm.then_inc(links["p", "v"], 1)
                hear("p", "v")
                r = y[:, 0:C3]
                V.run(DVE.tensor_tensor(r.rearrange("p (h w) -> p h w", h=2), ps_a[:, :, 0:H],
                                        bias[:].rearrange("p (h w) -> p h w", h=2), ALU.add))
                V.run(DVE.tensor_scalar(r, r, 0.0, None, ALU.max))
                tell("v", "p"); hear("v", "p")
                tell("v", "a")
                for b in range(6):
                    tr = PE.transpose(ps_b[:, b // 4, (b % 4) * P:(b % 4 + 1) * P], y[:, b * P:(b + 1) * P], ident[:])
                tr.then_inc(links["p", "a"], 1)
                hear("v", "a")
                S.run(ACTE.activation(sq[:], r, ACT.Square, accum_out=nn[:, 0:1]))
                hear("p", "a")
                S.go(ACTE.activation(rt[:, 0:512], ps_b[:, 0, :], ACT.Copy))
                S.run(ACTE.activation(rt[:, 512:C3], ps_b[:, 1, 0:256], ACT.Copy))
                tell("a", "p"); hear("a", "p")
                for b in range(6):
                    mm = PE.matmul(ps_c[:, b // 4, (b % 4) * P:(b % 4 + 1) * P], rt[:, b * P:(b + 1) * P], pw[:, b, :],
                                   start=True, stop=True)
                mm.then_inc(links["p", "a"], 1)
                hear("p", "a")
                S.go(ACTE.activation(y[:, C3:C3 + 512], ps_c[:, 0, :], ACT.Copy))
                S.run(ACTE.activation(y[:, C3 + 512:2 * C3], ps_c[:, 1, 0:256], ACT.Copy))
                S.run(ACTE.activation(sq[:], y[:, C3:2 * C3], ACT.Square, accum_out=nn[:, 1:2]))
                tell("a", "v"); hear("a", "v")
                V.run(DVE.tensor_tensor(nn[:, 2:3], nn[:, 0:1], nn[:, 1:2], ALU.add))
                tell("v", "a"); hear("v", "a")
                S.run(ACTE.activation(nn[:, 3:4], nn[:, 2:3], ACT.Sqrt))
                tell("a", "v")
                V.go(DVE.tensor_scalar(kk[:], qkv[:, :, 1, :], 0.0, None, ALU.max))
                V.sync()
                V.run(DVE.tensor_reduce(dots[:], kk[:], AX.X, ALU.add))
                hear("a", "v")
                V.run(DVE.tensor_scalar(nn[:, 3:4], nn[:, 3:4], MIN_NORM, None, ALU.max))
                V.run(DVE.reciprocal(nn[:, 3:4], nn[:, 3:4]))
                V.run(DVE.tensor_scalar(nn[:, 3:4], nn[:, 3:4], ATANH_MAX, 1.0, ALU.mult, ALU.min))
                V.go(DVE.tensor_scalar(dots[:], dots[:], nn[:, 3:4], nn[:, 3:4], ALU.mult, ALU.mult))
                V.go(DVE.tensor_scalar(vv[:], qkv[:, :, 2, :], nn[:, 3:4], None, ALU.mult))
                V.run(DVE.tensor_scalar(den[:], qkv[:, :, 2, :], nn[:, 3:4], 1e-15, ALU.mult, ALU.add))
                V.go(DVE.reciprocal(den[:], den[:]))
                V.run(DVE.scalar_tensor_tensor(vv[:], qkv[:, :, 0, :], 0.0, vv[:], ALU.max, ALU.mult))
                V.run(DVE.tensor_tensor(vv[:], vv[:], dots[:].unsqueeze(2).broadcast_to([P, 16, 32]), ALU.mult))
                V.run(DVE.tensor_tensor(o[:].rearrange("p (g j) -> p g j", g=16), vv[:], den[:], ALU.mult))
                tell("v", "p"); hear("v", "p")
                transpose(ps_d, o, 4).then_inc(links["p", "a"], 1)
                tell("v", "a"); hear("v", "a")
                S.run(ACTE.activation(sq[:, 0:512], o[:], ACT.Square, accum_out=nn[:, 4:5]))
                S.run(ACTE.activation(nn[:, 5:6], nn[:, 4:5], ACT.Sqrt))
                hear("p", "a")
                S.run(ACTE.activation(ot[:], ps_d[:], ACT.Copy))
                tell("a", "p"); hear("a", "p")
                tell("a", "v"); hear("a", "v")
                for k in range(4):
                    mm = PE.matmul(ps_a[:, 0, 0:D], ot[:, k * P:(k + 1) * P], rest[:, k, :], start=(k == 0), stop=(k == 3))
                mm.then_inc(links["p", "v"], 1)
                V.run(DVE.tensor_scalar(nn[:, 5:6], nn[:, 5:6], MIN_NORM, None, ALU.max))
                V.run(DVE.reciprocal(nn[:, 5:6], nn[:, 5:6]))
                V.run(DVE.tensor_scalar(nn[:, 5:6], nn[:, 5:6], ATANH_MAX, 1.0, ALU.mult, ALU.min))
                hear("p", "v")
                V.run(DVE.scalar_tensor_tensor(ft[:], ps_a[:, 0, 0:D], nn[:, 5:6], bres[:], ALU.mult, ALU.add))
                tell("v", "a"); hear("v", "a")
                S.run(ACTE.activation(sq[:, 0:D], ft[:], ACT.Square, accum_out=nn[:, 6:7]))
                S.run(ACTE.activation(nn[:, 7:8], nn[:, 6:7], ACT.Sqrt))
                S.run(ACTE.activation(nn[:, 8:9], nn[:, 7:8], ACT.Tanh))
                tell("a", "v"); hear("a", "v")
                V.go(DVE.tensor_scalar(nn[:, 8:9], nn[:, 8:9], MAXNORM, None, ALU.min))
                V.run(DVE.tensor_scalar(nn[:, 7:8], nn[:, 7:8], MIN_NORM, None, ALU.max))
                V.run(DVE.reciprocal(nn[:, 7:8], nn[:, 7:8]))
                V.run(DVE.tensor_tensor(nn[:, 9:10], nn[:, 7:8], nn[:, 8:9], ALU.mult))
                V.run(DVE.scalar_tensor_tensor(row(x_all, t), ft[:], nn[:, 9:10], row(x_all, t), ALU.mult, ALU.add))
            tiles(body)
            barrier()

    def add_scaled(acc, deg):
        with DVE.Fori(0, NT) as t:
            V.run(DVE.scalar_tensor_tensor(row(x_all, t), row(acc, t), one(deg, t), row(x_all, t), ALU.mult, ALU.add))
            V.reset()

    GH = 4
    TW = 20

    def leaky(dst, src):
        return DVE.scalar_tensor_tensor(dst, src, 0.2, src, ALU.mult, ALU.max)

    def gat_scores(lst, list_done, tile_of, nch, gate):
        with ExitStack() as c:
            wg = sb(c, "wg", [P, 2, 16])
            att = sb(c, "att", [P, 2, 16])
            bg = sb(c, "bg", [P, 3, 16])
            node = sb(c, "node", [P, NT, TW])
            pr = sb(c, "pr", [P, NT, 16])
            dm = sb(c, "dm", [P, 2, NT * GH])
            top = sb(c, "topv", [P, NT, GH])
            least = sb(c, "least", [P, 1])
            shift = sb(c, "shift", [P, 1])
            sums = sb(c, "sums", [P, 5, NT * GH])
            rows_all = sb(c, "rows_all", [P, nch, TW])
            l_sb = sb(c, "l_sb", [P, nch, 2], I32)
            tl = sb(c, "tl", [1, nch], I32)
            load(wg[:], a["wgat"].rearrange("(k p) d -> p k d", p=P))
            broadcast_row(att[:, 0, :], a["att_src"], 16)
            broadcast_row(att[:, 1, :], a["att_dst"], 16)
            for q, n in enumerate(("bgat", "lng", "lnb")):
                broadcast_row(bg[:, q, :], a[n], 16)
            list_done(ACTE)
            load(l_sb[:], lst.rearrange("(p c) w -> p c w", p=P))
            load(tl[:], tile_of)
            loads_done(DVE, PE, ACTE)
            table = dram("gat_table", [NP, TW])
            with ExitStack() as d:
                xn = sb(d, "xn", [P, D])
                xnt = sb(d, "xnt", [P, D])
                ps_x = ps(d, "ps_x", [P, 512])
                ps_h = ps(d, "ps_h", [P, 512])

                def body(t, slot, last):
                    V.run(normalize(xn[:], t))
                    tell("v", "p"); hear("v", "p")
                    transpose(ps_x, xn, 2).then_inc(links["p", "a"], 1)
                    hear("p", "a")
                    S.run(ACTE.activation(xnt[:], ps_x[:, 0:D], ACT.Copy))
                    tell("a", "p"); hear("a", "p")
                    for k in range(2):
                        mm = PE.matmul(ps_h[:, 0:16], xnt[:, k * P:(k + 1) * P], wg[:, k, :], start=(k == 0), stop=(k == 1))
                    mm.then_inc(links["p", "v"], 1)
                    hear("p", "v")
                    at = node[:, t, 0:16] if isinstance(t, int) else node[:, bass.ds(t, 1), 0:16]
                    V.run(DVE.tensor_copy(at, ps_h[:, 0:16]))
                tiles(body)
                tgt_logit = dm[:, 0, :].rearrange("p (t h) -> p t h", h=GH)
                for q, dst in enumerate((node[:, :, 16:20], tgt_logit)):
                    V.run(DVE.tensor_tensor(pr[:], node[:, :, 0:16], att[:, q, :].unsqueeze(1).broadcast_to([P, NT, 16]), ALU.mult))
                    V.run(DVE.tensor_reduce(dst, pr[:].rearrange("p t (h j) -> p t h j", h=GH), AX.X, ALU.add))
                V.run(DVE.tensor_reduce(least[:], node[:, :, 16:20], AX.XY, ALU.min))
                tell("v", "p"); hear("v", "p")
                PE.transpose(ps_x[0:1, 0:P], least[:], ident[:]).then_inc(links["p", "v"], 1)
                hear("p", "v")
                V.run(DVE.tensor_reduce(least[0:1, :], ps_x[0:1, 0:P], AX.X, ALU.min))
                tell("v", "p"); hear("v", "p")
                PE.matmul(ps_h[:, 0:1], ones[0:1, :], least[0:1, :], start=True, stop=True).then_inc(links["p", "v"], 1)
                hear("p", "v")
                V.run(DVE.tensor_scalar(shift[:], ps_h[:, 0:1], -1.0, 1.0, ALU.mult, ALU.add))
                V.run(DVE.tensor_scalar(top[:], node[:, :, 16:20], shift[:, 0:1], None, ALU.add))
                tell("v", "a"); hear("v", "a")
                load(tile_rows(table), node[:])
                loads_done(ACTE)
                barrier()
            with ExitStack() as d:
                oh = sb(d, "oh", [P, 2, U, P])
                sv = sb(d, "sv", [P, 2, U, GH])
                diag = sb(d, "diag", [P, 2, U, GH, P])
                mx = sb(d, "mx", [P, U, GH])
                pp = ps(d, "pp", [P, 2, U, 512])
                sv_made = sem("gat_sv_made")
                diag_made = sem("gat_diag_made")
                summed = sem("gat_summed")
                got, slot_free = gathers("gat", table, lst, nch, TW)
                flat_top = top[:].rearrange("p t h -> p (t h)")

                def begin(i, s):
                    first = (i * RING + s) * U
                    V.go(onehots(oh[:, s % 2], l_sb[:, bass.ds(first, U), 1:2].bitcast(F32)))
                    DVE.wait_ge(got[s], i * (16 * U) + 16 * U)
                    V.go(DVE.tensor_scalar(sv[:, s % 2], row_slot[:, s, :, 16:20], shift[:, 0:1], None, ALU.add))
                    V.go(DVE.tensor_copy(rows_all[:, bass.ds(first, U), 0:TW], row_slot[:, s, :, 0:TW]))
                    V.sync()
                    DVE.sem_inc(sv_made, 1)
                    DVE.sem_inc(slot_free[s], 1)
                    take(ACTE, sv_made)
                    for u in range(U):
                        for h in range(GH):
                            S.go(ACTE.activation(diag[:, s % 2, u, h, :], ident[:], ACT.Copy, scale=sv[:, s % 2, u, h:h + 1]))
                    S.sync()
                    ACTE.sem_inc(diag_made, 1)
                    take(PE, diag_made)
                    for u in range(U):
                        mm = PE.matmul(pp[:, s % 2, u, :], oh[:, s % 2, u, :], diag[:, s % 2, u].rearrange("p h j -> p (h j)"),
                                       start=True, stop=True)
                    mm.then_inc(summed, 1)

                def end(i, s):
                    offsets = tile_offsets(tl, (i * RING + s) * U, U, (NT - 1) * GH)
                    take(DVE, summed)
                    V.run(DVE.tensor_reduce(mx[:], pp[:, s % 2].rearrange("p u (h j) -> p u h j", h=GH), AX.X, ALU.max))
                    for u in range(U):
                        at = flat_top[:, bass.ds(offsets[u], GH)]
                        V.run(DVE.tensor_tensor(at, at, mx[:, u, :], ALU.max))
                ring_loop(nch, begin, end)
                barrier()
            sl = sb(c, "sl", [P, NT, GH])
            V.run(DVE.tensor_scalar(top[:], top[:], shift[:, 0:1], None, ALU.subtract))
            tgt_logit, top_logit = (dm[:, q, :].rearrange("p (t h) -> p t h", h=GH) for q in range(2))
            V.run(DVE.tensor_tensor(top[:], top[:], tgt_logit, ALU.add))
            V.run(leaky(top_logit, top[:]))
            V.run(DVE.tensor_tensor(sl[:], node[:, :, 16:20], tgt_logit, ALU.add))
            V.run(leaky(top[:], sl[:]))
            V.run(DVE.tensor_tensor(top[:], top[:], top_logit, ALU.subtract))
            V.run(DVE.tensor_scalar(top[:], top[:], 0.0, None, ALU.min))
            tell("v", "a"); hear("v", "a")
            weight = sums[:, 4, :].rearrange("p (t h) -> p t h", h=GH)
            S.run(ACTE.activation(weight, top[:], ACT.Exp))
            tell("a", "v"); hear("a", "v")
            for h in range(GH):
                V.run(DVE.tensor_tensor(sums[:, h, :].rearrange("p (t j) -> p t j", j=GH), node[:, :, GH * h:GH * h + GH],
                                        weight[:, :, h:h + 1].broadcast_to([P, NT, GH]), ALU.mult))
            W = 2 * U
            with ExitStack() as d:
                oh = sb(d, "oh", [P, 2, W, P])
                oht = sb(d, "oht", [P, 2, W, P])
                tgt = sb(d, "tgt", [P, 2, W, 8])
                lg = sb(d, "lg", [P, 2, W, GH])
                ex = sb(d, "ex", [P, 2, W, GH])
                msg = sb(d, "msg", [P, 2, W, TW])
                ps_t = ps(d, "ps_t", [P, 2, 2, 512])
                ps_m = ps(d, "ps_m", [P, 2, 512])
                ps_s = ps(d, "ps_s", [P, 2, 512])
                v2p = sem("gat2_onehots")
                p2a = sem("gat2_turned")
                a2p = sem("gat2_turned_copied")
                p2v = sem("gat2_targets")
                v2a = sem("gat2_logits")
                a2v = sem("gat2_weights")
                v2p2 = sem("gat2_messages")
                p2v2 = sem("gat2_sums")
                S.reset(); V.reset()
                with nc.Fori(0, nch // (2 * W)) as i:
                    for s in range(2):
                        first = (i * 2 + s) * W
                        V.go(onehots(oh[:, s], l_sb[:, bass.ds(first, W), 1:2].bitcast(F32)))
                        offsets = tile_offsets(tl, first, W, (NT - 1) * GH)
                        for w in range(W):
                            V.go(DVE.tensor_copy(tgt[:, s, w, :].rearrange("p (a h) -> p a h", a=2),
                                                 dm[:, :, bass.ds(offsets[w], GH)]))
                        V.sync()
                        DVE.sem_inc(v2p, 1)
                        V.reset()
                        take(PE, v2p)
                        for w in range(W):
                            tr = PE.transpose(ps_t[:, s, w // 4, (w % 4) * P:(w % 4 + 1) * P], oh[:, s, w, :], ident[:])
                        tr.then_inc(p2a, 1)
                        take(ACTE, p2a)
                        S.run(ACTE.activation(oht[:, s].rearrange("p (b w) j -> p b (w j)", b=2), ps_t[:, s], ACT.Copy))
                        ACTE.sem_inc(a2p, 1)
                        S.reset()
                    for s in range(2):
                        take(PE, a2p)
                        for w in range(W):
                            mm = PE.matmul(ps_m[:, s, 8 * w:8 * w + 8], oht[:, s, w, :], tgt[:, s, w, :], start=True, stop=True)
                        mm.then_inc(p2v, 1)
                    for s in range(2):
                        first = (i * 2 + s) * W
                        pm = ps_m[:, s, 0:8 * W].rearrange("p (w j) -> p w j", j=8)
                        take(DVE, p2v)
                        V.run(DVE.tensor_tensor(lg[:, s], rows_all[:, bass.ds(first, W), 16:20], pm[:, :, 0:4], ALU.add))
                        V.run(leaky(ex[:, s], lg[:, s]))
                        V.run(DVE.tensor_tensor(lg[:, s], ex[:, s], pm[:, :, 4:8], ALU.subtract))
                        V.run(DVE.tensor_scalar(lg[:, s], lg[:, s], 0.0, None, ALU.min))
                        DVE.sem_inc(v2a, 1)
                        V.reset()
                        take(ACTE, v2a)
                        S.run(ACTE.activation(msg[:, s, :, 16:20], lg[:, s], ACT.Exp))
                        ACTE.sem_inc(a2v, 1)
                        S.reset()
                    for s in range(2):
                        first = (i * 2 + s) * W
                        take(DVE, a2v)
                        for h in range(GH):
                            V.go(DVE.tensor_tensor(msg[:, s, :, 4 * h:4 * h + 4], rows_all[:, bass.ds(first, W), 4 * h:4 * h + 4],
                                                   msg[:, s, :, 16 + h:17 + h].broadcast_to([P, W, GH]), ALU.mult))
                        V.sync()
                        DVE.sem_inc(v2p2, 1)
                        V.reset()
                        take(PE, v2p2)
                        for w in range(W):
                            mm = PE.matmul(ps_s[:, s, 32 * w:32 * w + TW], oh[:, s, w, :], msg[:, s, w, :], start=True, stop=True)
                        mm.then_inc(p2v2, 1)
                    for s in range(2):
                        first = (i * 2 + s) * W
                        offsets = tile_offsets(tl, first, W, (NT - 1) * GH)
                        take(DVE, p2v2)
                        for w in range(W):
                            at = sums[:, :, bass.ds(offsets[w], GH)]
                            V.run(DVE.tensor_tensor(at, at, ps_s[:, s, 32 * w:32 * w + TW].rearrange("p (q h) -> p q h", h=GH), ALU.add))
                        V.reset()
                barrier()
            den = sb(c, "den", [P, NT, GH])
            sc = sb(c, "sc", [P, NT, GH])
            m1 = sb(c, "m1", [P, NT])
            v1 = sb(c, "v1", [P, NT])

            def over_nodes(q):
                return bg[:, q, :].unsqueeze(1).broadcast_to([P, NT, 16])

            def per_node(x):
                return x[:].unsqueeze(2).broadcast_to([P, NT, 16])
            V.run(DVE.tensor_scalar(den[:], weight, 1e-16, None, ALU.add))
            V.run(DVE.reciprocal(den[:], den[:]))
            for h in range(GH):
                V.run(DVE.tensor_tensor(pr[:, :, GH * h:GH * h + GH], sums[:, h, :].rearrange("p (t j) -> p t j", j=GH),
                                        den[:, :, h:h + 1].broadcast_to([P, NT, GH]), ALU.mult))
            V.run(DVE.tensor_tensor(pr[:], pr[:], over_nodes(0), ALU.add))
            V.run(DVE.tensor_reduce(m1[:], pr[:], AX.X, ALU.add))
            V.run(DVE.tensor_scalar(m1[:], m1[:], 1.0 / 16, None, ALU.mult))
            V.run(DVE.tensor_tensor(pr[:], pr[:], per_node(m1), ALU.subtract))
            V.run(DVE.tensor_tensor(node[:, :, 0:16], pr[:], pr[:], ALU.mult))
            V.run(DVE.tensor_reduce(v1[:], node[:, :, 0:16], AX.X, ALU.add))
            V.run(DVE.tensor_scalar(v1[:], v1[:], 1.0 / 16, LN_EPS, ALU.mult, ALU.add))
            tell("v", "a"); hear("v", "a")
            S.run(ACTE.activation(v1[:], v1[:], ACT.Sqrt))
            tell("a", "v"); hear("a", "v")
            V.run(DVE.reciprocal(v1[:], v1[:]))
            V.run(DVE.tensor_tensor(pr[:], pr[:], per_node(v1), ALU.mult))
            V.run(DVE.tensor_tensor(pr[:], pr[:], over_nodes(1), ALU.mult))
            V.run(DVE.tensor_tensor(pr[:], pr[:], over_nodes(2), ALU.add))
            V.run(DVE.tensor_reduce(sc[:], pr[:].rearrange("p t (h j) -> p t j h", h=GH), AX.X, ALU.add))
            V.run(DVE.tensor_scalar(sc[:], sc[:], 1.0 / GH, None, ALU.mult))
            top2(sc, gate, GH)
            barrier()

    def top2(sc, gate, n):
        with ExitStack() as c:
            earlier = sb(c, "earlier", [P, n, n])
            gt = sb(c, "gt", [P, NT, n, n])
            eq = sb(c, "eq", [P, NT, n, n])
            rank = sb(c, "rank", [P, NT, n])
            m = sb(c, "m", [P, NT])
            full = [P, NT, n, n]
            mine, other = sc[:].unsqueeze(3).broadcast_to(full), sc[:].unsqueeze(2).broadcast_to(full)
            V.run(DVE.memset(earlier[:], 0.0))
            for e in range(1, n):
                V.go(DVE.memset(earlier[:, e, 0:e], 1.0))
            V.go(DVE.tensor_tensor(gt[:], other, mine, ALU.is_gt))
            V.run(DVE.tensor_tensor(eq[:], other, mine, ALU.is_equal))
            V.run(DVE.tensor_tensor(eq[:].rearrange("p t a b -> p t (a b)"), eq[:].rearrange("p t a b -> p t (a b)"),
                                    earlier[:].rearrange("p a b -> p (a b)").unsqueeze(1).broadcast_to([P, NT, n * n]), ALU.mult))
            V.run(DVE.tensor_tensor(gt[:], gt[:], eq[:], ALU.add))
            V.go(DVE.tensor_reduce(rank[:], gt[:], AX.X, ALU.add))
            V.run(DVE.tensor_reduce(m[:], sc[:], AX.X, ALU.max))
            V.go(DVE.tensor_scalar(rank[:], rank[:], 1.5, None, ALU.is_lt))
            V.run(DVE.tensor_tensor(gate[:], sc[:], m[:].unsqueeze(2).broadcast_to([P, NT, n]), ALU.subtract))
            tell("v", "a"); hear("v", "a")
            S.run(ACTE.activation(gate[:], gate[:], ACT.Exp))
            tell("a", "v"); hear("a", "v")
            V.run(DVE.tensor_tensor(gate[:], gate[:], rank[:], ALU.mult))
            V.run(DVE.tensor_reduce(m[:], gate[:], AX.X, ALU.add))
            V.run(DVE.reciprocal(m[:], m[:]))
            V.run(DVE.tensor_tensor(gate[:], gate[:], m[:].unsqueeze(2).broadcast_to([P, NT, n]), ALU.mult))

    def experts(tag, n, gate, rs, affine):
        BT = 7
        HALF = BT * P // 2
        with ExitStack() as c:
            w1 = sb(c, "w1", [P, n, 2, 512])
            w2 = sb(c, "w2", [P, n, 4, D])
            b1 = sb(c, "b1", [P, n, 4])
            b2 = sb(c, "b2", [P, n, D])
            xs = sb(c, "xs", [P, 2, D])
            xnt = sb(c, "xnt", [P, 2, BT * P])
            ht = sb(c, "ht", [P, 2, 4, BT * P])
            ps_x = ps(c, "ps_x", [P, 2, 512])
            ps_h = ps(c, "ps_h", [P, 2, 2, 512])
            ps_y = ps(c, "ps_y", [P, 2, 512])
            x_made, x_turned, xs_free, px_free, xnt_full = (sem(f"{q}_{tag}") for q in
                                                           ("x_made", "x_turned", "xs_free", "px_free", "xnt_full"))
            h_full, h_free, ht_full, ht_free, y_full, y_free = (
                sem(f"{q}_{tag}") for q in ("h_full", "h_free", "ht_full", "ht_free", "y_full", "y_free"))
            for e in range(n):
                load(w1[:, e], a["w1_" + tag][e].rearrange("(k p) d -> p k d", p=P))
                load(w2[:, e], a["w2_" + tag][e].rearrange("(k p) d -> p k d", p=P))
                broadcast_row(b2[:, e], a["b2_" + tag][e:e + 1, :], D)
            load(b1[:], a["b1_" + tag])
            loads_done(PE, ACTE, DVE)
            PE.sem_inc(h_free, 2)
            PE.sem_inc(y_free, 2)
            PE.sem_inc(px_free, 2)
            ACTE.sem_inc(ht_free, 2)
            DVE.sem_inc(xs_free, 2)
            V.reset(); S.reset()
            with nc.Fori(0, NT // BT) as blk:
                for j in range(BT):
                    t = blk * BT + j
                    take(DVE, xs_free)
                    V.run(DVE.tensor_scalar(xs[:, j % 2, :], row(x_all, t), one(mean, t), one(rs, t), ALU.subtract, ALU.mult))
                    DVE.sem_inc(x_made, 1)
                    take(PE, x_made)
                    take(PE, px_free)
                    transpose(ps_x[:, j % 2], xs[:, j % 2], 2).then_inc(x_turned, 1)
                    take(ACTE, x_turned)
                    for k in range(2):
                        src = ps_x[:, j % 2, k * P:(k + 1) * P]
                        if affine is None:
                            S.go(ACTE.activation(xnt[:, k, j * P:(j + 1) * P], src, ACT.Copy))
                        else:
                            S.go(ACTE.activation(xnt[:, k, j * P:(j + 1) * P], src, ACT.Identity,
                                                 scale=affine[:, 0, k:k + 1], bias=affine[:, 1, k:k + 1]))
                    S.sync()
                    ACTE.sem_inc(px_free, 1)
                    ACTE.sem_inc(xs_free, 1)
                ACTE.sem_inc(xnt_full, 1)
                S.reset()
                V.reset()

                def hidden(e):
                    for hb in range(4):
                        take(PE, h_free)
                        for half in range(2):
                            for k in range(2):
                                mm = PE.matmul(ps_h[:, hb % 2, half, 0:HALF], w1[:, e, k, hb * P:(hb + 1) * P],
                                               xnt[:, k, half * HALF:(half + 1) * HALF], start=(k == 0), stop=(k == 1))
                        mm.then_inc(h_full, 1)
                        if hb == 0:
                            take(ACTE, ht_free)
                        take(ACTE, h_full)
                        S.run(ACTE.activation(ht[:, e % 2, hb, :].rearrange("p (h w) -> p h w", h=2), ps_h[:, hb % 2, :, 0:HALF],
                                              ACT.Gelu, bias=b1[:, e, hb:hb + 1]))
                        ACTE.sem_inc(h_free, 1)
                    ACTE.sem_inc(ht_full, 1)
                    S.reset()

                def output(e):
                    take(PE, ht_full)
                    for j in range(BT):
                        if j % 2 == 0:
                            take(PE, y_free)
                        for hb in range(4):
                            mm = PE.matmul(ps_y[:, j // 2 % 2, (j % 2) * D:(j % 2 + 1) * D], ht[:, e % 2, hb, j * P:(j + 1) * P],
                                           w2[:, e, hb, :], start=(hb == 0), stop=(hb == 3))
                        if j % 2 == 1 or j == BT - 1:
                            mm.then_inc(y_full, 1)
                    for j in range(BT):
                        t = blk * BT + j
                        g = gate[:, bass.ds(t, 1), e:e + 1]
                        if j % 2 == 0:
                            take(DVE, y_full)
                        V.run(DVE.scalar_tensor_tensor(row(x_all, t), ps_y[:, j // 2 % 2, (j % 2) * D:(j % 2 + 1) * D], g,
                                                       row(x_all, t), ALU.mult, ALU.add))
                        if j % 2 == 1 or j == BT - 1:
                            DVE.sem_inc(y_free, 1)
                    DVE.sem_inc(ht_free, 1)
                    for j in range(BT):
                        t = blk * BT + j
                        V.run(DVE.scalar_tensor_tensor(row(x_all, t), b2[:, e, :], gate[:, bass.ds(t, 1), e:e + 1],
                                                       row(x_all, t), ALU.mult, ALU.add))
                    V.reset()

                take(PE, xnt_full)
                hidden(0)
                for e in range(n):
                    if e + 1 < n:
                        hidden(e + 1)
                    output(e)
            take(PE, h_free, 2)
            take(PE, y_free, 2)
            take(PE, px_free, 2)
            take(ACTE, ht_free, 2)
            take(DVE, xs_free, 2)
            barrier()

    HD = 64
    NH = 8

    def attention_matrix(mat):
        with ExitStack() as c:
            wkv = sb(c, "wkv", [P, 2, 2 * NH, HD])
            mu = sb(c, "mu", [P, 2, 2 * NH])
            wqn = sb(c, "wqn", [HD, NH, D])
            wo = sb(c, "wo", [HD, NH, D])
            xn = sb(c, "xn", [P, 2, D])
            xnt = sb(c, "xnt", [P, 2, D])
            kv = sb(c, "kv", [P, 2, 2 * NH, HD])
            sq = sb(c, "sq", [P, 2 * NH, HD])
            vr = sb(c, "vr", [P, 2 * NH])
            dots = sb(c, "dots", [HD, NH * HD])
            bh = sb(c, "bh", [HD, NH, D])
            ps_x = ps(c, "ps_x", [P, 2, 512])
            ps_kv = ps(c, "ps_kv", [P, 2, 2, 512])
            ps_d = ps(c, "ps_d", [P, 512])
            x_made, x_free, x_turned, px_free, xt_full, xt_free, kv_full, kv_free, sq_made, sd_asked, sd_made, out_made, out_free = (
                sem("mix1_" + q) for q in ("x_made", "x_free", "x_turned", "px_free", "xt_full", "xt_free", "kv_full", "kv_free",
                                           "sq_made", "sd_asked", "sd_made", "out_made", "out_free"))
            load(wkv[:].rearrange("p k h e -> p k (h e)"), a["mqkvt"][:, NH * HD:3 * NH * HD].rearrange("(k p) d -> p k d", p=P))
            load(wqn[:], a["mqkv"][0:NH * HD, :].rearrange("(h e) d -> e h d", e=HD))
            load(wo[:], a["woutt"].rearrange("(h e) d -> e h d", e=HD))
            loads_done(DVE, PE)
            for k in range(2):
                V.run(DVE.tensor_reduce(mu[:, k, :], wkv[:, k], AX.X, ALU.add))
                V.run(DVE.tensor_scalar(mu[:, k, :], mu[:, k, :], 1.0 / HD, None, ALU.mult))
                V.run(DVE.tensor_tensor(wkv[:, k], wkv[:, k], mu[:, k, :].unsqueeze(2).broadcast_to([P, 2 * NH, HD]), ALU.subtract))
            tell("v", "p"); hear("v", "p")
            PE.matmul(ps_d[0:HD, :], zeros[:, 0:HD], wkv[:, 0, 0:NH, :].rearrange("p h e -> p (h e)"), start=True, stop=False)
            PE.sem_inc(px_free, 2)
            PE.sem_inc(xt_free, 2)
            PE.sem_inc(kv_free, 2)
            DVE.sem_inc(x_free, 2)
            DVE.sem_inc(out_free, 2)

            def prepare(t, s):
                take(DVE, x_free)
                V.run(normalize(xn[:, s, :], t))
                DVE.sem_inc(x_made, 1)
                take(PE, x_made)
                take(PE, px_free)
                transpose(ps_x[:, s], xn[:, s], 2).then_inc(x_turned, 1)
                take(ACTE, x_turned)
                S.run(ACTE.activation(xnt[:, s, :], ps_x[:, s, 0:D], ACT.Copy))
                ACTE.sem_inc(px_free, 1)
                ACTE.sem_inc(x_free, 1)
                ACTE.sem_inc(xt_full, 1)
                take(PE, xt_full)
                take(PE, kv_free)
                for h in range(2):
                    for k in range(2):
                        mm = PE.matmul(ps_kv[:, s, h, :], xnt[:, s, k * P:(k + 1) * P],
                                       wkv[:, k, NH * h:NH * h + NH, :].rearrange("p h e -> p (h e)"), start=(k == 0), stop=(k == 1))
                mm.then_inc(kv_full, 1)

            def finish(t, s, rows):
                take(DVE, kv_full)
                take(DVE, out_free)
                V.run(DVE.tensor_copy(kv[:, s].rearrange("p (b h) e -> p b (h e)", b=2), ps_kv[:, s]))
                DVE.sem_inc(kv_free, 1)
                V.run(DVE.tensor_tensor(sq[:], kv[:, s], kv[:, s], ALU.mult))
                V.run(DVE.tensor_reduce(vr[:], sq[:], AX.X, ALU.add))
                V.run(DVE.tensor_scalar(vr[:], vr[:], 1.0 / HD, LN_EPS, ALU.mult, ALU.add))
                DVE.sem_inc(sd_asked, 1)
                take(ACTE, sd_asked)
                S.run(ACTE.activation(vr[:], vr[:], ACT.Sqrt))
                ACTE.sem_inc(sd_made, 1)
                take(DVE, sd_made)
                V.run(DVE.tensor_tensor(vr[:, 0:NH], vr[:, 0:NH], vr[:, NH:2 * NH], ALU.mult))
                V.run(DVE.reciprocal(vr[:, 0:NH], vr[:, 0:NH]))
                V.run(DVE.tensor_tensor(kv[:, s, 0:NH, :], kv[:, s, 0:NH, :], vr[:, 0:NH].unsqueeze(2).broadcast_to([P, NH, HD]), ALU.mult))
                DVE.sem_inc(out_made, 1)
                take(PE, out_made)
                for h in range(NH):
                    mm = PE.matmul(ps_d[0:HD, h * HD:(h + 1) * HD], kv[0:rows, s, NH + h, :], kv[0:rows, s, h, :],
                                   start=False, stop=False)
                mm.then_inc(out_free, 1)

            V.reset(); S.reset()
            with nc.Fori(0, NT // 2) as i:
                for s in range(2):
                    prepare(i * 2 + s, s)
                for s in range(2):
                    finish(i * 2 + s, s, P)
                V.reset(); S.reset()
            prepare(NT - 1, 0)
            finish(NT - 1, 0, LAST)
            PE.matmul(ps_d[0:HD, :], zeros[:, 0:HD], wkv[:, 0, 0:NH, :].rearrange("p h e -> p (h e)"),
                      start=False, stop=True).then_inc(links["p", "v"], 1)
            hear("p", "v")
            take(DVE, out_free, 2)
            take(DVE, x_free, 2)
            take(PE, kv_free, 2)
            take(PE, px_free, 2)
            take(PE, xt_free, 2)
            V.run(DVE.tensor_scalar(dots[:], ps_d[0:HD, :], 1.0 / N, None, ALU.mult))
            tell("v", "p"); hear("v", "p")
            for h in range(NH):
                mm = PE.matmul(ps_kv[0:HD, h // 4, h // 2 % 2, (h % 2) * D:(h % 2 + 1) * D], dots[:, h * HD:(h + 1) * HD], wo[:, h, :],
                               start=True, stop=True)
            mm.then_inc(links["p", "v"], 1)
            hear("p", "v")
            V.run(DVE.tensor_copy(bh[:].rearrange("p (b h) d -> p b (h d)", b=4), ps_kv[0:HD].rearrange("p a b w -> p (a b) w")))
            tell("v", "p"); hear("v", "p")
            for k in range(2):
                for h in range(NH):
                    mm = PE.matmul(ps_x[:, k, 0:D], wqn[:, h, k * P:(k + 1) * P], bh[:, h, :], start=(h == 0), stop=(h == NH - 1))
            mm.then_inc(links["p", "v"], 1)
            hear("p", "v")
            V.run(DVE.tensor_copy(mat[:], ps_x[:, :, 0:D]))
            barrier()

    def gcn1_project(layer, acc, res, table, mat):
        with ExitStack() as c:
            w = sb(c, "w", [P, 2, D])
            rw = sb(c, "rw", [P, 2, D])
            b = sb(c, "b", [P, 3, D])
            x = sb(c, "x", [P, D])
            xt = sb(c, "xt", [P, D])
            ps_x = ps(c, "ps_x", [P, 512])
            ps_h = ps(c, "ps_h", [P, 3, 512])
            load(w[:], a["gw"][layer].rearrange("(k p) d -> p k d", p=P))
            load(rw[:], a["resw"].rearrange("(k p) d -> p k d", p=P))
            broadcast_row(b[:, 0, :], a["gb"][layer:layer + 1, :], D)
            broadcast_row(b[:, 1, :], a["resb"], D)
            broadcast_row(b[:, 2, :], a["bout"], D)
            loads_done(PE, DVE)
            V.run(DVE.tensor_tensor(b[:, 0, :], b[:, 0, :], b[:, 1, :], ALU.add))

            def body(t, slot, last):
                if layer == 0:
                    V.run(normalize(x[:], t))
                else:
                    V.run(DVE.scalar_tensor_tensor(x[:], row(acc, t), one(deg_dst, t), row(res, t), ALU.mult, ALU.add))
                    V.run(DVE.tensor_scalar(x[:], x[:], 0.0, None, ALU.max))
                tell("v", "p"); hear("v", "p")
                transpose(ps_x, x, 2).then_inc(links["p", "a"], 1)
                hear("p", "a")
                S.run(ACTE.activation(xt[:], ps_x[:, 0:D], ACT.Copy))
                tell("a", "p"); hear("a", "p")
                for q, m in enumerate((w, rw) if layer else (w, rw, mat)):
                    for k in range(2):
                        mm = PE.matmul(ps_h[:, q, 0:D], xt[:, k * P:(k + 1) * P], m[:, k, :], start=(k == 0), stop=(k == 1))
                mm.then_inc(links["p", "v"], 1)
                hear("p", "v")
                V.go(DVE.tensor_scalar(row(acc, t), ps_h[:, 0, 0:D], one(deg_dst, t), None, ALU.mult))
                V.go(DVE.tensor_tensor(row(res, t), ps_h[:, 1, 0:D], b[:, 0, :], ALU.add))
                if layer == 0:
                    V.run(DVE.tensor_tensor(row(x_all, t), row(x_all, t), ps_h[:, 2, 0:D], ALU.add))
                    V.run(DVE.tensor_tensor(row(x_all, t), row(x_all, t), b[:, 2, :], ALU.add))
                V.sync()
            tiles(body)
            tell("v", "a"); hear("v", "a")
            load(tile_rows(table), acc[:])
            loads_done(ACTE)
            barrier()

    def gcn1_finish(acc, res):
        V.reset()
        with DVE.Fori(0, NT) as t:
            V.run(DVE.scalar_tensor_tensor(row(acc, t), row(acc, t), one(deg_dst, t), row(res, t), ALU.mult, ALU.add))
            V.run(DVE.scalar_tensor_tensor(row(x_all, t), row(acc, t), 0.0, row(x_all, t), ALU.max, ALU.add))
            V.reset()
        barrier()

    def route1(gate, rs, affine):
        with ExitStack() as c:
            wr = sb(c, "wr", [P, 2, 8])
            br = sb(c, "br", [P, 8])
            sc = sb(c, "sc", [P, NT, 8])
            x = sb(c, "x", [P, D])
            xt = sb(c, "xt", [P, D])
            ps_x = ps(c, "ps_x", [P, 512])
            ps_h = ps(c, "ps_h", [P, 512])
            load(wr[:], a["wr"].rearrange("(k p) d -> p k d", p=P))
            load(affine[:, 0, :], a["fg"])
            load(affine[:, 1, :], a["fb"])
            broadcast_row(br[:], a["br"], 8)
            loads_done(PE, DVE, ACTE)
            V.run(DVE.tensor_tensor(rs[:], rstd[:], rstd[:], ALU.mult))
            V.run(DVE.tensor_tensor(rs[:], rs[:], var[:], ALU.mult))
            V.run(DVE.tensor_scalar(rs[:], rs[:], LN_EPS, None, ALU.add))
            tell("v", "a"); hear("v", "a")
            S.run(ACTE.activation(rs[:], rs[:], ACT.Sqrt))
            tell("a", "v"); hear("a", "v")
            V.run(DVE.reciprocal(rs[:], rs[:]))
            V.run(DVE.tensor_tensor(rs[:], rs[:], rstd[:], ALU.mult))

            def body(t, slot, last):
                V.run(DVE.tensor_scalar(x[:], row(x_all, t), one(mean, t), one(rs, t), ALU.subtract, ALU.mult))
                tell("v", "p"); hear("v", "p")
                transpose(ps_x, x, 2).then_inc(links["p", "a"], 1)
                hear("p", "a")
                for k in range(2):
                    S.run(ACTE.activation(xt[:, k * P:(k + 1) * P], ps_x[:, k * P:(k + 1) * P], ACT.Identity,
                                          scale=affine[:, 0, k:k + 1], bias=affine[:, 1, k:k + 1]))
                tell("a", "p"); hear("a", "p")
                for k in range(2):
                    mm = PE.matmul(ps_h[:, 0:8], xt[:, k * P:(k + 1) * P], wr[:, k, :], start=(k == 0), stop=(k == 1))
                mm.then_inc(links["p", "v"], 1)
                hear("p", "v")
                V.run(DVE.tensor_tensor(row(sc, t), ps_h[:, 0:8], br[:], ALU.add))
            tiles(body)
            top2(sc, gate, 8)
            barrier()

    def edges(name, rows):
        return a[name].rearrange("(r c) -> r c", r=rows)

    def show(stage):
        if dbg.get("stage") == stage:
            load(out[0:(NT - 1) * P, :].rearrange("(t p) d -> p t d", p=P), x_all[:, 0:NT - 1, :])
            load(out[(NT - 1) * P:N, :], x_all[0:LAST, NT - 1, :])
            loads_done(ACTE)
            return True

    chunk_tiles = sb(top, "chunk_tiles", [P, NCH_GNN])
    list0, offs0, list0_done = bucket("l0", edges("src", GNN_ROWS), edges("dst", GNN_ROWS), GNN_ROWS, GNN_COLS,
                                             NCH_GNN, False, D, chunk_tiles)
    norm_stats()
    table0 = dram("table0", [NP, D])
    degrees(list0, list0_done, chunk_tiles, NCH_GNN, deg_src)
    with ExitStack() as c:
        acc = sb(c, "acc", [P, NT, D])
        z_scale = sb(c, "z_scale", [P, NT])
        cov = sb(c, "cov", [P, 2, D])
        zmean = sb(c, "zmean", [P, 2, 1])
        gcn0_table(acc, table0, z_scale, cov, zmean)
        gather_sum("l0", acc, table0, list0, offs0, NCH_GNN)
        with ExitStack() as d:
            listg, offsg, listg_done = bucket("gat", edges("gat_dst", GAT_ROWS), edges("gat_src", GAT_ROWS),
                                                     GAT_ROWS, GAT_COLS, NCH_GAT, True, GH)
        mix0(z_scale, cov, zmean)
        add_scaled(acc, deg_src)
        barrier()
    if show(3):
        return
    norm_stats()
    gate0 = sb(top, "gate0", [P, NT, GH])
    gat_scores(listg, listg_done, offsg, NCH_GAT, gate0)
    if dbg.get("stage") == 4:
        load(dbg["gate"], gate0[:].rearrange("p t e -> p (t e)"))
        loads_done(ACTE)
        show(4)
        return
    list1, offs1, list1_done = bucket("l1", edges("dst", GNN_ROWS), edges("src", GNN_ROWS), GNN_ROWS, GNN_COLS,
                                             NCH_GNN, False, D, chunk_tiles)
    experts("0", GH, gate0, rstd, None)
    if show(5):
        return
    degrees(list1, list1_done, chunk_tiles, NCH_GNN, deg_dst)
    norm_stats()
    with ExitStack() as c:
        mat = sb(c, "mat", [P, 2, D])
        attention_matrix(mat)
        acc = sb(c, "acc", [P, NT, D])
        res = sb(c, "res", [P, NT, D])
        for layer in range(2):
            table = dram(f"table1{layer}", [NP, D])
            gcn1_project(layer, acc, res, table, mat)
            gather_sum(f"l1{layer}", acc, table, list1, offs1, NCH_GNN)
        gcn1_finish(acc, res)
    if show(6):
        return
    norm_stats()
    gate1 = sb(top, "gate1", [P, NT, 8])
    rs = sb(top, "rs", [P, NT])
    affine = sb(top, "affine", [P, 2, 2])
    route1(gate1, rs, affine)
    experts("1", 8, gate1, rs, affine)
    store_sem = sem("stores")
    ACTE.dma_start(out[0:(NT - 1) * P, :].rearrange("(t p) d -> p t d", p=P), x_all[:, 0:NT - 1, :]).then_inc(store_sem, 16)
    ACTE.dma_start(out[(NT - 1) * P:N, :], x_all[0:LAST, NT - 1, :]).then_inc(store_sem, 16)
    ACTE.wait_ge(store_sem, 32)


def lay_out(inputs):
    c = np.ascontiguousarray
    i = {k: np.asarray(v) for k, v in inputs.items()}
    return {
        "x": c(i["x"]), "src": c(i["src"]), "dst": c(i["dst"]),
        "gat_src": c(i["L0_ffn_edge_index"][0]), "gat_dst": c(i["L0_ffn_edge_index"][1]),
        "w0t": c(i["L0_gnn_W"].T),
        "qkvt": c(i["L0_mix_w_qkv"][:, :, 2].T),
        "gamma": c(i["L0_mix_bn_gamma"].reshape(1, -1)), "beta": c(i["L0_mix_bn_beta"].reshape(1, -1)),
        "dw": c(i["L0_mix_w_dw"][:, 0, 2].reshape(6, P).T),
        "pwt": c(i["L0_mix_w_pw"][:, :, 0].reshape(24, 32, 32).transpose(0, 2, 1)),
        "rest": c(i["L0_mix_w_res"][:, :, 0].T), "bres": c(i["L0_mix_b_res"].reshape(1, -1)),
        "wgat": c(i["L0_ffn_W_gat"]),
        "att_src": c(i["L0_ffn_att_src"].reshape(1, -1)), "att_dst": c(i["L0_ffn_att_dst"].reshape(1, -1)),
        "bgat": c(i["L0_ffn_b_gat"].reshape(1, -1)),
        "lng": c(i["L0_ffn_ln_gamma"].reshape(1, -1)), "lnb": c(i["L0_ffn_ln_beta"].reshape(1, -1)),
        "w1_0": c(i["L0_ffn_W1"]), "b1_0": c(i["L0_ffn_b1"].reshape(4, 4, P).transpose(2, 0, 1)), "w2_0": c(i["L0_ffn_W2"]), "b2_0": c(i["L0_ffn_b2"]),
        "gw": c(i["L1_gnn_W"]), "gb": c(i["L1_gnn_b"]), "resw": c(i["L1_gnn_resW"]),
        "resb": c(i["L1_gnn_resb"].reshape(1, -1)),
        "mqkv": c(i["L1_mix_w_qkv"]), "mqkvt": c(i["L1_mix_w_qkv"].T), "woutt": c(i["L1_mix_w_out"].T),
        "bout": c(i["L1_mix_b_out"].reshape(1, -1)),
        "fg": c(i["L1_ffn_gamma"].reshape(2, P).T), "fb": c(i["L1_ffn_beta"].reshape(2, P).T),
        "wr": c(i["L1_ffn_Wr"]), "br": c(i["L1_ffn_br"].reshape(1, -1)),
        "w1_1": c(i["L1_ffn_W1"]), "b1_1": c(i["L1_ffn_b1"].reshape(8, 4, P).transpose(2, 0, 1)), "w2_1": c(i["L1_ffn_W2"]), "b2_1": c(i["L1_ffn_b2"]),
    }


def kernel(**inputs):
    import concourse.bacc as _bacc
    from concourse import mybir as _mybir
    from concourse.bass_utils import run_bass_kernel_spmd as _run

    laid = lay_out(inputs)
    nc = _bacc.Bacc("TRN2", target_bir_lowering=False, num_devices=1)
    arrays, aps = {}, {}
    for name, v in laid.items():
        arrays[f"in_{name}"] = v
        aps[name] = nc.dram_tensor(f"in_{name}", v.shape, _mybir.dt.from_np(v.dtype), kind="ExternalInput").ap()
    out = nc.dram_tensor("out_x", (N, D), F32, kind="ExternalOutput").ap()
    program(nc, aps, out)
    r = _run(nc, [arrays], core_ids=[0])
    return r.results[0]["out_x"]
```

```python
from contextlib import ExitStack

import numpy as np

import concourse.bass as bass
from concourse import mybir

F32 = mybir.dt.float32
BF16 = mybir.dt.bfloat16
I32 = mybir.dt.int32
U8 = mybir.dt.uint8
ALU = mybir.AluOpType
ACT = mybir.ActivationFunctionType
AX = mybir.AxisListType

P = 128
N = 6250
D = 256
NT = (N + P - 1) // P
NP = NT * P
LAST = N - (NT - 1) * P
LN_EPS = 1e-5
MAXNORM = float(np.float32(1.0 - 1e-5))
ATANH_MAX = float(np.arctanh(np.float64(MAXNORM)))
MIN_NORM = 1e-15
U = 4


def rounded_chunks(n_edges):
    most = (n_edges + NT * (P - 1)) // P
    return -(-most // (8 * U)) * 8 * U


E_GNN = 100000
GNN_ROWS, GNN_COLS = 125, 800
E_GAT = 131072
GAT_ROWS, GAT_COLS = 128, 1024
NCH_GNN = rounded_chunks(E_GNN)
NCH_GAT = rounded_chunks(E_GAT)


class Chain:

    def __init__(self, engine, sem):
        self.engine, self.sem, self.count = engine, sem, 0

    def go(self, instruction):
        instruction.then_inc(self.sem, 1)
        self.count += 1

    def sync(self):
        if self.count:
            self.engine.wait_ge(self.sem, self.count)

    def run(self, instruction):
        self.go(instruction)
        self.sync()

    def reset(self):
        if self.count:
            self.sync()
            self.engine.sem_inc(self.sem, -self.count)
            self.count = 0


def take(engine, sem, n=1):
    engine.wait_ge(sem, n)
    engine.sem_inc(sem, -n)


def program(nc, a, out):
    with ExitStack() as top:
        _program(nc, a, out, top)


def _program(nc, a, out, top):
    PE, DVE, ACTE, POOL, SP = nc.tensor, nc.vector, nc.scalar, nc.gpsimd, nc.sync

    names = {}

    def fresh(name):
        names[name] = names.get(name, 0) + 1
        return name if names[name] == 1 else f"{name}_{names[name]}"

    def sem(name):
        return top.enter_context(nc.semaphore(fresh(name)))

    lane = [0]

    class Links:
        def __init__(self):
            self.sems = [{(p, q): sem(f"{p}_to_{q}_{x}") for p, q in ("vp", "pv", "va", "av", "ap", "pa", "as", "ag")} for x in range(2)]

        def __getitem__(self, pair):
            return self.sems[lane[0]][pair]

    links = Links()
    engines = {"v": DVE, "p": PE, "a": ACTE, "g": POOL, "s": SP}

    def tell(p, q):
        engines[p].sem_inc(links[p, q], 1)

    def hear(p, q):
        take(engines[q], links[p, q])

    V = Chain(DVE, sem("dve_own"))
    S = Chain(ACTE, sem("act_own"))

    def sb(ctx, name, shape, dt=F32):
        return ctx.enter_context(nc.sbuf_tensor(fresh(name), shape, dt))

    def ps(ctx, name, shape, dt=F32):
        return ctx.enter_context(nc.psum_tensor(fresh(name), shape, dt))

    def dram(name, shape, dt=F32):
        return nc.dram_tensor(fresh(name), shape, dt).ap()

    met = {q: sem(f"met_{q}") for q in ("pe_to_dve", "act_to_dve", "dve_to_pe", "dve_to_act")}

    def barrier():
        V.reset(); S.reset()
        PE.drain().then_inc(met["pe_to_dve"], 1)
        ACTE.sem_inc(met["act_to_dve"], 1)
        take(DVE, met["pe_to_dve"]); take(DVE, met["act_to_dve"])
        DVE.sem_inc(met["dve_to_pe"], 1); DVE.sem_inc(met["dve_to_act"], 1)
        take(PE, met["dve_to_pe"]); take(ACTE, met["dve_to_act"])

    load_sem = sem("loads")
    loads = [0]

    def load(dst, src):
        ACTE.dma_start(dst, src).then_inc(load_sem, 16)
        loads[0] += 16

    def loads_done(*engines):
        for e in engines:
            e.wait_ge(load_sem, loads[0])

    def tiles(steps, slots):
        turns = (NT - 1) // slots
        assert (NT - 1) % slots == 0 and slots % 2 == 0
        half, n = slots // 2, len(steps)
        mid = n // 2

        def both(step, first_tile, first_slot):
            lane[0] = 1 if first_slot else 0
            for s in range(half):
                step(first_tile + s, first_slot + s)
            lane[0] = 0

        def turn(i, then):
            for k in range(n):
                both(steps[k], i * slots, 0)
                if k < n - mid:
                    both(steps[mid + k], i * slots + half, half)
                else:
                    then(steps[k - (n - mid)])

        def last_tile(step):
            lane[0] = 1
            step(NT - 1, half)
            lane[0] = 0
        V.reset(); S.reset()
        for k in range(mid):
            both(steps[k], half, half)
        V.reset(); S.reset()
        with nc.Fori(0, turns - 1) as i:
            turn(i, lambda step: both(step, i * slots + (slots + half), half))
            V.reset(); S.reset()
        turn(turns - 1, last_tile)
        for k in range(mid, n):
            last_tile(steps[k])
        V.reset(); S.reset()

    def tiles_in_step(steps, slots):
        assert (NT - 1) % slots == 0
        V.reset(); S.reset()
        with nc.Fori(0, (NT - 1) // slots) as i:
            for step in steps:
                for slot in range(slots):
                    step(i * slots + slot, slot)
            V.reset(); S.reset()
        for step in steps:
            step(NT - 1, 0)
        V.reset(); S.reset()

    ident = sb(top, "ident", [P, P])
    ones = sb(top, "ones", [P, P])
    before = sb(top, "before", [P, P])
    iota_row = sb(top, "iota_row", [P, P])
    zeros = sb(top, "zeros", [P, P])
    zwide = sb(top, "zwide", [P, D + 1])
    row_no = sb(top, "row_no", [P, 1])
    window = sb(top, "window", [P, 2 * NT])
    x_all = sb(top, "x_all", [P, NT, D])
    RING = 4
    COLS = 8
    place_slot = sb(top, "place_slot", [P, RING, COLS, 3], I32)
    index_slot = sb(top, "index_slot", [P, RING, U, 2], I32)
    row_slot = sb(top, "row_slot", [P, RING, U, D])
    deg_src = sb(top, "deg_src", [P, NT])
    deg_dst = sb(top, "deg_dst", [P, NT])
    mean = sb(top, "mean", [P, NT])
    var = sb(top, "var", [P, NT])
    rstd = sb(top, "rstd", [P, NT])

    with ExitStack() as c:
        it = sb(c, "it", [P, P], I32)
        ir = sb(c, "ir", [P, 1], I32)
        s_iota = sem("iota_made")
        POOL.iota(it[:], [[1, P]], 0, 0).then_inc(s_iota, 1)
        POOL.iota(ir[:], [[0, 1]], 0, 1).then_inc(s_iota, 1)
        DVE.wait_ge(s_iota, 2)
        V.go(DVE.memset(ones[:], 1.0))
        V.go(DVE.memset(zeros[:], 0.0))
        V.go(DVE.memset(zwide[:], 0.0))
        V.go(DVE.memset(window[:], 0.0))
        V.go(DVE.memset(x_all[:, NT - 1, :], 0.0))
        V.go(DVE.tensor_copy(iota_row[:], it[:]))
        V.run(DVE.tensor_copy(row_no[:], ir[:]))
        V.go(DVE.memset(zeros[:], 0.0))
        V.go(DVE.memset(zwide[:], 0.0))
        V.go(DVE.memset(window[:, NT - 1:NT], 1.0))
        V.go(DVE.tensor_scalar(ident[:], iota_row[:], row_no[:, 0:1], None, ALU.is_equal))
        V.run(DVE.tensor_scalar(before[:], iota_row[:], row_no[:, 0:1], None, ALU.is_gt))
        barrier()
    load(x_all[:, 0:NT - 1, :], a["x"][0:(NT - 1) * P, :].rearrange("(t p) d -> p t d", p=P))
    load(x_all[0:LAST, NT - 1, :], a["x"][(NT - 1) * P:N, :])
    loads_done(DVE)

    def bucket(tag, key, other, rows, cols, nch, clamp, stride, first_place, tile_f=None):
        places = dram(f"places_{tag}", [rows, cols, 3], I32)
        written = [sem(f"written_{tag}{s}") for s in range(RING)]
        lst = dram(f"list_{tag}", [P * nch, 2], I32)
        tile_of = dram(f"tile_of_{tag}", [1, nch], I32)
        with ExitStack() as c:
            if tile_f is None:
                tile_f = sb(c, "tile_f", [P, nch])
            k_i = sb(c, "k_i", [rows, cols], I32)
            t_i = sb(c, "t_i", [rows, cols], I32)
            t_f = sb(c, "t_f", [rows, cols])
            place = sb(c, "place", [rows, cols, 3], I32)
            o_i = sb(c, "o_i", [rows, cols], I32)
            same = sb(c, "same", [rows, cols])
            mask = sb(c, "mask", [rows, cols], U8)
            run_ = sb(c, "run", [rows, cols])
            pos = sb(c, "pos", [rows, cols])
            zero = sb(c, "zero", [rows, cols])
            total = sb(c, "total", [rows, NT])
            start = sb(c, "start", [rows, NT])
            cap_f = sb(c, "cap_f", [NT, 1])
            cap_i = sb(c, "cap_i", [NT, 1], I32)
            base = sb(c, "base", [NT, 1])
            end = sb(c, "end", [NT, 1])
            dbase = sb(c, "dbase", [NT, NT])
            ge = sb(c, "ge", [NT, nch])
            tl = sb(c, "tl", [1, nch], I32)
            empty = sb(c, "empty", [P, nch, 2], I32)
            ps_a = ps(c, "ps_a", [P, 512])
            ps_b = ps(c, "ps_b", [P, 512])
            ps_t = ps(c, "ps_t", [P, 3, 512])
            cleared = sem("cleared")
            staged = [sem(f"staged{s}") for s in range(RING)]
            placed = sem("placed")

            load(k_i[:], key)
            load(o_i[:], other)
            loads_done(DVE)
            V.go(DVE.memset(empty[:, :, 0], NP - 1))
            V.run(DVE.memset(empty[:, :, 1].bitcast(F32), -1.0))
            tell("v", "a")
            hear("v", "a")
            ACTE.dma_start(lst.rearrange("(p c) w -> p c w", p=P), empty[:]).then_inc(cleared, 16)
            if clamp:
                V.go(DVE.tensor_scalar(k_i[:], k_i[:], NP - 1, None, ALU.min))
                V.run(DVE.tensor_scalar(o_i[:], o_i[:], N - 1, None, ALU.min))
            V.go(DVE.tensor_scalar(t_i[:], k_i[:], 7, None, ALU.arith_shift_right))
            V.go(DVE.tensor_copy(place[:, :, 1], o_i[:]))
            V.go(DVE.memset(zero[:], 0.0))
            V.run(DVE.tensor_scalar(k_i[:], k_i[:], 127, None, ALU.bitwise_and))
            V.go(DVE.tensor_copy(place[:, :, 2].bitcast(F32), k_i[:]))
            V.run(DVE.tensor_copy(t_f[:], t_i[:]))
            for b in range(NT):
                V.run(DVE.tensor_scalar(same[:], t_f[:], float(b), 0.0, ALU.is_equal, ALU.add,
                                        accum_out=total[:, b:b + 1]))
            tell("v", "p")
            hear("v", "p")
            PE.matmul(ps_b[0:NT, 0:1], total[:], ones[0:rows, 0:1], start=True, stop=True).then_inc(links["p", "v"], 1)
            hear("p", "v")
            V.run(DVE.tensor_scalar(cap_i[:], ps_b[0:NT, 0:1], 127.0, None, ALU.add))
            V.run(DVE.tensor_scalar(cap_i[:], cap_i[:], 7, 7, ALU.arith_shift_right, ALU.arith_shift_left))
            V.run(DVE.tensor_copy(cap_f[:], cap_i[:]))
            tell("v", "p")
            hear("v", "p")
            PE.matmul(ps_b[0:NT, 1:2], before[0:NT, 0:NT], cap_f[:], start=True, stop=True).then_inc(links["p", "v"], 1)
            hear("p", "v")
            V.run(DVE.tensor_copy(base[:], ps_b[0:NT, 1:2]))
            V.go(DVE.tensor_tensor(end[:], base[:], cap_f[:], ALU.add))
            V.run(DVE.tensor_scalar(dbase[:], ident[0:NT, 0:NT], base[:, 0:1], None, ALU.mult))
            tell("v", "p")
            hear("v", "p")
            PE.matmul(ps_a[0:rows, 0:NT], before[0:rows, 0:rows], total[:], start=True, stop=False)
            PE.matmul(ps_a[0:rows, 0:NT], ones[0:NT, 0:rows], dbase[:], start=False, stop=True).then_inc(links["p", "v"], 1)
            hear("p", "v")
            V.run(DVE.tensor_scalar(start[:], ps_a[0:rows, 0:NT], -1.0, None, ALU.add))
            V.run(DVE.tensor_scalar(ge[:], first_place[:, 0:nch], end[:, 0:1], None, ALU.is_ge))
            tell("v", "p")
            hear("v", "p")
            for q in range(0, nch, 512):
                w = min(512, nch - q)
                mm = PE.matmul(ps_t[:, q // 512, 0:w], ones[0:NT, :], ge[:, q:q + w], start=True, stop=True)
            mm.then_inc(links["p", "v"], 1)
            hear("p", "v")
            for q in range(0, nch, 512):
                w = min(512, nch - q)
                V.go(DVE.tensor_scalar(tile_f[:, q:q + w], ps_t[:, q // 512, 0:w], float(NT - 1), None, ALU.min))
            V.sync()
            V.run(DVE.tensor_scalar(tl[:], tile_f[0:1, :], float(stride), None, ALU.mult))
            tell("v", "a")
            hear("v", "a")
            ACTE.dma_start(tile_of, tl[:]).then_inc(load_sem, 16)
            loads[0] += 16
            for b in range(NT):
                V.go(DVE.tensor_scalar(mask[:], t_f[:], float(b), None, ALU.is_equal))
                V.run(DVE.tensor_scalar(same[:], t_f[:], float(b), None, ALU.is_equal))
                V.run(DVE.tensor_tensor_scan(run_[:], same[:], zero[:], start[:, b:b + 1], ALU.add, ALU.add))
                V.run(DVE.copy_predicated(pos[:], mask[:], run_[:]) if b else DVE.tensor_copy(pos[:], run_[:]))
            V.run(DVE.tensor_copy(k_i[:], pos[:]))
            V.go(DVE.tensor_scalar(t_i[:], k_i[:], 7, None, ALU.arith_shift_right))
            V.run(DVE.tensor_scalar(k_i[:], k_i[:], 127, None, ALU.bitwise_and))
            V.run(DVE.scalar_tensor_tensor(place[:, :, 0], k_i[:], float(nch), t_i[:], ALU.mult, ALU.add))
            tell("v", "a")
            hear("v", "a")
            ACTE.dma_start(places, place[:]).then_inc(placed, 16)
            ACTE.wait_ge(placed, 16)
            ACTE.wait_ge(cleared, 16)
            POOL.wait_ge(cleared, 16)
            loads_done(ACTE)
            barrier()

        def bring(first, s):
            SP.dma_start(place_slot[0:rows, s], places[:, bass.ds(first, COLS), :]).then_inc(staged[s], 16)

        def put(s):
            take(POOL, staged[s], 16)
            for j in range(COLS):
                POOL.indirect_dma_start(lst, bass.IndirectOffsetOnAxis(ap=place_slot[0:rows, s, j, 0:1], axis=0),
                                        place_slot[0:rows, s, j, 1:3], None).then_inc(written[s], 16)

        turns = cols // (COLS * RING)

        def list_done(engine):
            for s in range(RING):
                engine.wait_ge(written[s], turns * 16 * COLS)

        def send():
            SP.wait_ge(placed, 16)
            for s in range(RING):
                bring(COLS * s, s)
            with SP.Fori(1, turns) as i:
                for s in range(RING):
                    SP.wait_ge(written[s], i * (16 * COLS))
                    bring(i * (COLS * RING) + COLS * s, s)
            with POOL.Fori(0, turns) as i:
                for s in range(RING):
                    put(s)
            list_done(SP)
        return lst, tile_of, list_done, send

    def onehots(dst, low):
        n = dst.shape[1]
        return DVE.tensor_tensor(dst, iota_row[:].unsqueeze(1).broadcast_to([P, n, P]),
                                 low.broadcast_to([P, n, P]), ALU.is_equal)

    def tile_offsets(tl, first, n, most):
        _, values = nc.values_load_multi_w_load_instructions(
            tl[0:1, bass.ds(first, n)], engines=[mybir.EngineType.DVE], min_val=0, max_val=most,
            skip_runtime_bounds_check_because="bucket() takes the minimum with the last tile")
        return values

    def degrees(lst, list_done, tile_f, nch, deg):
        W = 4 * U
        with ExitStack() as c:
            l_sb = sb(c, "l_sb", [P, nch, 2], I32)
            oh = sb(c, "oh_deg", [P, 2, W, P], BF16)
            at = sb(c, "at_deg", [P, 2, W, NT], BF16)
            cnt = ps(c, "cnt", [P, 512])
            made = sem("oh_made")
            free = sem("oh_free")
            list_done(ACTE)
            load(l_sb[:], lst.rearrange("(p c) w -> p c w", p=P))
            loads_done(DVE)
            PE.matmul(cnt[:, 0:NT], zeros[:], zeros[:, 0:NT], start=True, stop=False)
            V.reset()
            DVE.sem_inc(free, 2)
            with nc.Fori(0, nch // (2 * W)) as i:
                for slot in range(2):
                    first = (i * 2 + slot) * W
                    take(DVE, free)
                    V.go(onehots(oh[:, slot], l_sb[:, bass.ds(first, W), 1:2].bitcast(F32)))
                    V.go(DVE.tensor_tensor(at[:, slot], iota_row[:, 0:NT].unsqueeze(1).broadcast_to([P, W, NT]),
                                           tile_f[:, bass.ds(first, W)].unsqueeze(2).broadcast_to([P, W, NT]), ALU.is_equal))
                    V.sync()
                    DVE.sem_inc(made, 1)
                    V.reset()
                    take(PE, made)
                    for w in range(W):
                        mm = PE.matmul(cnt[:, 0:NT], oh[:, slot, w, :], at[:, slot, w, :], start=False, stop=False)
                    mm.then_inc(free, 1)
            PE.matmul(cnt[:, 0:NT], zeros[:], zeros[:, 0:NT], start=False, stop=True).then_inc(links["p", "v"], 1)
            hear("p", "v")
            take(DVE, free, 2)
            V.run(DVE.tensor_scalar(deg[:], cnt[:, 0:NT], 1.0, None, ALU.add))
            V.run(DVE.reciprocal(deg[:], deg[:]))
            tell("v", "a")
            hear("v", "a")
            S.run(ACTE.activation(deg[:], deg[:], ACT.Sqrt))
            barrier()

    def gathers(tag, table, lst, nch, width):
        staged = [sem(f"index_staged_{tag}{s}") for s in range(RING)]
        got = [sem(f"got_{tag}{s}") for s in range(RING)]
        slot_free = [sem(f"slot_free_{tag}{s}") for s in range(RING)]
        tell("a", "s"); hear("a", "s")
        tell("a", "g"); hear("a", "g")
        indices = lst.rearrange("(p c) w -> p c w", p=P)
        for s in range(RING):
            SP.sem_inc(slot_free[s], 1)
        with SP.Fori(0, nch // (RING * U)) as i:
            for s in range(RING):
                take(SP, slot_free[s])
                SP.dma_start(index_slot[:, s], indices[:, bass.ds((i * RING + s) * U, U), :]).then_inc(staged[s], 16)
        for s in range(RING):
            take(SP, slot_free[s])
        with POOL.Fori(0, nch // (RING * U)) as i:
            for s in range(RING):
                take(POOL, staged[s], 16)
                for u in range(U):
                    POOL.indirect_dma_start(row_slot[:, s, u, 0:width], None, table,
                                            bass.IndirectOffsetOnAxis(ap=index_slot[:, s, u, 0:1], axis=0)
                                            ).then_inc(got[s], 16)
        return got, slot_free

    def ring_loop(nch, begin, end, behind=1):
        turns = nch // (RING * U)

        def turn(i, first):
            for s in range(RING):
                begin(i, s)
                if s >= behind:
                    end(i, s - behind)
                elif not first:
                    end(i - 1, RING + s - behind)
        V.reset(); S.reset()
        turn(0, True)
        V.reset(); S.reset()
        with nc.Fori(1, turns) as i:
            turn(i, False)
            V.reset(); S.reset()
        for s in range(RING - behind, RING):
            end(turns - 1, s)
        V.reset(); S.reset()

    def gather_sum(tag, acc, table, lst, tile_of, nch):
        with ExitStack() as c:
            l_sb = sb(c, "l_sb", [P, nch, 2], I32)
            tl = sb(c, "tl", [1, nch], I32)
            oh = sb(c, "oh", [P, 2, U, P])
            pp = ps(c, "pp", [P, 2, U, D])
            oh_made = sem("oh_made")
            summed = sem("summed")
            load(l_sb[:], lst.rearrange("(p c) w -> p c w", p=P))
            load(tl[:], tile_of)
            loads_done(DVE)
            got, slot_free = gathers(tag, table, lst, nch, D)
            flat = acc[:].rearrange("p t d -> p (t d)")

            def begin(i, s):
                V.run(onehots(oh[:, s % 2], l_sb[:, bass.ds((i * RING + s) * U, U), 1:2].bitcast(F32)))
                DVE.sem_inc(oh_made, 1)
                take(PE, oh_made)
                PE.wait_ge(got[s], i * (16 * U) + 16 * U)
                for u in range(U):
                    mm = PE.matmul(pp[:, s % 2, u, :], oh[:, s % 2, u, :], row_slot[:, s, u, :], start=True, stop=True)
                mm.then_inc(summed, 1)

            def end(i, s):
                offsets = tile_offsets(tl, (i * RING + s) * U, U, (NT - 1) * D)
                take(DVE, summed)
                DVE.sem_inc(slot_free[s], 1)
                for u in range(U):
                    at = flat[:, bass.ds(offsets[u], D)]
                    V.run(DVE.tensor_tensor(at, at, pp[:, s % 2, u, :], ALU.add))
            ring_loop(nch, begin, end)
            barrier()

    def norm_stats():
        with ExitStack() as c:
            st = sb(c, "st", [P, NT, 6])
            tmp = sb(c, "tmp", [P, NT])
            V.reset()
            with DVE.Fori(0, NT) as t:
                V.run(DVE.bn_stats(st[:, bass.ds(t, 1), :], x_all[:, bass.ds(t, 1), :]))
                V.reset()
            V.go(DVE.tensor_tensor(mean[:], st[:, :, 1], st[:, :, 4], ALU.add))
            V.go(DVE.tensor_tensor(tmp[:], st[:, :, 1], st[:, :, 4], ALU.subtract))
            V.go(DVE.tensor_tensor(var[:], st[:, :, 2], st[:, :, 5], ALU.add))
            V.sync()
            V.go(DVE.tensor_scalar(mean[:], mean[:], 0.5, None, ALU.mult))
            V.run(DVE.tensor_tensor(tmp[:], tmp[:], tmp[:], ALU.mult))
            V.go(DVE.tensor_scalar(tmp[:], tmp[:], 0.25, None, ALU.mult))
            V.run(DVE.tensor_scalar(var[:], var[:], 1.0 / D, None, ALU.mult))
            V.run(DVE.tensor_tensor(var[:], var[:], tmp[:], ALU.add))
            V.run(DVE.tensor_scalar(rstd[:], var[:], LN_EPS, None, ALU.add))
            tell("v", "a")
            hear("v", "a")
            S.run(ACTE.activation(rstd[:], rstd[:], ACT.Sqrt))
            tell("a", "v")
            hear("a", "v")
            V.run(DVE.reciprocal(rstd[:], rstd[:]))
            barrier()

    def one(x, t):
        return x[:, t:t + 1] if isinstance(t, int) else x[:, bass.ds(t, 1)]

    def row(x, t):
        return x[:, t, :] if isinstance(t, int) else x[:, bass.ds(t, 1), :]

    def normalize(dst, t, scale=None):
        return DVE.tensor_scalar(dst, row(x_all, t), one(mean, t), one(rstd, t), ALU.subtract, ALU.mult)

    def transpose(dst_ps, src, blocks):
        for k in range(blocks):
            last = PE.transpose(dst_ps[:, k * P:(k + 1) * P], src[:, k * P:(k + 1) * P], ident[:])
        return last

    def broadcast_row(dst, src, width):
        load(dst, src.broadcast_to([P, width]))

    def tile_rows(x):
        return x.rearrange("(t p) d -> p t d", p=P)

    def gcn0_project(acc, z_scale, cov, zmean):
        with ExitStack() as c:
            w0t = sb(c, "w0t", [P, 2, D])
            xn = sb(c, "xn", [P, 4, D])
            z = sb(c, "z", [P, 4, D + 1])
            xnt = sb(c, "xnt", [P, 4, D])
            ps_xh = ps(c, "ps_xh", [P, 4, 512])
            ps_x, ps_h = ps_xh[:, :, 0:D], ps_xh[:, :, D:2 * D]
            gram = ps(c, "gram", [P, 2, 512])
            tmp = sb(c, "tmp", [P, NT])
            tm2 = sb(c, "tm2", [P, NT])
            nrm = sb(c, "nrm", [P, NT])
            msk = sb(c, "msk", [P, NT])
            load(w0t[:], a["w0t"].rearrange("(k p) d -> p k d", p=P))
            loads_done(PE)
            tell("v", "a"); hear("v", "a")
            S.run(ACTE.activation(nrm[:], var[:], ACT.Sqrt, scale=float(D)))
            tell("a", "v"); hear("a", "v")
            V.run(DVE.tensor_tensor(nrm[:], nrm[:], rstd[:], ALU.mult))
            V.go(DVE.tensor_scalar(msk[:], nrm[:], MAXNORM, None, ALU.is_gt))
            V.go(DVE.tensor_scalar(tmp[:], nrm[:], MAXNORM, None, ALU.min))
            V.run(DVE.tensor_scalar(nrm[:], nrm[:], MIN_NORM, None, ALU.max))
            V.go(DVE.tensor_scalar(tm2[:], tmp[:], -1.0, 1.0, ALU.mult, ALU.add))
            V.run(DVE.tensor_scalar(tmp[:], tmp[:], 1.0, None, ALU.add))
            V.run(DVE.reciprocal(tm2[:], tm2[:]))
            V.run(DVE.tensor_tensor(tmp[:], tmp[:], tm2[:], ALU.mult))
            tell("v", "a"); hear("v", "a")
            S.run(ACTE.activation(tmp[:], tmp[:], ACT.Ln))
            tell("a", "v"); hear("a", "v")
            V.run(DVE.tensor_scalar(tmp[:], tmp[:], 0.5, None, ALU.mult))
            V.go(DVE.tensor_scalar(tm2[:], msk[:], ATANH_MAX, None, ALU.mult))
            V.run(DVE.tensor_scalar(msk[:], msk[:], -1.0, 1.0, ALU.mult, ALU.add))
            V.run(DVE.tensor_tensor(tmp[:], tmp[:], msk[:], ALU.mult))
            V.run(DVE.tensor_tensor(tmp[:], tmp[:], tm2[:], ALU.add))
            V.run(DVE.reciprocal(nrm[:], nrm[:]))
            V.run(DVE.tensor_tensor(z_scale[:], tmp[:], nrm[:], ALU.mult))
            V.run(DVE.memset(z[:, :, D:D + 1], 1.0))
            for k in range(2):
                PE.matmul(gram[:, k, 0:D + 1], zeros[:], zwide[:, 0:D + 1], start=True, stop=False)

            def normalized(t, s):
                V.run(normalize(xn[:, s, :], t))
                V.run(DVE.tensor_scalar(z[:, s, 0:D], xn[:, s, :], one(z_scale, t), None, ALU.mult))
                tell("v", "p")

            def turned(t, s):
                hear("v", "p")
                transpose(ps_x[:, s], xn[:, s], 2).then_inc(links["p", "a"], 1)
                for k in range(2):
                    PE.matmul(gram[:, k, 0:D + 1], z[:, s, k * P:(k + 1) * P], z[:, s, :], start=False, stop=False)

            def copied(t, s):
                hear("p", "a")
                S.run(ACTE.activation(xnt[:, s, :], ps_x[:, s, 0:D], ACT.Copy))
                tell("a", "p")

            def multiplied(t, s):
                hear("a", "p")
                for k in range(2):
                    mm = PE.matmul(ps_h[:, s, 0:D], xnt[:, s, k * P:(k + 1) * P], w0t[:, k, :], start=(k == 0), stop=(k == 1))
                mm.then_inc(links["p", "v"], 1)

            def kept(t, s):
                hear("p", "v")
                V.run(DVE.tensor_copy(row(acc, t), ps_h[:, s, 0:D]))
            tiles((normalized, turned, copied, multiplied, kept), 4)
            for k in range(2):
                mm = PE.matmul(gram[:, k, 0:D + 1], zeros[:], zwide[:], start=False, stop=True)
            mm.then_inc(links["p", "v"], 1)
            hear("p", "v")
            mr = sb(c, "mr", [P, 2, D])
            dm = sb(c, "dm", [P, 2, P])
            for k in range(2):
                V.run(DVE.tensor_scalar(zmean[:, k, :], gram[:, k, D:D + 1], 1.0 / N, None, ALU.mult))
                V.run(DVE.tensor_scalar(dm[:, k, :], ident[:], zmean[:, k, 0:1], None, ALU.mult))
                V.run(DVE.tensor_scalar(cov[:, k, :], gram[:, k, 0:D], 1.0 / N, None, ALU.mult))
            tell("v", "p"); hear("v", "p")
            for k in range(2):
                mm = PE.matmul(ps_h[:, 0, k * P:(k + 1) * P], ones[:], dm[:, k, :], start=True, stop=True)
            mm.then_inc(links["p", "v"], 1)
            hear("p", "v")
            for k in range(2):
                V.run(DVE.tensor_scalar(mr[:, k, :], ps_h[:, 0, 0:D], zmean[:, k, 0:1], None, ALU.mult))
                V.run(DVE.tensor_tensor(cov[:, k, :], cov[:, k, :], mr[:, k, :], ALU.subtract))
            barrier()

    def scaled_table(acc, deg, table):
        V.reset()
        with DVE.Fori(0, NT) as t:
            V.run(DVE.tensor_scalar(row(acc, t), row(acc, t), one(deg, t), None, ALU.mult))
            V.reset()
        tell("v", "a"); hear("v", "a")
        load(tile_rows(table), acc[:])
        loads_done(ACTE)

    C3 = 768

    def mix0(z_scale, cov, zmean):
        M = 4
        with ExitStack() as c:
            wq = sb(c, "wq", [P, 2, C3])
            vec = sb(c, "vec", [P, C3])
            bias = sb(c, "bias", [P, C3])
            prod = sb(c, "prod", [P, 2, C3])
            mb = sb(c, "mb", [P, 2, P])
            pw = sb(c, "pw", [P, 6, P])
            dw = sb(c, "dw", [P, 6])
            rest = sb(c, "rest", [P, 4, D])
            bres = sb(c, "bres", [P, D])
            xn = sb(c, "xn", [P, M, D])
            zt = sb(c, "zt", [P, M, D])
            y = sb(c, "y", [P, M, 2 * C3])
            rt = sb(c, "rt", [P, M, C3])
            sq = sb(c, "sq", [P, C3])
            vv = sb(c, "vv", [P, M, 16, 32])
            dots = sb(c, "dots", [P, M, 16])
            den = rt[:, :, 0:512].rearrange("p m (g j) -> p m g j", g=16)
            o = vv[:].rearrange("p m g j -> p m (g j)")
            ot = rt
            ft = xn
            nn = sb(c, "nn", [P, M, 12])
            banks = ps(c, "banks", [P, M, 2, 512])
            ps_a, ps_b, ps_c = banks[:, 0], banks[:, 1], banks[:, 2]
            V.run(DVE.memset(pw[:], 0.0))
            tell("v", "a"); hear("v", "a")
            load(wq[:], a["qkvt"].rearrange("(k p) d -> p k d", p=P))
            load(dw[:], a["dw"])
            for g in range(4):
                load(pw[32 * g:32 * g + 32, :, 32 * g:32 * g + 32],
                     a["pwt"].rearrange("(b g) i o -> g i b o", g=4)[g])
            load(rest[:], a["rest"].rearrange("(k p) d -> p k d", p=P))
            broadcast_row(bres[:], a["bres"], D)
            broadcast_row(vec[:], a["gamma"], C3)
            broadcast_row(bias[:], a["beta"], C3)
            loads_done(DVE, PE)
            for b in range(6):
                V.go(DVE.tensor_scalar(pw[:, b, :], pw[:, b, :], dw[:, b:b + 1], None, ALU.mult))
            for k in range(2):
                V.go(DVE.tensor_scalar(mb[:, k, :], ones[:], zmean[:, k, 0:1], None, ALU.mult))
            V.sync()
            tell("v", "p"); hear("v", "p")
            H = C3 // 2
            for m in range(2):
                for h in range(2):
                    for k in range(2):
                        mm = PE.matmul((ps_a if m == 0 else ps_b)[:, h, 0:H], cov[:, k, m * P:(m + 1) * P],
                                       wq[:, k, h * H:(h + 1) * H], start=(k == 0), stop=(k == 1))
            for h in range(2):
                for k in range(2):
                    mm = PE.matmul(ps_c[:, h, 0:H], mb[:, k, :], wq[:, k, h * H:(h + 1) * H],
                                   start=(k == 0), stop=(k == 1))
            mm.then_inc(links["p", "v"], 1)
            hear("p", "v")
            for m in range(2):
                V.go(DVE.tensor_tensor(prod[:, m, :].rearrange("p (h w) -> p h w", h=2), (ps_a if m == 0 else ps_b)[:, :, 0:H],
                                       wq[:, m, :].rearrange("p (h w) -> p h w", h=2), ALU.mult))
            V.sync()
            tell("v", "p"); hear("v", "p")
            for h in range(2):
                for m in range(2):
                    mm = PE.matmul(ps_a[:, h, 0:H], ones[:], prod[:, m, h * H:(h + 1) * H], start=(m == 0), stop=(m == 1))
            mm.then_inc(links["p", "v"], 1)
            hear("p", "v")
            var_row = prod[:, 0, :].rearrange("p (h w) -> p h w", h=2)
            V.run(DVE.tensor_scalar(var_row, ps_a[:, :, 0:H], 0.0, LN_EPS, ALU.max, ALU.add))
            tell("v", "a"); hear("v", "a")
            S.run(ACTE.activation(prod[:, 0, :], prod[:, 0, :], ACT.Sqrt))
            tell("a", "v"); hear("a", "v")
            V.run(DVE.reciprocal(prod[:, 0, :], prod[:, 0, :]))
            V.run(DVE.tensor_tensor(vec[:], vec[:], prod[:, 0, :], ALU.mult))
            V.run(DVE.tensor_tensor(prod[:, 1, :].rearrange("p (h w) -> p h w", h=2), ps_c[:, :, 0:H],
                                    vec[:].rearrange("p (h w) -> p h w", h=2), ALU.mult))
            V.go(DVE.tensor_tensor(bias[:], bias[:], prod[:, 1, :], ALU.subtract))
            for k in range(2):
                V.go(DVE.tensor_tensor(wq[:, k, :], wq[:, k, :], vec[:], ALU.mult))
            V.sync()
            ys = [y[:, s, :] for s in range(M)]
            qkvs = [y[:, s, :].rearrange("p (g s j) -> p g s j", g=16, s=3) for s in range(M)]

            def two(x):
                return x.rearrange("p (h w) -> p h w", h=2)

            def n_(s, q):
                return nn[:, s, q:q + 1]

            def z_row(t, s):
                V.run(normalize(xn[:, s, :], t))
                V.run(DVE.tensor_scalar(xn[:, s, :], xn[:, s, :], one(z_scale, t), None, ALU.mult))
                tell("v", "p")

            def z_turned(t, s):
                hear("v", "p")
                transpose(banks[:, s, 0], xn[:, s], 2).then_inc(links["p", "a"], 1)

            def z_copied(t, s):
                hear("p", "a")
                S.run(ACTE.activation(zt[:, s, :], banks[:, s, 0, 0:D], ACT.Copy))
                tell("a", "p")

            def projected(t, s):
                hear("a", "p")
                for h in range(2):
                    for k in range(2):
                        mm = PE.matmul(banks[:, s, h, 0:H], zt[:, s, k * P:(k + 1) * P], wq[:, k, h * H:(h + 1) * H],
                                       start=(k == 0), stop=(k == 1))
                mm.then_inc(links["p", "v"], 1)

            def relued(t, s):
                hear("p", "v")
                r = ys[s][:, 0:C3]
                V.run(DVE.tensor_tensor(two(r), banks[:, s, :, 0:H], two(bias[:]), ALU.add))
                V.run(DVE.tensor_scalar(r, r, 0.0, None, ALU.max))
                tell("v", "p")
                tell("v", "a")

            def r_turned(t, s):
                hear("v", "p")
                for b in range(6):
                    tr = PE.transpose(banks[:, s, b // 4, (b % 4) * P:(b % 4 + 1) * P], ys[s][:, b * P:(b + 1) * P], ident[:])
                tr.then_inc(links["p", "a"], 1)

            def r_copied(t, s):
                hear("v", "a")
                S.run(ACTE.activation(sq[:], ys[s][:, 0:C3], ACT.Square, accum_out=n_(s, 0)))
                hear("p", "a")
                S.go(ACTE.activation(rt[:, s, 0:512], banks[:, s, 0, :], ACT.Copy))
                S.run(ACTE.activation(rt[:, s, 512:C3], banks[:, s, 1, 0:256], ACT.Copy))
                tell("a", "p")

            def grouped(t, s):
                hear("a", "p")
                for b in range(6):
                    mm = PE.matmul(banks[:, s, b // 4, (b % 4) * P:(b % 4 + 1) * P], rt[:, s, b * P:(b + 1) * P], pw[:, b, :],
                                   start=True, stop=True)
                mm.then_inc(links["p", "a"], 1)

            def s_copied(t, s):
                hear("p", "a")
                S.go(ACTE.activation(ys[s][:, C3:C3 + 512], banks[:, s, 0, :], ACT.Copy))
                S.run(ACTE.activation(ys[s][:, C3 + 512:2 * C3], banks[:, s, 1, 0:256], ACT.Copy))
                tell("a", "v")
                S.run(ACTE.activation(sq[:], ys[s][:, C3:2 * C3], ACT.Square, accum_out=n_(s, 1)))
                S.run(ACTE.activation(n_(s, 3), n_(s, 0), ACT.Sqrt, bias=n_(s, 1)))
                tell("a", "v")

            def attended(t, s):
                hear("a", "v")
                qkv = qkvs[s]
                V.run(DVE.tensor_scalar(vv[:, s], qkv[:, :, 1, :], 0.0, None, ALU.max))
                V.run(DVE.tensor_reduce(dots[:, s, :], vv[:, s], AX.X, ALU.add))
                hear("a", "v")
                V.run(DVE.tensor_scalar(n_(s, 3), n_(s, 3), MIN_NORM, None, ALU.max))
                V.run(DVE.reciprocal(n_(s, 3), n_(s, 3)))
                V.run(DVE.tensor_scalar(n_(s, 3), n_(s, 3), ATANH_MAX, 1.0, ALU.mult, ALU.min))
                V.go(DVE.tensor_scalar(dots[:, s, :], dots[:, s, :], n_(s, 3), n_(s, 3), ALU.mult, ALU.mult))
                V.go(DVE.tensor_scalar(vv[:, s], qkv[:, :, 2, :], n_(s, 3), None, ALU.mult))
                V.run(DVE.tensor_scalar(den[:, s], qkv[:, :, 2, :], n_(s, 3), 1e-15, ALU.mult, ALU.add))
                V.go(DVE.reciprocal(den[:, s], den[:, s]))
                V.run(DVE.scalar_tensor_tensor(vv[:, s], qkv[:, :, 0, :], 0.0, vv[:, s], ALU.max, ALU.mult))
                V.run(DVE.tensor_tensor(vv[:, s], vv[:, s], dots[:, s, :].unsqueeze(2).broadcast_to([P, 16, 32]), ALU.mult))
                V.run(DVE.tensor_tensor(o[:, s, :].rearrange("p (g j) -> p g j", g=16), vv[:, s], den[:, s], ALU.mult))
                tell("v", "p")
                tell("v", "a")

            def o_turned(t, s):
                hear("v", "p")
                transpose(banks[:, s, 0], o[:, s], 4).then_inc(links["p", "a"], 1)

            def o_copied(t, s):
                hear("v", "a")
                S.run(ACTE.activation(sq[:, 0:512], o[:, s, :], ACT.Square, accum_out=n_(s, 4)))
                hear("p", "a")
                S.run(ACTE.activation(ot[:, s, 0:512], banks[:, s, 0, :], ACT.Copy))
                tell("a", "p")
                S.run(ACTE.activation(n_(s, 5), n_(s, 4), ACT.Sqrt))
                tell("a", "v")

            def o_projected(t, s):
                hear("a", "p")
                for k in range(4):
                    mm = PE.matmul(banks[:, s, 1, 0:D], ot[:, s, k * P:(k + 1) * P], rest[:, k, :], start=(k == 0), stop=(k == 3))
                mm.then_inc(links["p", "v"], 1)

            def ft_made(t, s):
                hear("a", "v")
                V.run(DVE.tensor_scalar(n_(s, 5), n_(s, 5), MIN_NORM, None, ALU.max))
                V.run(DVE.reciprocal(n_(s, 5), n_(s, 5)))
                V.run(DVE.tensor_scalar(n_(s, 5), n_(s, 5), ATANH_MAX, 1.0, ALU.mult, ALU.min))
                hear("p", "v")
                V.run(DVE.scalar_tensor_tensor(ft[:, s, :], banks[:, s, 1, 0:D], n_(s, 5), bres[:], ALU.mult, ALU.add))
                tell("v", "a")

            def ft_normed(t, s):
                hear("v", "a")
                S.run(ACTE.activation(sq[:, 0:D], ft[:, s, :], ACT.Square, accum_out=n_(s, 6)))
                S.run(ACTE.activation(n_(s, 7), n_(s, 6), ACT.Sqrt))

            def ft_tanh(t, s):
                S.run(ACTE.activation(n_(s, 8), n_(s, 7), ACT.Tanh))
                tell("a", "v")

            def added(t, s):
                hear("a", "v")
                V.go(DVE.tensor_scalar(n_(s, 8), n_(s, 8), MAXNORM, None, ALU.min))
                V.run(DVE.tensor_scalar(n_(s, 7), n_(s, 7), MIN_NORM, None, ALU.max))
                V.run(DVE.reciprocal(n_(s, 7), n_(s, 7)))
                V.run(DVE.tensor_tensor(n_(s, 9), n_(s, 7), n_(s, 8), ALU.mult))
                V.run(DVE.scalar_tensor_tensor(row(x_all, t), ft[:, s, :], n_(s, 9), row(x_all, t), ALU.mult, ALU.add))
            tiles((z_row, z_turned, z_copied, projected, relued, r_turned, r_copied, grouped, s_copied, attended,
                   o_turned, o_copied, o_projected, ft_made, ft_normed, ft_tanh, added), M)
            barrier()

    def add_scaled(acc, deg):
        with DVE.Fori(0, NT) as t:
            V.run(DVE.scalar_tensor_tensor(row(x_all, t), row(acc, t), one(deg, t), row(x_all, t), ALU.mult, ALU.add))
            V.reset()

    GH = 4
    TW = 20

    def leaky(dst, src):
        return DVE.scalar_tensor_tensor(dst, src, 0.2, src, ALU.mult, ALU.max)

    def gat_scores(lst, list_done, tile_of, nch, gate):
        with ExitStack() as c:
            wg = sb(c, "wg", [P, 2, 16])
            att = sb(c, "att", [P, 2, 16])
            bg = sb(c, "bg", [P, 3, 16])
            node = sb(c, "node", [P, NT, TW])
            pr = sb(c, "pr", [P, NT, 16])
            dm = sb(c, "dm", [P, 2, NT * GH])
            top = sb(c, "topv", [P, NT, GH])
            least = sb(c, "least", [P, 1])
            shift = sb(c, "shift", [P, 1])
            sums = sb(c, "sums", [P, 5, NT * GH])
            rows_all = sb(c, "rows_all", [P, nch, TW])
            low = sb(c, "low", [P, nch], BF16)
            tl = sb(c, "tl", [1, nch], I32)
            load(wg[:], a["wgat"].rearrange("(k p) d -> p k d", p=P))
            broadcast_row(att[:, 0, :], a["att_src"], 16)
            broadcast_row(att[:, 1, :], a["att_dst"], 16)
            for q, n in enumerate(("bgat", "lng", "lnb")):
                broadcast_row(bg[:, q, :], a[n], 16)
            list_done(ACTE)
            load(tl[:], tile_of)
            table = dram("gat_table", [NP, TW])
            with ExitStack() as d:
                l_sb = sb(d, "l_sb", [P, nch, 2], I32)
                load(l_sb[:], lst.rearrange("(p c) w -> p c w", p=P))
                loads_done(DVE, PE, ACTE)
                V.go(DVE.tensor_copy(low[:], l_sb[:, :, 1].bitcast(F32)))
                xn = sb(d, "xn", [P, 4, D])
                xnt = sb(d, "xnt", [P, 4, D])
                ps_x = ps(d, "ps_x", [P, 4, 512])
                ps_h = ps(d, "ps_h", [P, 4, 512])

                def normalized(t, s):
                    V.run(normalize(xn[:, s, :], t))
                    tell("v", "p")

                def turned(t, s):
                    hear("v", "p")
                    transpose(ps_x[:, s], xn[:, s], 2).then_inc(links["p", "a"], 1)

                def copied(t, s):
                    hear("p", "a")
                    S.run(ACTE.activation(xnt[:, s, :], ps_x[:, s, 0:D], ACT.Copy))
                    tell("a", "p")

                def multiplied(t, s):
                    hear("a", "p")
                    for k in range(2):
                        mm = PE.matmul(ps_h[:, s, 0:16], xnt[:, s, k * P:(k + 1) * P], wg[:, k, :], start=(k == 0), stop=(k == 1))
                    mm.then_inc(links["p", "v"], 1)

                def kept(t, s):
                    hear("p", "v")
                    at = node[:, t, 0:16] if isinstance(t, int) else node[:, bass.ds(t, 1), 0:16]
                    V.run(DVE.tensor_copy(at, ps_h[:, s, 0:16]))
                tiles((normalized, turned, copied, multiplied, kept), 4)
                tgt_logit = dm[:, 0, :].rearrange("p (t h) -> p t h", h=GH)
                for q, dst in enumerate((node[:, :, 16:20], tgt_logit)):
                    V.run(DVE.tensor_tensor(pr[:], node[:, :, 0:16], att[:, q, :].unsqueeze(1).broadcast_to([P, NT, 16]), ALU.mult))
                    V.run(DVE.tensor_reduce(dst, pr[:].rearrange("p t (h j) -> p t h j", h=GH), AX.X, ALU.add))
                V.run(DVE.tensor_reduce(least[:], node[:, :, 16:20], AX.XY, ALU.min))
                tell("v", "p"); hear("v", "p")
                PE.transpose(ps_x[0:1, 0, 0:P], least[:], ident[:]).then_inc(links["p", "v"], 1)
                hear("p", "v")
                V.run(DVE.tensor_reduce(least[0:1, :], ps_x[0:1, 0, 0:P], AX.X, ALU.min))
                tell("v", "p"); hear("v", "p")
                PE.matmul(ps_h[:, 0, 0:1], ones[0:1, :], least[0:1, :], start=True, stop=True).then_inc(links["p", "v"], 1)
                hear("p", "v")
                V.run(DVE.tensor_scalar(shift[:], ps_h[:, 0, 0:1], -1.0, 1.0, ALU.mult, ALU.add))
                V.run(DVE.tensor_scalar(top[:], node[:, :, 16:20], shift[:, 0:1], None, ALU.add))
                tell("v", "a"); hear("v", "a")
                load(tile_rows(table), node[:])
                loads_done(ACTE)
                barrier()
            with ExitStack() as d:
                oh = sb(d, "oh", [P, RING, U, P])
                sv = sb(d, "sv", [P, RING, U, GH])
                diag = sb(d, "diag", [P, 2, U, GH, P])
                mx = sb(d, "mx", [P, U, GH])
                pp = ps(d, "pp", [P, 2, U, 512])
                sv_made = sem("gat_sv_made")
                diag_free = sem("gat_diag_free")
                diag_made = sem("gat_diag_made")
                banks_free = sem("gat_banks_free")
                summed = sem("gat_summed")
                got, slot_free = gathers("gat", table, lst, nch, TW)
                top_odd = sb(d, "top_odd", [P, NT, GH])
                V.run(DVE.tensor_copy(top_odd[:], top[:]))
                flat_top = [x[:].rearrange("p t h -> p (t h)") for x in (top, top_odd)]
                ACTE.sem_inc(diag_free, 2)
                PE.sem_inc(banks_free, 2)

                def begin(i, s):
                    first = (i * RING + s) * U
                    V.go(onehots(oh[:, s], low[:, bass.ds(first, U)].unsqueeze(2)))
                    DVE.wait_ge(got[s], i * (16 * U) + 16 * U)
                    V.run(DVE.tensor_scalar(sv[:, s], row_slot[:, s, :, 16:20], shift[:, 0:1], None, ALU.add))
                    DVE.sem_inc(sv_made, 1)
                    V.run(DVE.tensor_copy(rows_all[:, bass.ds(first, U), 0:TW], row_slot[:, s, :, 0:TW]))
                    DVE.sem_inc(slot_free[s], 1)
                    take(ACTE, sv_made)
                    take(ACTE, diag_free)
                    for u in range(U):
                        for h in range(GH):
                            S.go(ACTE.activation(diag[:, s % 2, u, h, :], ident[:], ACT.Copy, scale=sv[:, s, u, h:h + 1]))
                    S.sync()
                    ACTE.sem_inc(diag_made, 1)
                    take(PE, diag_made)
                    take(PE, banks_free)
                    for u in range(U):
                        mm = PE.matmul(pp[:, s % 2, u, :], oh[:, s, u, :], diag[:, s % 2, u].rearrange("p h j -> p (h j)"),
                                       start=True, stop=True)
                    mm.then_inc(summed, 1)

                def end(i, s):
                    offsets = tile_offsets(tl, (i * RING + s) * U, U, (NT - 1) * GH)
                    take(DVE, summed)
                    DVE.sem_inc(diag_free, 1)
                    V.run(DVE.tensor_reduce(mx[:], pp[:, s % 2].rearrange("p u (h j) -> p u h j", h=GH), AX.X, ALU.max))
                    DVE.sem_inc(banks_free, 1)
                    for u in range(U):
                        at = flat_top[u % 2][:, bass.ds(offsets[u], GH)]
                        V.go(DVE.tensor_tensor(at, at, mx[:, u, :], ALU.max))
                        if u % 2:
                            V.sync()
                ring_loop(nch, begin, end, behind=2)
                take(ACTE, diag_free, 2)
                take(PE, banks_free, 2)
                V.run(DVE.tensor_tensor(top[:], top[:], top_odd[:], ALU.max))
                barrier()
            sl = sb(c, "sl", [P, NT, GH])
            V.run(DVE.tensor_scalar(top[:], top[:], shift[:, 0:1], None, ALU.subtract))
            tgt_logit, top_logit = (dm[:, q, :].rearrange("p (t h) -> p t h", h=GH) for q in range(2))
            V.run(DVE.tensor_tensor(top[:], top[:], tgt_logit, ALU.add))
            V.run(leaky(top_logit, top[:]))
            V.run(DVE.tensor_tensor(sl[:], node[:, :, 16:20], tgt_logit, ALU.add))
            V.run(leaky(top[:], sl[:]))
            V.run(DVE.tensor_tensor(top[:], top[:], top_logit, ALU.subtract))
            V.run(DVE.tensor_scalar(top[:], top[:], 0.0, None, ALU.min))
            tell("v", "a"); hear("v", "a")
            weight = sums[:, 4, :].rearrange("p (t h) -> p t h", h=GH)
            S.run(ACTE.activation(weight, top[:], ACT.Exp))
            tell("a", "v"); hear("a", "v")
            for h in range(GH):
                V.run(DVE.tensor_tensor(sums[:, h, :].rearrange("p (t j) -> p t j", j=GH), node[:, :, GH * h:GH * h + GH],
                                        weight[:, :, h:h + 1].broadcast_to([P, NT, GH]), ALU.mult))
            W = 2 * U
            with ExitStack() as d:
                oh = sb(d, "oh", [P, 4, W, P], BF16)
                oht = sb(d, "oht", [P, 2, W, P], BF16)
                dm3 = sb(d, "dm3", [P, 6, NT * GH], BF16)
                dm_rest = sb(d, "dm_rest", [P, 2, NT * GH])
                tgt = sb(d, "tgt", [P, 2, W, 3, 8], BF16)
                back = sb(d, "back", [P, W, 8])
                msg3 = sb(d, "msg3", [P, 2, W, 3, TW], BF16)
                rest = sb(d, "rest", [P, W, TW])
                ident_b = sb(d, "ident_b", [P, P], BF16)
                lg = sb(d, "lg", [P, 2, W, GH])
                ex = sb(d, "ex", [P, W, GH])
                msg = sb(d, "msg", [P, 2, W, TW])
                ps_t = ps(d, "ps_t", [P, 2, 1024], BF16)
                ps_m = ps(d, "ps_m", [P, 2, 512])
                ps_s = ps(d, "ps_s", [P, 2, 512])
                V.go(DVE.tensor_copy(ident_b[:], ident[:]))
                V.run(DVE.tensor_copy(dm3[:, 0:2], dm[:]))
                V.run(DVE.tensor_tensor(dm_rest[:], dm[:], dm3[:, 0:2], ALU.subtract))
                V.run(DVE.tensor_copy(dm3[:, 2:4], dm_rest[:]))
                V.run(DVE.tensor_tensor(dm_rest[:], dm_rest[:], dm3[:, 2:4], ALU.subtract))
                V.run(DVE.tensor_copy(dm3[:, 4:6], dm_rest[:]))
                onehots_made = sem("gat2_onehots")
                turned = sem("gat2_turned")
                turned_copied = sem("gat2_turned_copied")
                targets = sem("gat2_targets")
                logits = sem("gat2_logits")
                weights = sem("gat2_weights")
                messages = sem("gat2_messages")
                products = sem("gat2_sums")
                sums_odd = node[:].rearrange("p t w -> p (t w)").rearrange("p (q x) -> p q x", q=5)
                V.run(DVE.memset(sums_odd, 0.0))
                both = (sums[:], sums_odd)

                def spread(g, s):
                    V.go(onehots(oh[:, s], low[:, bass.ds(g * W, W)].unsqueeze(2)))
                    offsets = tile_offsets(tl, g * W, W, (NT - 1) * GH)
                    for w in range(W):
                        V.go(DVE.tensor_copy(tgt[:, s % 2, w].rearrange("p k (a h) -> p (k a) h", a=2), dm3[:, :, bass.ds(offsets[w], GH)]))
                    V.sync()
                    DVE.sem_inc(onehots_made, 1)
                    take(PE, onehots_made)
                    for w in range(W):
                        tr = PE.transpose(ps_t[:, s % 2, w * P:(w + 1) * P], oh[:, s, w, :], ident_b[:])
                    tr.then_inc(turned, 1)
                    take(ACTE, turned)
                    S.run(ACTE.activation(oht[:, s % 2].rearrange("p w j -> p (w j)"), ps_t[:, s % 2], ACT.Copy))
                    ACTE.sem_inc(turned_copied, 1)
                    take(PE, turned_copied)
                    for w in range(W):
                        mm = PE.matmul(ps_m[:, s % 2, 24 * w:24 * w + 24], oht[:, s % 2, w, :], tgt[:, s % 2, w].rearrange("p k q -> p (k q)"),
                                       start=True, stop=True)
                    mm.then_inc(targets, 1)

                def weigh(g, s):
                    s %= 2
                    take(DVE, targets)
                    V.run(DVE.tensor_reduce(back[:], ps_m[:, s, 0:24 * W].rearrange("p (w k q) -> p w q k", k=3, q=8), AX.X, ALU.add))
                    V.run(DVE.tensor_tensor(lg[:, s], rows_all[:, bass.ds(g * W, W), 16:20], back[:, :, 0:4], ALU.add))
                    V.run(leaky(ex[:], lg[:, s]))
                    V.run(DVE.tensor_tensor(lg[:, s], ex[:], back[:, :, 4:8], ALU.subtract))
                    V.run(DVE.tensor_scalar(lg[:, s], lg[:, s], 0.0, None, ALU.min))
                    DVE.sem_inc(logits, 1)
                    take(ACTE, logits)
                    S.run(ACTE.activation(msg[:, s, :, 16:20], lg[:, s], ACT.Exp))
                    ACTE.sem_inc(weights, 1)

                def multiply(g, s):
                    take(DVE, weights)
                    for h in range(GH):
                        V.go(DVE.tensor_tensor(msg[:, s % 2, :, 4 * h:4 * h + 4], rows_all[:, bass.ds(g * W, W), 4 * h:4 * h + 4],
                                               msg[:, s % 2, :, 16 + h:17 + h].broadcast_to([P, W, GH]), ALU.mult))
                    V.sync()
                    V.run(DVE.tensor_copy(msg3[:, s % 2, :, 0, :], msg[:, s % 2]))
                    V.run(DVE.tensor_tensor(rest[:], msg[:, s % 2], msg3[:, s % 2, :, 0, :], ALU.subtract))
                    V.run(DVE.tensor_copy(msg3[:, s % 2, :, 1, :], rest[:]))
                    V.run(DVE.tensor_tensor(msg3[:, s % 2, :, 2, :], rest[:], msg3[:, s % 2, :, 1, :], ALU.subtract))
                    DVE.sem_inc(messages, 1)
                    take(PE, messages)
                    for w in range(W):
                        for k in range(3):
                            mm = PE.matmul(ps_s[:, s % 2, 32 * w:32 * w + TW], oh[:, s, w, :], msg3[:, s % 2, w, k, :],
                                           start=(k == 0), stop=(k == 2))
                    mm.then_inc(products, 1)

                def add(g, s):
                    offsets = tile_offsets(tl, g * W, W, (NT - 1) * GH)
                    take(DVE, products)
                    for w in range(W):
                        at = both[w % 2][:, :, bass.ds(offsets[w], GH)]
                        V.go(DVE.tensor_tensor(at, at, ps_s[:, s % 2, 32 * w:32 * w + TW].rearrange("p (q h) -> p q h", h=GH), ALU.add))
                        if w % 2:
                            V.sync()

                groups = nch // W
                begun = 2 + (groups - 2) % 4
                S.reset(); V.reset()
                spread(0, 0)
                for g in range(1, begun):
                    spread(g, g % 4)
                    weigh(g - 1, (g - 1) % 4)
                    if g > 1:
                        add(g - 2, (g - 2) % 4)
                    multiply(g - 1, (g - 1) % 4)
                S.reset(); V.reset()
                with nc.Fori(0, (groups - begun) // 4) as i:
                    for j in range(4):
                        g = i * 4 + (begun + j)
                        spread(g, (begun + j) % 4)
                        weigh(g - 1, (begun + j - 1) % 4)
                        add(g - 2, (begun + j - 2) % 4)
                        multiply(g - 1, (begun + j - 1) % 4)
                    S.reset(); V.reset()
                weigh(groups - 1, (groups - 1) % 4)
                add(groups - 2, (groups - 2) % 4)
                multiply(groups - 1, (groups - 1) % 4)
                add(groups - 1, (groups - 1) % 4)
                V.run(DVE.tensor_tensor(sums[:], sums[:], sums_odd, ALU.add))
                barrier()
            den = sb(c, "den", [P, NT, GH])
            sc = sb(c, "sc", [P, NT, GH])
            m1 = sb(c, "m1", [P, NT])
            v1 = sb(c, "v1", [P, NT])

            def over_nodes(q):
                return bg[:, q, :].unsqueeze(1).broadcast_to([P, NT, 16])

            def per_node(x):
                return x[:].unsqueeze(2).broadcast_to([P, NT, 16])
            V.run(DVE.tensor_scalar(den[:], weight, 1e-16, None, ALU.add))
            V.run(DVE.reciprocal(den[:], den[:]))
            for h in range(GH):
                V.run(DVE.tensor_tensor(pr[:, :, GH * h:GH * h + GH], sums[:, h, :].rearrange("p (t j) -> p t j", j=GH),
                                        den[:, :, h:h + 1].broadcast_to([P, NT, GH]), ALU.mult))
            V.run(DVE.tensor_tensor(pr[:], pr[:], over_nodes(0), ALU.add))
            V.run(DVE.tensor_reduce(m1[:], pr[:], AX.X, ALU.add))
            V.run(DVE.tensor_scalar(m1[:], m1[:], 1.0 / 16, None, ALU.mult))
            V.run(DVE.tensor_tensor(pr[:], pr[:], per_node(m1), ALU.subtract))
            V.run(DVE.tensor_tensor(node[:, :, 0:16], pr[:], pr[:], ALU.mult))
            V.run(DVE.tensor_reduce(v1[:], node[:, :, 0:16], AX.X, ALU.add))
            V.run(DVE.tensor_scalar(v1[:], v1[:], 1.0 / 16, LN_EPS, ALU.mult, ALU.add))
            tell("v", "a"); hear("v", "a")
            S.run(ACTE.activation(v1[:], v1[:], ACT.Sqrt))
            tell("a", "v"); hear("a", "v")
            V.run(DVE.reciprocal(v1[:], v1[:]))
            V.run(DVE.tensor_tensor(pr[:], pr[:], per_node(v1), ALU.mult))
            V.run(DVE.tensor_tensor(pr[:], pr[:], over_nodes(1), ALU.mult))
            V.run(DVE.tensor_tensor(pr[:], pr[:], over_nodes(2), ALU.add))
            V.run(DVE.tensor_reduce(sc[:], pr[:].rearrange("p t (h j) -> p t j h", h=GH), AX.X, ALU.add))
            V.run(DVE.tensor_scalar(sc[:], sc[:], 1.0 / GH, None, ALU.mult))
            top2(sc, gate, GH)
            barrier()

    def top2(sc, gate, n):
        with ExitStack() as c:
            earlier = sb(c, "earlier", [P, n, n])
            gt = sb(c, "gt", [P, NT, n, n])
            eq = sb(c, "eq", [P, NT, n, n])
            rank = sb(c, "rank", [P, NT, n])
            m = sb(c, "m", [P, NT])
            full = [P, NT, n, n]
            mine, other = sc[:].unsqueeze(3).broadcast_to(full), sc[:].unsqueeze(2).broadcast_to(full)
            V.run(DVE.memset(earlier[:], 0.0))
            for e in range(1, n):
                V.go(DVE.memset(earlier[:, e, 0:e], 1.0))
            V.go(DVE.tensor_tensor(gt[:], other, mine, ALU.is_gt))
            V.run(DVE.tensor_tensor(eq[:], other, mine, ALU.is_equal))
            V.run(DVE.tensor_tensor(eq[:].rearrange("p t a b -> p t (a b)"), eq[:].rearrange("p t a b -> p t (a b)"),
                                    earlier[:].rearrange("p a b -> p (a b)").unsqueeze(1).broadcast_to([P, NT, n * n]), ALU.mult))
            V.run(DVE.tensor_tensor(gt[:], gt[:], eq[:], ALU.add))
            V.go(DVE.tensor_reduce(rank[:], gt[:], AX.X, ALU.add))
            V.run(DVE.tensor_reduce(m[:], sc[:], AX.X, ALU.max))
            V.go(DVE.tensor_scalar(rank[:], rank[:], 1.5, None, ALU.is_lt))
            V.run(DVE.tensor_tensor(gate[:], sc[:], m[:].unsqueeze(2).broadcast_to([P, NT, n]), ALU.subtract))
            tell("v", "a"); hear("v", "a")
            S.run(ACTE.activation(gate[:], gate[:], ACT.Exp))
            tell("a", "v"); hear("a", "v")
            V.run(DVE.tensor_tensor(gate[:], gate[:], rank[:], ALU.mult))
            V.run(DVE.tensor_reduce(m[:], gate[:], AX.X, ALU.add))
            V.run(DVE.reciprocal(m[:], m[:]))
            V.run(DVE.tensor_tensor(gate[:], gate[:], m[:].unsqueeze(2).broadcast_to([P, NT, n]), ALU.mult))

    def expert_weights(c, tag, n):
        w1 = sb(c, "w1", [P, n, 2, 512])
        w2 = sb(c, "w2", [P, n, 4, D])
        b1 = sb(c, "b1", [P, n, 4])
        b2 = sb(c, "b2", [P, n, D])
        weights_in = sem(f"weights_in_{tag}")
        for e in range(n):
            ACTE.dma_start(w1[:, e], a["w1_" + tag][e].rearrange("(k p) d -> p k d", p=P)).then_inc(weights_in, 16)
            ACTE.dma_start(w2[:, e], a["w2_" + tag][e].rearrange("(k p) d -> p k d", p=P)).then_inc(weights_in, 16)
            ACTE.dma_start(b2[:, e], a["b2_" + tag][e:e + 1, :].broadcast_to([P, D])).then_inc(weights_in, 16)
        ACTE.dma_start(b1[:], a["b1_" + tag]).then_inc(weights_in, 16)
        return w1, w2, b1, b2, weights_in

    def experts(tag, n, gate, rs, affine, weights):
        BT = 7
        HALF = BT * P // 2
        with ExitStack() as c:
            w1, w2, b1, b2, weights_in = weights
            xs = sb(c, "xs", [P, 2, D])
            xnt = sb(c, "xnt", [P, 2, 2, BT * P])
            ht = sb(c, "ht", [P, 2, 4, BT * P])
            ps_x = ps(c, "ps_x", [P, 2, 512])
            ps_h = ps(c, "ps_h", [P, 2, 2, 512])
            ps_y = ps(c, "ps_y", [P, 2, 512])
            x_made, x_turned, xs_free, px_free, xnt_full = (sem(f"{q}_{tag}") for q in
                                                           ("x_made", "x_turned", "xs_free", "px_free", "xnt_full"))
            h_full, h_free, ht_full, ht_free, y_full, y_free = (
                sem(f"{q}_{tag}") for q in ("h_full", "h_free", "ht_full", "ht_free", "y_full", "y_free"))
            for engine in (PE, ACTE, DVE):
                engine.wait_ge(weights_in, (3 * n + 1) * 16)
            PE.sem_inc(h_free, 2)
            PE.sem_inc(y_free, 2)
            PE.sem_inc(px_free, 2)
            ACTE.sem_inc(ht_free, 2)
            DVE.sem_inc(xs_free, 2)
            V.reset(); S.reset()

            def normalize_row(t, j, half):
                take(DVE, xs_free)
                V.run(DVE.tensor_scalar(xs[:, (half + j) % 2, :], row(x_all, t), one(mean, t), one(rs, t), ALU.subtract, ALU.mult))
                DVE.sem_inc(x_made, 1)

            def turn_row(j, half):
                take(PE, x_made)
                take(PE, px_free)
                transpose(ps_x[:, (half + j) % 2], xs[:, (half + j) % 2], 2).then_inc(x_turned, 1)
                take(ACTE, x_turned)
                for k in range(2):
                    src = ps_x[:, (half + j) % 2, k * P:(k + 1) * P]
                    if affine is None:
                        S.go(ACTE.activation(xnt[:, half, k, j * P:(j + 1) * P], src, ACT.Copy))
                    else:
                        S.go(ACTE.activation(xnt[:, half, k, j * P:(j + 1) * P], src, ACT.Identity,
                                             scale=affine[:, 0, k:k + 1], bias=affine[:, 1, k:k + 1]))
                S.sync()
                ACTE.sem_inc(px_free, 1)
                ACTE.sem_inc(xs_free, 1)
                if j == BT - 1:
                    ACTE.sem_inc(xnt_full, 1)

            def hidden(e, half):
                for hb in range(4):
                    take(PE, h_free)
                    for q in range(2):
                        for k in range(2):
                            mm = PE.matmul(ps_h[:, hb % 2, q, 0:HALF], w1[:, e, k, hb * P:(hb + 1) * P],
                                           xnt[:, half, k, q * HALF:(q + 1) * HALF], start=(k == 0), stop=(k == 1))
                    mm.then_inc(h_full, 1)
                    if hb == 0:
                        take(ACTE, ht_free)
                    take(ACTE, h_full)
                    S.run(ACTE.activation(ht[:, e % 2, hb, :].rearrange("p (h w) -> p h w", h=2), ps_h[:, hb % 2, :, 0:HALF],
                                          ACT.Gelu, bias=b1[:, e, hb:hb + 1]))
                    ACTE.sem_inc(h_free, 1)
                ACTE.sem_inc(ht_full, 1)

            def output(e, first):
                take(PE, ht_full)
                for j in range(BT):
                    if j % 2 == 0:
                        take(PE, y_free)
                    for hb in range(4):
                        mm = PE.matmul(ps_y[:, j // 2 % 2, (j % 2) * D:(j % 2 + 1) * D], ht[:, e % 2, hb, j * P:(j + 1) * P],
                                       w2[:, e, hb, :], start=(hb == 0), stop=(hb == 3))
                    if j % 2 == 1 or j == BT - 1:
                        mm.then_inc(y_full, 1)
                for j in range(BT):
                    t = first + j
                    if j % 2 == 0:
                        take(DVE, y_full)
                    V.run(DVE.scalar_tensor_tensor(row(x_all, t), ps_y[:, j // 2 % 2, (j % 2) * D:(j % 2 + 1) * D],
                                                   gate_of(t, e), row(x_all, t), ALU.mult, ALU.add))
                    if j % 2 == 1 or j == BT - 1:
                        DVE.sem_inc(y_free, 1)
                DVE.sem_inc(ht_free, 1)
                for j in range(BT):
                    t = first + j
                    V.go(DVE.scalar_tensor_tensor(row(x_all, t), b2[:, e, :], gate_of(t, e), row(x_all, t), ALU.mult, ALU.add))
                V.sync()

            def gate_of(t, e):
                return gate[:, t, e:e + 1] if isinstance(t, int) else gate[:, bass.ds(t, 1), e:e + 1]

            def block(first, half, more):
                per = -(-BT // n)
                take(PE, xnt_full)
                hidden(0, half)
                for e in range(n):
                    ahead = range(min(e * per, BT), min((e + 1) * per, BT)) if more else ()
                    for j in ahead:
                        normalize_row(first + (BT + j), j, 1 - half)
                    if e + 1 < n:
                        hidden(e + 1, half)
                    for j in ahead:
                        turn_row(j, 1 - half)
                    output(e, first)

            assert NT // BT % 2 == 1 and NT % BT == 0
            for j in range(BT):
                normalize_row(j, j, 0)
                turn_row(j, 0)
            V.reset(); S.reset()
            with nc.Fori(0, NT // BT // 2) as i:
                block(i * (2 * BT), 0, True)
                block(i * (2 * BT) + BT, 1, True)
                V.reset(); S.reset()
            block(NT - BT, 0, False)
            take(PE, h_free, 2)
            take(PE, y_free, 2)
            take(PE, px_free, 2)
            take(ACTE, ht_free, 2)
            take(DVE, xs_free, 2)
            barrier()

    HD = 64
    NH = 8

    def attention_matrix(mat):
        M = 3
        with ExitStack() as c:
            wkv = sb(c, "wkv", [P, 2, 2 * NH, HD])
            mu = sb(c, "mu", [P, 2, 2 * NH])
            wqn = sb(c, "wqn", [HD, NH, D])
            wo = sb(c, "wo", [HD, NH, D])
            xn = sb(c, "xn", [P, M, D])
            xnt = sb(c, "xnt", [P, M, D])
            kv = sb(c, "kv", [P, M, 2 * NH, HD])
            sq = sb(c, "sq", [P, 2 * NH, HD])
            vr = sb(c, "vr", [P, M, 2 * NH])
            dots = sb(c, "dots", [HD, NH * HD])
            bh = sb(c, "bh", [HD, NH, D])
            ps_kv = ps(c, "ps_kv", [P, M, 2, 512])
            ps_d = ps(c, "ps_d", [P, 512])
            load(wkv[:].rearrange("p k h e -> p k (h e)"), a["mqkvt"][:, NH * HD:3 * NH * HD].rearrange("(k p) d -> p k d", p=P))
            load(wqn[:], a["mqkv"][0:NH * HD, :].rearrange("(h e) d -> e h d", e=HD))
            load(wo[:], a["woutt"].rearrange("(h e) d -> e h d", e=HD))
            loads_done(DVE, PE)
            for k in range(2):
                V.run(DVE.tensor_reduce(mu[:, k, :], wkv[:, k], AX.X, ALU.add))
                V.run(DVE.tensor_scalar(mu[:, k, :], mu[:, k, :], 1.0 / HD, None, ALU.mult))
                V.run(DVE.tensor_tensor(wkv[:, k], wkv[:, k], mu[:, k, :].unsqueeze(2).broadcast_to([P, 2 * NH, HD]), ALU.subtract))
            tell("v", "p"); hear("v", "p")
            PE.matmul(ps_d[0:HD, :], zeros[:, 0:HD], wkv[:, 0, 0:NH, :].rearrange("p h e -> p (h e)"), start=True, stop=False)

            def normalized(t, s):
                V.run(normalize(xn[:, s, :], t))
                tell("v", "p")

            def turned(t, s):
                hear("v", "p")
                transpose(ps_kv[:, s, 0], xn[:, s], 2).then_inc(links["p", "a"], 1)

            def copied(t, s):
                hear("p", "a")
                S.run(ACTE.activation(xnt[:, s, :], ps_kv[:, s, 0, 0:D], ACT.Copy))
                tell("a", "p")

            def projected(t, s):
                hear("a", "p")
                for h in range(2):
                    for k in range(2):
                        mm = PE.matmul(ps_kv[:, s, h, :], xnt[:, s, k * P:(k + 1) * P],
                                       wkv[:, k, NH * h:NH * h + NH, :].rearrange("p h e -> p (h e)"), start=(k == 0), stop=(k == 1))
                mm.then_inc(links["p", "a"], 1)

            def kept(t, s):
                hear("p", "a")
                S.run(ACTE.activation(kv[:, s].rearrange("p (b h) e -> p b (h e)", b=2), ps_kv[:, s], ACT.Copy))
                tell("a", "v")

            def squared(t, s):
                hear("a", "v")
                V.run(DVE.tensor_tensor(sq[:], kv[:, s], kv[:, s], ALU.mult))
                V.run(DVE.tensor_reduce(vr[:, s], sq[:], AX.X, ALU.add))
                V.run(DVE.tensor_scalar(vr[:, s], vr[:, s], 1.0 / HD, LN_EPS, ALU.mult, ALU.add))
                V.run(DVE.tensor_tensor(vr[:, s, 0:NH], vr[:, s, 0:NH], vr[:, s, NH:2 * NH], ALU.mult))
                tell("v", "a")

            def rooted(t, s):
                hear("v", "a")
                S.run(ACTE.activation(vr[:, s, 0:NH], vr[:, s, 0:NH], ACT.Sqrt))
                tell("a", "v")

            def scaled(t, s):
                hear("a", "v")
                V.run(DVE.reciprocal(vr[:, s, 0:NH], vr[:, s, 0:NH]))
                V.run(DVE.tensor_tensor(kv[:, s, 0:NH, :], kv[:, s, 0:NH, :], vr[:, s, 0:NH].unsqueeze(2).broadcast_to([P, NH, HD]),
                                        ALU.mult))
                tell("v", "p")

            def multiplied(t, s):
                rows = LAST if isinstance(t, int) and t == NT - 1 else P
                hear("v", "p")
                for h in range(NH):
                    mm = PE.matmul(ps_d[0:HD, h * HD:(h + 1) * HD], kv[0:rows, s, NH + h, :], kv[0:rows, s, h, :],
                                   start=False, stop=False)
                mm.then_inc(links["p", "a"], 1)

            def summed(t, s):
                hear("p", "a")
            tiles_in_step((normalized, turned, copied, projected, kept, squared, rooted, scaled, multiplied, summed), M)
            PE.matmul(ps_d[0:HD, :], zeros[:, 0:HD], wkv[:, 0, 0:NH, :].rearrange("p h e -> p (h e)"),
                      start=False, stop=True).then_inc(links["p", "v"], 1)
            hear("p", "v")
            V.run(DVE.tensor_scalar(dots[:], ps_d[0:HD, :], 1.0 / N, None, ALU.mult))
            tell("v", "p"); hear("v", "p")
            for h in range(NH):
                mm = PE.matmul(ps_kv[0:HD, h // 4, h // 2 % 2, (h % 2) * D:(h % 2 + 1) * D], dots[:, h * HD:(h + 1) * HD], wo[:, h, :],
                               start=True, stop=True)
            mm.then_inc(links["p", "v"], 1)
            hear("p", "v")
            V.run(DVE.tensor_copy(bh[:].rearrange("p (b h) d -> p b (h d)", b=4), ps_kv[0:HD, 0:2].rearrange("p a b w -> p (a b) w")))
            tell("v", "p"); hear("v", "p")
            for k in range(2):
                for h in range(NH):
                    mm = PE.matmul(ps_kv[:, 2, k, 0:D], wqn[:, h, k * P:(k + 1) * P], bh[:, h, :], start=(h == 0), stop=(h == NH - 1))
            mm.then_inc(links["p", "v"], 1)
            hear("p", "v")
            V.run(DVE.tensor_copy(mat[:], ps_kv[:, 2, :, 0:D]))
            barrier()

    def gcn1_project(layer, acc, res, table, mat):
        M = 4
        with ExitStack() as c:
            w = sb(c, "w", [P, 2, D])
            rw = sb(c, "rw", [P, 2, D])
            b = sb(c, "b", [P, 3, D])
            x = sb(c, "x", [P, M, D])
            xt = sb(c, "xt", [P, M, D])
            banks = ps(c, "banks", [P, M, 2, 512])
            load(w[:], a["gw"][layer].rearrange("(k p) d -> p k d", p=P))
            load(rw[:], a["resw"].rearrange("(k p) d -> p k d", p=P))
            broadcast_row(b[:, 0, :], a["gb"][layer:layer + 1, :], D)
            broadcast_row(b[:, 1, :], a["resb"], D)
            broadcast_row(b[:, 2, :], a["bout"], D)
            loads_done(PE, DVE)
            V.run(DVE.tensor_tensor(b[:, 0, :], b[:, 0, :], b[:, 1, :], ALU.add))

            def made(t, s):
                if layer == 0:
                    V.run(normalize(x[:, s, :], t))
                else:
                    V.run(DVE.scalar_tensor_tensor(x[:, s, :], row(acc, t), one(deg_dst, t), row(res, t), ALU.mult, ALU.add))
                    V.run(DVE.tensor_scalar(x[:, s, :], x[:, s, :], 0.0, None, ALU.max))
                tell("v", "p")

            def turned(t, s):
                hear("v", "p")
                transpose(banks[:, s, 0], x[:, s], 2).then_inc(links["p", "a"], 1)

            def copied(t, s):
                hear("p", "a")
                S.run(ACTE.activation(xt[:, s, :], banks[:, s, 0, 0:D], ACT.Copy))
                tell("a", "p")

            def multiplied(t, s):
                hear("a", "p")
                for q, m in enumerate((w, rw) if layer else (w, rw, mat)):
                    for k in range(2):
                        mm = PE.matmul(banks[:, s, 1 - q // 2, (q % 2) * D:(q % 2 + 1) * D], xt[:, s, k * P:(k + 1) * P], m[:, k, :],
                                       start=(k == 0), stop=(k == 1))
                mm.then_inc(links["p", "v"], 1)

            def kept(t, s):
                hear("p", "v")
                V.go(DVE.tensor_scalar(row(acc, t), banks[:, s, 1, 0:D], one(deg_dst, t), None, ALU.mult))
                V.go(DVE.tensor_tensor(row(res, t), banks[:, s, 1, D:2 * D], b[:, 0, :], ALU.add))
                if layer == 0:
                    V.run(DVE.tensor_tensor(row(x_all, t), row(x_all, t), banks[:, s, 0, 0:D], ALU.add))
                    V.run(DVE.tensor_tensor(row(x_all, t), row(x_all, t), b[:, 2, :], ALU.add))
                V.sync()
            tiles((made, turned, copied, multiplied, kept), M)
            tell("v", "a"); hear("v", "a")
            load(tile_rows(table), acc[:])
            loads_done(ACTE)
            barrier()

    def gcn1_finish(acc, res):
        V.reset()
        with DVE.Fori(0, NT) as t:
            V.run(DVE.scalar_tensor_tensor(row(acc, t), row(acc, t), one(deg_dst, t), row(res, t), ALU.mult, ALU.add))
            V.run(DVE.scalar_tensor_tensor(row(x_all, t), row(acc, t), 0.0, row(x_all, t), ALU.max, ALU.add))
            V.reset()
        barrier()

    def route1(gate, rs, affine):
        with ExitStack() as c:
            wr = sb(c, "wr", [P, 2, 8])
            br = sb(c, "br", [P, 8])
            sc = sb(c, "sc", [P, NT, 8])
            x = sb(c, "x", [P, 4, D])
            xt = sb(c, "xt", [P, 4, D])
            ps_x = ps(c, "ps_x", [P, 4, 512])
            ps_h = ps(c, "ps_h", [P, 4, 512])
            load(wr[:], a["wr"].rearrange("(k p) d -> p k d", p=P))
            load(affine[:, 0, :], a["fg"])
            load(affine[:, 1, :], a["fb"])
            broadcast_row(br[:], a["br"], 8)
            loads_done(PE, DVE, ACTE)
            V.run(DVE.tensor_tensor(rs[:], rstd[:], rstd[:], ALU.mult))
            V.run(DVE.tensor_tensor(rs[:], rs[:], var[:], ALU.mult))
            V.run(DVE.tensor_scalar(rs[:], rs[:], LN_EPS, None, ALU.add))
            tell("v", "a"); hear("v", "a")
            S.run(ACTE.activation(rs[:], rs[:], ACT.Sqrt))
            tell("a", "v"); hear("a", "v")
            V.run(DVE.reciprocal(rs[:], rs[:]))
            V.run(DVE.tensor_tensor(rs[:], rs[:], rstd[:], ALU.mult))

            def made(t, s):
                V.run(DVE.tensor_scalar(x[:, s, :], row(x_all, t), one(mean, t), one(rs, t), ALU.subtract, ALU.mult))
                tell("v", "p")

            def turned(t, s):
                hear("v", "p")
                transpose(ps_x[:, s], x[:, s], 2).then_inc(links["p", "a"], 1)

            def copied(t, s):
                hear("p", "a")
                for k in range(2):
                    S.go(ACTE.activation(xt[:, s, k * P:(k + 1) * P], ps_x[:, s, k * P:(k + 1) * P], ACT.Identity,
                                         scale=affine[:, 0, k:k + 1], bias=affine[:, 1, k:k + 1]))
                S.sync()
                tell("a", "p")

            def multiplied(t, s):
                hear("a", "p")
                for k in range(2):
                    mm = PE.matmul(ps_h[:, s, 0:8], xt[:, s, k * P:(k + 1) * P], wr[:, k, :], start=(k == 0), stop=(k == 1))
                mm.then_inc(links["p", "v"], 1)

            def kept(t, s):
                hear("p", "v")
                V.run(DVE.tensor_tensor(row(sc, t), ps_h[:, s, 0:8], br[:], ALU.add))
            tiles((made, turned, copied, multiplied, kept), 4)
            top2(sc, gate, 8)
            barrier()

    def edges(name, rows):
        return a[name].rearrange("(r c) -> r c", r=rows)

    tiles_src, tiles_dst = (sb(top, f"chunk_tiles_{q}", [P, NCH_GNN], BF16) for q in ("src", "dst"))
    with ExitStack() as c:
        first_place = sb(c, "first_place", [NT, NCH_GAT], I32)
        POOL.iota(first_place[:], [[P, NCH_GAT]], 0, 0).then_inc(s_iota, 1)
        DVE.wait_ge(s_iota, 3)
        list0, offs0, list0_done, send0 = bucket("l0", edges("src", GNN_ROWS), edges("dst", GNN_ROWS), GNN_ROWS, GNN_COLS,
                                                 NCH_GNN, False, D, first_place, tiles_src)
        send0()
        listg, offsg, listg_done, sendg = bucket("gat", edges("gat_dst", GAT_ROWS), edges("gat_src", GAT_ROWS),
                                                 GAT_ROWS, GAT_COLS, NCH_GAT, True, GH, first_place)
        sendg()
        list1, offs1, list1_done, send1 = bucket("l1", edges("dst", GNN_ROWS), edges("src", GNN_ROWS), GNN_ROWS, GNN_COLS,
                                                 NCH_GNN, False, D, first_place, tiles_dst)
    norm_stats()
    table0 = dram("table0", [NP, D])
    with ExitStack() as c:
        acc = sb(c, "acc", [P, NT, D])
        z_scale = sb(c, "z_scale", [P, NT])
        cov = sb(c, "cov", [P, 2, D])
        zmean = sb(c, "zmean", [P, 2, 1])
        gcn0_project(acc, z_scale, cov, zmean)
        degrees(list0, list0_done, tiles_src, NCH_GNN, deg_src)
        scaled_table(acc, deg_src, table0)
        mix0(z_scale, cov, zmean)
        gather_sum("l0", acc, table0, list0, offs0, NCH_GNN)
        add_scaled(acc, deg_src)
        barrier()
    norm_stats()
    gate0 = sb(top, "gate0", [P, NT, GH])
    gat_scores(listg, listg_done, offsg, NCH_GAT, gate0)
    send1()
    with ExitStack() as c:
        experts("0", GH, gate0, rstd, None, expert_weights(c, "0", GH))
    degrees(list1, list1_done, tiles_dst, NCH_GNN, deg_dst)
    norm_stats()
    with ExitStack() as c:
        mat = sb(c, "mat", [P, 2, D])
        attention_matrix(mat)
        acc = sb(c, "acc", [P, NT, D])
        res = sb(c, "res", [P, NT, D])
        for layer in range(2):
            table = dram(f"table1{layer}", [NP, D])
            gcn1_project(layer, acc, res, table, mat)
            gather_sum(f"l1{layer}", acc, table, list1, offs1, NCH_GNN)
        gcn1_finish(acc, res)
    weights1 = expert_weights(top, "1", 8)
    norm_stats()
    gate1 = sb(top, "gate1", [P, NT, 8])
    rs = sb(top, "rs", [P, NT])
    affine = sb(top, "affine", [P, 2, 2])
    route1(gate1, rs, affine)
    experts("1", 8, gate1, rs, affine, weights1)
    store_sem = sem("stores")
    ACTE.dma_start(out[0:(NT - 1) * P, :].rearrange("(t p) d -> p t d", p=P), x_all[:, 0:NT - 1, :]).then_inc(store_sem, 16)
    ACTE.dma_start(out[(NT - 1) * P:N, :], x_all[0:LAST, NT - 1, :]).then_inc(store_sem, 16)
    ACTE.wait_ge(store_sem, 32)


def lay_out(inputs):
    c = np.ascontiguousarray
    i = {k: np.asarray(v) for k, v in inputs.items()}
    return {
        "x": c(i["x"]), "src": c(i["src"]), "dst": c(i["dst"]),
        "gat_src": c(i["L0_ffn_edge_index"][0]), "gat_dst": c(i["L0_ffn_edge_index"][1]),
        "w0t": c(i["L0_gnn_W"].T),
        "qkvt": c(i["L0_mix_w_qkv"][:, :, 2].T),
        "gamma": c(i["L0_mix_bn_gamma"].reshape(1, -1)), "beta": c(i["L0_mix_bn_beta"].reshape(1, -1)),
        "dw": c(i["L0_mix_w_dw"][:, 0, 2].reshape(6, P).T),
        "pwt": c(i["L0_mix_w_pw"][:, :, 0].reshape(24, 32, 32).transpose(0, 2, 1)),
        "rest": c(i["L0_mix_w_res"][:, :, 0].T), "bres": c(i["L0_mix_b_res"].reshape(1, -1)),
        "wgat": c(i["L0_ffn_W_gat"]),
        "att_src": c(i["L0_ffn_att_src"].reshape(1, -1)), "att_dst": c(i["L0_ffn_att_dst"].reshape(1, -1)),
        "bgat": c(i["L0_ffn_b_gat"].reshape(1, -1)),
        "lng": c(i["L0_ffn_ln_gamma"].reshape(1, -1)), "lnb": c(i["L0_ffn_ln_beta"].reshape(1, -1)),
        "w1_0": c(i["L0_ffn_W1"]), "b1_0": c(i["L0_ffn_b1"].reshape(4, 4, P).transpose(2, 0, 1)), "w2_0": c(i["L0_ffn_W2"]), "b2_0": c(i["L0_ffn_b2"]),
        "gw": c(i["L1_gnn_W"]), "gb": c(i["L1_gnn_b"]), "resw": c(i["L1_gnn_resW"]),
        "resb": c(i["L1_gnn_resb"].reshape(1, -1)),
        "mqkv": c(i["L1_mix_w_qkv"]), "mqkvt": c(i["L1_mix_w_qkv"].T), "woutt": c(i["L1_mix_w_out"].T),
        "bout": c(i["L1_mix_b_out"].reshape(1, -1)),
        "fg": c(i["L1_ffn_gamma"].reshape(2, P).T), "fb": c(i["L1_ffn_beta"].reshape(2, P).T),
        "wr": c(i["L1_ffn_Wr"]), "br": c(i["L1_ffn_br"].reshape(1, -1)),
        "w1_1": c(i["L1_ffn_W1"]), "b1_1": c(i["L1_ffn_b1"].reshape(8, 4, P).transpose(2, 0, 1)), "w2_1": c(i["L1_ffn_W2"]), "b2_1": c(i["L1_ffn_b2"]),
    }


def kernel(**inputs):
    import concourse.bacc as _bacc
    from concourse import mybir as _mybir
    from concourse.bass_utils import run_bass_kernel_spmd as _run

    laid = lay_out(inputs)
    nc = _bacc.Bacc("TRN2", target_bir_lowering=False, num_devices=1)
    arrays, aps = {}, {}
    for name, v in laid.items():
        arrays[f"in_{name}"] = v
        aps[name] = nc.dram_tensor(f"in_{name}", v.shape, _mybir.dt.from_np(v.dtype), kind="ExternalInput").ap()
    out = nc.dram_tensor("out_x", (N, D), F32, kind="ExternalOutput").ap()
    program(nc, aps, out)
    r = _run(nc, [arrays], core_ids=[0])
    return r.results[0]["out_x"]
```
